# Optimizing a Trainium2 kernel written in Bass

```python
import numpy as np
import jax
import jax.numpy as jnp

def _softmax(x, axis=-1):
    return jax.nn.softmax(x, axis=axis)

def _gelu(x):
    return jax.nn.gelu(x, approximate=True)

def _silu(x):
    return jax.nn.silu(x)

def _sigmoid(x):
    return jax.nn.sigmoid(x)

def _layernorm(x, axis=-1, eps=1e-05):
    m = jnp.mean(x, axis=axis, keepdims=True)
    v = jnp.var(x, axis=axis, keepdims=True)
    return (x - m) / jnp.sqrt(v + eps)

def _scatter_add(tgt, idx, src, axis=0):
    return tgt.at[idx].add(src)

def _segment_sum(src, seg, n):
    return jax.ops.segment_sum(src, seg, n)
kernel_name = 'mk_xattn_ffn_d2_seqx_r8_2d5807'

def setup_inputs(seed: int=0):
    np.random.seed(seed)
    _w = jnp.asarray

    def _rec_inputs():
        import jax
        import jax.numpy as jnp
        _rk = jax.random.key(seed)
        x = 7.22e-05 + 1 * jax.random.normal(jax.random.fold_in(_rk, 1), (32, 128, 128), jnp.float32)
        _lenS = 128 - jax.random.randint(jax.random.fold_in(_rk, 7), (32,), 0, max(1, 128 // 4) + 1, jnp.int32)
        _lenS2 = 128 - jax.random.randint(jax.random.fold_in(_rk, 8), (32,), 0, max(1, 128 // 4) + 1, jnp.int32)
        _ctx_1024P = jax.random.normal(jax.random.fold_in(_rk, 11), (32, 16, 128), jnp.float32)
        _ctx_1024c = jax.random.dirichlet(jax.random.fold_in(_rk, 511), 0.3 * jnp.ones((16,), jnp.float32), (32, 128))
        _ctx_1024t = jnp.einsum('bsk,bkd->bsd', _ctx_1024c, _ctx_1024P)
        _ctx_1024t = _ctx_1024t * jax.lax.rsqrt(jnp.mean(jnp.square(_ctx_1024t)) + 1e-12) * 0.953939
        ctx_1024 = 4.13588e-05 + 0.999923 * (_ctx_1024t + 0.3 * jax.random.normal(jax.random.fold_in(_rk, 611), (32, 128, 128), jnp.float32))
        return (x, ctx_1024)
    x, ctx_1024 = _rec_inputs()

    def _L0_xattn_setup():
        import jax, jax.numpy as jnp
        import numpy as np
        import math
        B, S, D_MODEL, N_HEAD = (4, 256, 128, 16)
        D_K = D_MODEL // N_HEAD
        ROPE_THETA = 10000.0

        def _rope(x):
            b, h, s, d = x.shape
            inv_freq = ROPE_THETA ** (-jnp.arange(0, d, 2, dtype=jnp.float32) / d)
            ang = jnp.arange(s, dtype=jnp.float32)[:, None] * inv_freq[None, :]
            cos, sin = (jnp.cos(ang), jnp.sin(ang))
            x1, x2 = (x[..., 0::2], x[..., 1::2])
            r1 = x1 * cos - x2 * sin
            r2 = x1 * sin + x2 * cos
            return jnp.stack([r1, r2], axis=-1).reshape(b, h, s, d)

        def _split(x):
            b, s, d = x.shape
            return x.reshape(b, s, N_HEAD, d // N_HEAD).transpose(0, 2, 1, 3)
        key = jax.random.key(seed)
        ks = jax.random.split(key, 7)
        sc = 1.0 / math.sqrt(D_MODEL)
        return {'q': jax.random.normal(ks[0], (B, S, D_MODEL), jnp.float32), 'k': jax.random.normal(ks[1], (B, S, D_MODEL), jnp.float32), 'v': jax.random.normal(ks[2], (B, S, D_MODEL), jnp.float32), 'Wq': jax.random.normal(ks[3], (D_MODEL, D_MODEL), jnp.float32) * sc, 'Wk': jax.random.normal(ks[4], (D_MODEL, D_MODEL), jnp.float32) * sc, 'Wv': jax.random.normal(ks[5], (D_MODEL, D_MODEL), jnp.float32) * sc, 'Wo': jax.random.normal(ks[6], (D_MODEL, D_MODEL), jnp.float32) * sc}
    _L0_xattn_all = _L0_xattn_setup()
    _L0_xattn_in = {k: v for k, v in _L0_xattn_all.items() if k in ('Wq', 'Wk', 'Wv', 'Wo')}
    del _L0_xattn_all

    def _L0_ffn_setup():
        import jax, jax.numpy as jnp
        import numpy as np
        D_MODEL = 128
        NUM_EXPERTS = 8
        TOP_K = 2
        B, S = (4, 256)
        key = jax.random.key(seed)
        ks = jax.random.split(key, 7)
        scale_in = 1.0 / np.sqrt(D_MODEL)
        scale_hid = 1.0 / np.sqrt(2 * D_MODEL)
        return {'x': jax.random.normal(ks[0], (B, S, D_MODEL), dtype=jnp.float32), 'Wg': jax.random.normal(ks[1], (D_MODEL, NUM_EXPERTS), dtype=jnp.float32) * scale_in, 'bg': jnp.zeros((NUM_EXPERTS,), dtype=jnp.float32), 'W1': jax.random.normal(ks[2], (NUM_EXPERTS, D_MODEL, 2 * D_MODEL), dtype=jnp.float32) * scale_in, 'b1': jnp.zeros((NUM_EXPERTS, 2 * D_MODEL), dtype=jnp.float32), 'W2': jax.random.normal(ks[3], (NUM_EXPERTS, 2 * D_MODEL, D_MODEL), dtype=jnp.float32) * scale_hid, 'b2': jnp.zeros((NUM_EXPERTS, D_MODEL), dtype=jnp.float32)}
    _L0_ffn_all = _L0_ffn_setup()
    _L0_ffn_in = {k: v for k, v in _L0_ffn_all.items() if k in ('Wg', 'bg', 'W1', 'b1', 'W2', 'b2')}
    del _L0_ffn_all

    def _L1_xattn_setup():
        import jax, jax.numpy as jnp
        import numpy as np
        EMBED_DIM = 128
        NUM_HEADS = 16
        HEAD_DIM = EMBED_DIM // NUM_HEADS
        WINDOW = 64

        def apply_rope(x):
            B, H, S, d = x.shape
            half = d // 2
            pos = jnp.arange(S, dtype=x.dtype)
            freqs = 1.0 / 10000.0 ** (jnp.arange(half, dtype=x.dtype) / half)
            ang = pos[:, None] * freqs[None, :]
            cos, sin = (jnp.cos(ang), jnp.sin(ang))
            x1, x2 = (x[..., :half], x[..., half:])
            return jnp.concatenate([x1 * cos - x2 * sin, x1 * sin + x2 * cos], axis=-1)

        def _forward(query, key, value, q_w, q_b, k_w, k_b, v_w, v_b, o_w, o_b):
            B, S_q, D = query.shape
            S_k = key.shape[1]
            H, d, W = (NUM_HEADS, HEAD_DIM, WINDOW)
            q = (query @ q_w.T + q_b).reshape(B, S_q, H, d).transpose(0, 2, 1, 3)
            k = (key @ k_w.T + k_b).reshape(B, S_k, H, d).transpose(0, 2, 1, 3)
            v = (value @ v_w.T + v_b).reshape(B, S_k, H, d).transpose(0, 2, 1, 3)
            q = apply_rope(q) * d ** (-0.5)
            k = apply_rope(k)
            q_pos = jnp.arange(S_q)[:, None]
            offsets = jnp.arange(-W, 1)[None, :]
            idx = q_pos + offsets
            local_mask = (idx < 0) | (idx >= S_k)
            gidx = jnp.clip(idx, 0, S_k - 1)
            k_win = k[:, :, gidx, :]
            v_win = v[:, :, gidx, :]
            scores = jnp.einsum('bhqd,bhqwd->bhqw', q, k_win)
            mask = local_mask[None, None, :, :]
            scores = jnp.where(mask, -jnp.inf, scores)
            m = jnp.max(scores, axis=-1, keepdims=True)
            m = jnp.where(jnp.isfinite(m), m, 0.0)
            e = jnp.exp(scores - m)
            denom = jnp.sum(e, axis=-1, keepdims=True)
            probs = jnp.where(denom > 0, e / jnp.where(denom > 0, denom, 1.0), 0.0)
            ctx = jnp.einsum('bhqw,bhqwd->bhqd', probs, v_win)
            ctx = ctx.transpose(0, 2, 1, 3).reshape(B, S_q, D)
            return ctx @ o_w.T + o_b
        key = jax.random.key(seed)
        ks = jax.random.split(key, 12)
        B, S, D = (1, 256, EMBED_DIM)
        scale = 1.0 / np.sqrt(D)
        inp = {'query': jax.random.normal(ks[0], (B, S, D), jnp.float32), 'key': jax.random.normal(ks[1], (B, S, D), jnp.float32), 'value': jax.random.normal(ks[2], (B, S, D), jnp.float32), 'q_w': jax.random.normal(ks[3], (D, D), jnp.float32) * scale, 'q_b': jax.random.normal(ks[4], (D,), jnp.float32) * 0.01, 'k_w': jax.random.normal(ks[5], (D, D), jnp.float32) * scale, 'k_b': jax.random.normal(ks[6], (D,), jnp.float32) * 0.01, 'v_w': jax.random.normal(ks[7], (D, D), jnp.float32) * scale, 'v_b': jax.random.normal(ks[8], (D,), jnp.float32) * 0.01, 'o_w': jax.random.normal(ks[9], (D, D), jnp.float32) * scale, 'o_b': jax.random.normal(ks[10], (D,), jnp.float32) * 0.01}
        return inp
    _L1_xattn_all = _L1_xattn_setup()
    _L1_xattn_in = {k: v for k, v in _L1_xattn_all.items() if k in ('q_w', 'q_b', 'k_w', 'k_b', 'v_w', 'v_b', 'o_w', 'o_b')}
    del _L1_xattn_all

    def _L1_ffn_setup():
        import jax, jax.numpy as jnp
        import numpy as np
        QB = 127.0
        EPS = 1e-05

        def _ste(x, q):
            return x + jax.lax.stop_gradient(q - x)

        def bitlinear(x, W, b):
            w_scale = jnp.clip(jnp.mean(jnp.abs(W)), EPS, None)
            Wq = _ste(W, jnp.clip(jnp.round(W / w_scale), -1.0, 1.0) * w_scale)
            x_scale = jnp.clip(jnp.max(jnp.abs(x), axis=-1, keepdims=True), EPS, None)
            xq = _ste(x, jnp.clip(jnp.round(x * (QB / x_scale)), -QB - 1.0, QB) * (x_scale / QB))
            return jnp.einsum('bnd,hd->bnh', xq, Wq) + b
        key = jax.random.key(seed)
        k0, k1, k2 = jax.random.split(key, 3)
        B, N, D = (8, 512, 128)
        H = int(D * 4.0)
        x = jax.random.normal(k0, (B, N, D), dtype=jnp.float32)
        W1 = jax.random.normal(k1, (H, D), dtype=jnp.float32) * 0.02
        b1 = jnp.zeros((H,), dtype=jnp.float32)
        W2 = jax.random.normal(k2, (D, H), dtype=jnp.float32) * 0.02
        b2 = jnp.zeros((D,), dtype=jnp.float32)
        return {'x': x, 'W1': W1, 'b1': b1, 'W2': W2, 'b2': b2}
    _L1_ffn_all = _L1_ffn_setup()
    _L1_ffn_in = {k: v for k, v in _L1_ffn_all.items() if k in ('W1', 'b1', 'W2', 'b2')}
    del _L1_ffn_all
    return {'x': x, 'ctx_1024': ctx_1024, 'L0_xattn_Wq': _L0_xattn_in['Wq'], 'L0_xattn_Wk': _L0_xattn_in['Wk'], 'L0_xattn_Wv': _L0_xattn_in['Wv'], 'L0_xattn_Wo': _L0_xattn_in['Wo'], 'L0_ffn_Wg': _L0_ffn_in['Wg'], 'L0_ffn_bg': _L0_ffn_in['bg'], 'L0_ffn_W1': _L0_ffn_in['W1'], 'L0_ffn_b1': _L0_ffn_in['b1'], 'L0_ffn_W2': _L0_ffn_in['W2'], 'L0_ffn_b2': _L0_ffn_in['b2'], 'L1_xattn_q_w': _L1_xattn_in['q_w'], 'L1_xattn_q_b': _L1_xattn_in['q_b'], 'L1_xattn_k_w': _L1_xattn_in['k_w'], 'L1_xattn_k_b': _L1_xattn_in['k_b'], 'L1_xattn_v_w': _L1_xattn_in['v_w'], 'L1_xattn_v_b': _L1_xattn_in['v_b'], 'L1_xattn_o_w': _L1_xattn_in['o_w'], 'L1_xattn_o_b': _L1_xattn_in['o_b'], 'L1_ffn_W1': _L1_ffn_in['W1'], 'L1_ffn_b1': _L1_ffn_in['b1'], 'L1_ffn_W2': _L1_ffn_in['W2'], 'L1_ffn_b2': _L1_ffn_in['b2']}

def reference(x, ctx_1024, L0_xattn_Wq, L0_xattn_Wk, L0_xattn_Wv, L0_xattn_Wo, L0_ffn_Wg, L0_ffn_bg, L0_ffn_W1, L0_ffn_b1, L0_ffn_W2, L0_ffn_b2, L1_xattn_q_w, L1_xattn_q_b, L1_xattn_k_w, L1_xattn_k_b, L1_xattn_v_w, L1_xattn_v_b, L1_xattn_o_w, L1_xattn_o_b, L1_ffn_W1, L1_ffn_b1, L1_ffn_W2, L1_ffn_b2):
    import jax
    import jax.numpy as jnp

    def _L0_xattn_ref(q, k, v, Wq, Wk, Wv, Wo):
        import jax, jax.numpy as jnp
        import numpy as np
        import math
        B, S, D_MODEL, N_HEAD = (4, 256, 128, 16)
        D_K = D_MODEL // N_HEAD
        ROPE_THETA = 10000.0

        def _rope(x):
            b, h, s, d = x.shape
            inv_freq = ROPE_THETA ** (-jnp.arange(0, d, 2, dtype=jnp.float32) / d)
            ang = jnp.arange(s, dtype=jnp.float32)[:, None] * inv_freq[None, :]
            cos, sin = (jnp.cos(ang), jnp.sin(ang))
            x1, x2 = (x[..., 0::2], x[..., 1::2])
            r1 = x1 * cos - x2 * sin
            r2 = x1 * sin + x2 * cos
            return jnp.stack([r1, r2], axis=-1).reshape(b, h, s, d)

        def _split(x):
            b, s, d = x.shape
            return x.reshape(b, s, N_HEAD, d // N_HEAD).transpose(0, 2, 1, 3)
        q = jnp.einsum('bsd,de->bse', q, Wq)
        k = jnp.einsum('bsd,de->bse', k, Wk)
        v = jnp.einsum('bsd,de->bse', v, Wv)
        qh, kh, vh = (_split(q), _split(k), _split(v))
        qh, kh = (_rope(qh), _rope(kh))
        scale = 1.0 / math.sqrt(D_K)
        score = jnp.einsum('bhqd,bhkd->bhqk', qh, kh) * scale
        attn = jax.nn.softmax(score, axis=-1)
        out = jnp.einsum('bhqk,bhkd->bhqd', attn, vh)
        out = out.transpose(0, 2, 1, 3).reshape(q.shape[0], q.shape[1], D_MODEL)
        return jnp.einsum('bsd,de->bse', out, Wo)

    def _L0_ffn_ref(x, Wg, bg, W1, b1, W2, b2):
        import jax, jax.numpy as jnp
        import numpy as np
        D_MODEL = 128
        NUM_EXPERTS = 8
        TOP_K = 2
        B, S = (4, 256)
        Bb, Ss, D = x.shape
        E = Wg.shape[1]
        xf = x.reshape(-1, D)
        logits = xf @ Wg + bg
        probs = jax.nn.softmax(logits, axis=-1)
        w, idx = jax.lax.top_k(probs, TOP_K)
        w = w / jnp.sum(w, axis=-1, keepdims=True)
        comb = jnp.sum(jax.nn.one_hot(idx, E, dtype=xf.dtype) * w[..., None], axis=1)
        h = jax.nn.relu(jnp.einsum('nd,edh->enh', xf, W1) + b1[:, None, :])
        y = jnp.einsum('enh,ehd->end', h, W2) + b2[:, None, :]
        out = jnp.einsum('end,ne->nd', y, comb)
        return out.reshape(Bb, Ss, D)

    def _L1_xattn_ref(query, key, value, q_w, q_b, k_w, k_b, v_w, v_b, o_w, o_b):
        import jax, jax.numpy as jnp
        import numpy as np
        EMBED_DIM = 128
        NUM_HEADS = 16
        HEAD_DIM = EMBED_DIM // NUM_HEADS
        WINDOW = 64

        def apply_rope(x):
            B, H, S, d = x.shape
            half = d // 2
            pos = jnp.arange(S, dtype=x.dtype)
            freqs = 1.0 / 10000.0 ** (jnp.arange(half, dtype=x.dtype) / half)
            ang = pos[:, None] * freqs[None, :]
            cos, sin = (jnp.cos(ang), jnp.sin(ang))
            x1, x2 = (x[..., :half], x[..., half:])
            return jnp.concatenate([x1 * cos - x2 * sin, x1 * sin + x2 * cos], axis=-1)

        def _forward(query, key, value, q_w, q_b, k_w, k_b, v_w, v_b, o_w, o_b):
            B, S_q, D = query.shape
            S_k = key.shape[1]
            H, d, W = (NUM_HEADS, HEAD_DIM, WINDOW)
            q = (query @ q_w.T + q_b).reshape(B, S_q, H, d).transpose(0, 2, 1, 3)
            k = (key @ k_w.T + k_b).reshape(B, S_k, H, d).transpose(0, 2, 1, 3)
            v = (value @ v_w.T + v_b).reshape(B, S_k, H, d).transpose(0, 2, 1, 3)
            q = apply_rope(q) * d ** (-0.5)
            k = apply_rope(k)
            q_pos = jnp.arange(S_q)[:, None]
            offsets = jnp.arange(-W, 1)[None, :]
            idx = q_pos + offsets
            local_mask = (idx < 0) | (idx >= S_k)
            gidx = jnp.clip(idx, 0, S_k - 1)
            k_win = k[:, :, gidx, :]
            v_win = v[:, :, gidx, :]
            scores = jnp.einsum('bhqd,bhqwd->bhqw', q, k_win)
            mask = local_mask[None, None, :, :]
            scores = jnp.where(mask, -jnp.inf, scores)
            m = jnp.max(scores, axis=-1, keepdims=True)
            m = jnp.where(jnp.isfinite(m), m, 0.0)
            e = jnp.exp(scores - m)
            denom = jnp.sum(e, axis=-1, keepdims=True)
            probs = jnp.where(denom > 0, e / jnp.where(denom > 0, denom, 1.0), 0.0)
            ctx = jnp.einsum('bhqw,bhqwd->bhqd', probs, v_win)
            ctx = ctx.transpose(0, 2, 1, 3).reshape(B, S_q, D)
            return ctx @ o_w.T + o_b
        return _forward(query, key, value, q_w, q_b, k_w, k_b, v_w, v_b, o_w, o_b)

    def _L1_ffn_ref(x, W1, b1, W2, b2):
        import jax, jax.numpy as jnp
        import numpy as np
        QB = 127.0
        EPS = 1e-05

        def _ste(x, q):
            return x + jax.lax.stop_gradient(q - x)

        def bitlinear(x, W, b):
            w_scale = jnp.clip(jnp.mean(jnp.abs(W)), EPS, None)
            Wq = _ste(W, jnp.clip(jnp.round(W / w_scale), -1.0, 1.0) * w_scale)
            x_scale = jnp.clip(jnp.max(jnp.abs(x), axis=-1, keepdims=True), EPS, None)
            xq = _ste(x, jnp.clip(jnp.round(x * (QB / x_scale)), -QB - 1.0, QB) * (x_scale / QB))
            return jnp.einsum('bnd,hd->bnh', xq, Wq) + b
        h = bitlinear(x, W1, b1)
        h = jax.nn.gelu(h, approximate=False)
        return bitlinear(h, W2, b2)
    x = x + _L0_xattn_ref(_layernorm(x, axis=-1), ctx_1024, ctx_1024, L0_xattn_Wq, L0_xattn_Wk, L0_xattn_Wv, L0_xattn_Wo)
    x = x + _L0_ffn_ref(_layernorm(x, axis=-1), L0_ffn_Wg, L0_ffn_bg, L0_ffn_W1, L0_ffn_b1, L0_ffn_W2, L0_ffn_b2)
    x = x + _L1_xattn_ref(_layernorm(x, axis=-1), ctx_1024, ctx_1024, L1_xattn_q_w, L1_xattn_q_b, L1_xattn_k_w, L1_xattn_k_b, L1_xattn_v_w, L1_xattn_v_b, L1_xattn_o_w, L1_xattn_o_b)
    x = x + _L1_ffn_ref(_layernorm(x, axis=-1), L1_ffn_W1, L1_ffn_b1, L1_ffn_W2, L1_ffn_b2)
    return x

_drawn_inputs = setup_inputs


def setup_inputs(seed=0):
    import zlib

    import numpy as np

    out = dict(_drawn_inputs(seed))
    spreads = {'L0_ffn_bg': (0.0, 0.1),
     'L0_ffn_b1': (0.0, 0.1),
     'L0_ffn_b2': (0.0, 0.1),
     'L1_ffn_b1': (0.0, 0.713),
     'L1_ffn_b2': (0.0, 0.1)}
    factors = {'L1_xattn_q_b': 30.919,
     'L1_xattn_k_b': 47.445,
     'L1_xattn_v_b': 6.926,
     'L1_xattn_o_b': 6.956,
     'L1_ffn_W1': 3.374,
     'L1_ffn_W2': 2.851}
    for name, (base, spread) in spreads.items():
        noise = np.random.default_rng([zlib.crc32(name.encode()), seed]).standard_normal(out[name].shape)
        drawn = base * np.exp(spread * noise) if base else spread * noise
        out[name] = jnp.asarray(drawn.astype(out[name].dtype))
    for name, factor in factors.items():
        out[name] = (out[name] * factor).astype(out[name].dtype)
    return out
```

```python
from contextlib import ExitStack

import concourse.bass as bass
from concourse import mybir

F32 = mybir.dt.float32
BF16 = mybir.dt.bfloat16
U32 = mybir.dt.uint32
ACT = mybir.ActivationFunctionType
ALU = mybir.AluOpType
AX = mybir.AxisListType

B, S, D = 32, 128, 128
H = 16
DH = D // H
E = 8
HID = 256
NCH = HID // 128
G = 4
NG = B // G
F = 512
FC = F // 128
WINDOW = 64
EPS = 1e-5
QB = 127.0
MAGIC = 1.5 * 2.0 ** 23
SLOT = 64
ROWS = 6 * DH
Q_L, K_L = 4, 3

CONSTS = ("c_ident", "c_rope_c0", "c_rope_s0", "c_rope_c1", "c_rope_s1", "c_pick", "c_mask_qk", "c_mask_kq",
          "c_iota")


class AttentionEvents:

    def __init__(self, sem, L):
        self.xn_ready = sem(f"L{L}_xn_ready")
        self.ctx_ready = sem(f"L{L}_ctx_ready")
        self.xnT_ps = sem(f"L{L}_xnT_ps")
        self.xnT_sb = sem(f"L{L}_xnT_sb")
        self.proj_ps = sem(f"L{L}_proj_ps")
        self.proj_read = sem(f"L{L}_proj_read")
        self.v_copied = sem(f"L{L}_v_copied")
        self.qk_ready = sem(f"L{L}_qk_ready")
        self.h_ready = sem(f"L{L}_h_ready")
        self.rest_ready = sem(f"L{L}_rest_ready")
        self.m_ready = sem(f"L{L}_m_ready")
        self.l_ready = sem(f"L{L}_l_ready")
        self.dup_ready = sem(f"L{L}_dup_ready")
        self.qT_ps = sem(f"L{L}_qT_ps")
        self.kT_ps = sem(f"L{L}_kT_ps")
        self.qT_sb = sem(f"L{L}_qT_sb")
        self.kT_sb = sem(f"L{L}_kT_sb")
        self.s0_ps = sem(f"L{L}_s0_ps")
        self.s1_ps = sem(f"L{L}_s1_ps")
        self.max0 = sem(f"L{L}_max0")
        self.max1 = sem(f"L{L}_max1")
        self.mh_ready = sem(f"L{L}_mh_ready")
        self.ms_ready = sem(f"L{L}_ms_ready")
        self.mT_ps = sem(f"L{L}_mT_ps")
        self.mT_sb = sem(f"L{L}_mT_sb")
        self.st0_ps = sem(f"L{L}_st0_ps")
        self.st1_ps = sem(f"L{L}_st1_ps")
        self.exp0 = sem(f"L{L}_exp0")
        self.exp1 = sem(f"L{L}_exp1")
        self.pv1 = sem(f"L{L}_pv1")
        self.oT_sb = sem(f"L{L}_oT_sb")
        self.o_ps = sem(f"L{L}_o_ps")
        self.rden_ready = sem(f"L{L}_rden_ready")
        self.on_ready = sem(f"L{L}_on_ready")
        self.onT_ps = sem(f"L{L}_onT_ps")
        self.onT_sb = sem(f"L{L}_onT_sb")
        self.y_ps = sem(f"L{L}_y_ps")
        self.x_done = sem(f"L{L}_x_done")


def build(nc, t, out):
    ctx = ExitStack()
    with ctx:
        def sb(name, shape, dt=F32):
            return ctx.enter_context(nc.sbuf_tensor(name, shape, dt))

        def ps(name, shape, dt=F32):
            return ctx.enter_context(nc.psum_tensor(name, shape, dt))

        def sem(name):
            return ctx.enter_context(nc.semaphore(name))

        X = sb("X", [128, B, D])
        ctxT = sb("ctxT", [128, B, S])
        ident = sb("ident", [128, 128])
        identb = sb("identb", [128, 128], BF16)
        rope_c = [sb(f"rope_c{i}", [128, 2, DH]) for i in range(2)]
        rope_s = [sb(f"rope_s{i}", [128, 2, DH]) for i in range(2)]
        pickf = sb("pickf", [128, H, 128])
        pick = sb("pick", [128, H, 128], BF16)
        maskf = sb("maskf", [128, 2, 128])
        mask = sb("mask", [128, 2, 128], BF16)
        iota = sb("iota", [128, E])
        ones = sb("ones", [1, 128])
        wq = [sb(f"wq{i}", [128, D]) for i in range(2)]
        wkv = [sb(f"wkv{i}", [128, 2 * D]) for i in range(2)]
        wo = [sb(f"wo{i}", [128, D]) for i in range(2)]
        qkvb = sb("qkvb", [1, 3 * D])
        ob = sb("ob", [1, D])
        wg = sb("wg", [128, E])
        bg = sb("bg", [1, E])
        w1 = sb("w1", [128, E, HID])
        b1 = sb("b1", [128, E, NCH])
        w2 = sb("w2", [128, E, NCH, D])
        b2 = sb("b2", [E, D])
        fw1 = sb("fw1", [128, F])
        fw2 = sb("fw2", [128, FC, D])
        fw1q = sb("fw1q", [128, F], BF16)
        fw2q = sb("fw2q", [128, FC, D], BF16)
        fb1 = sb("fb1", [128, F])
        fb2 = sb("fb2", [128, D])
        onesq = sb("onesq", [128, 128])
        minus_half = sb("minus_half", [128, B])
        wsum = sb("wsum", [128, 2])
        wscale = sb("wscale", [128, 2])
        wrecip = sb("wrecip", [128, 2])
        wtmp = sb("wtmp", [128, F])

        stats = sb("stats", [128, B, 6])
        mean = sb("mean", [128, B])
        half_d = sb("half_d", [128, B])
        var = sb("var", [128, B])
        var2 = sb("var2", [128, B])
        rstd = sb("rstd", [128, B])

        xn = [sb(f"xn{i}", [128, D]) for i in range(2)]
        xnT = [sb(f"xnT{i}", [128, 128]) for i in range(2)]
        ctx_now = [sb(f"ctx_now{i}", [128, 128]) for i in range(2)]
        rot1 = sb("rot1", [128, 2 * H, DH])
        rot2 = sb("rot2", [128, 2 * H, DH])
        qk = sb("qk", [128, 2 * H, DH])
        qk_rest = sb("qk_rest", [128, 2 * H, DH])
        stack = sb("stack", [128, 2 * H, SLOT], BF16)
        QT = [sb(f"QT{i}", [128, H // 2, 128], BF16) for i in range(2)]
        KT = [sb(f"KT{i}", [128, H // 2, 128], BF16) for i in range(2)]
        V = [sb(f"V{i}", [128, H, 32]) for i in range(2)]
        nmax = sb("nmax", [128, H])
        msplit = sb("msplit", [128, 128], BF16)
        mT = sb("mT", [128, 128], BF16)
        PT = [sb(f"PT{i}", [128, H // 2, 128]) for i in range(2)]
        rden = sb("rden", [128, H])
        on = sb("on", [128, D])
        oT = sb("oT", [128, 4, 128])
        onT = sb("onT", [128, 128])

        xg = sb("xg", [128, G, D])
        xgT = [sb(f"xgT{i}", [128, G, 128]) for i in range(2)]
        logit = sb("logit", [128, G, E])
        top = sb("top", [128, G, 8])
        topi = sb("topi", [128, G, 8], U32)
        topf = sb("topf", [128, G, 8])
        carry = sb("carry", [128, 2])
        gap = sb("gap", [128, G])
        egap = sb("egap", [128, G])
        egap1 = sb("egap1", [128, G])
        w_first = sb("w_first", [128, G])
        w_second = sb("w_second", [128, G])
        pick1 = sb("pick1", [128, G, E])
        pick2 = sb("pick2", [128, G, E])
        comb = [sb(f"comb{i}", [128, G, E]) for i in range(2)]
        combT = [sb(f"combT{i}", [E, G, 128]) for i in range(2)]
        hid = [[sb(f"hid{i}{c}", [128, G, 128]) for c in range(NCH)] for i in range(2)]

        fxn = sb("fxn", [128, D])
        fxq = sb("fxq", [128, D], BF16)
        fxr = sb("fxr", [128, D])
        fxqT = sb("fxqT", [128, 128], BF16)
        amax = sb("amax", [128, 2, 4])
        hmax = sb("hmax", [128, 2, 4])
        hpre = [sb(f"hpre{i}", [128, F]) for i in range(2)]
        hact = [sb(f"hact{i}", [128, F]) for i in range(2)]
        hround = sb("hround", [128, F])
        hq = sb("hq", [128, F], BF16)
        hqT = sb("hqT", [128, FC, 128], BF16)
        xb = sb("xb", [128, D])
        yout = [sb(f"yout{i}", [128, D]) for i in range(2)]

        pairs = [ps(f"pair{i}", [128, 2, 4, 128]) for i in range(2)]
        M = [ps(f"M{i}", [128, 512]) for i in range(4)]
        Mb = [m[:, :].bitcast(BF16) for m in M]

        loaded = sem("loaded")
        consts_dve = sem("consts_dve")
        consts_pool = sem("consts_pool")
        wabs_ready = sem("wabs_ready")
        wsum_ps = sem("wsum_ps")
        wstep = sem("wstep")
        out_done = [sem(f"out_done{i}") for i in range(2)]
        LOADS = 16 * 29

        stats_ready = sem("stats_ready")
        ln_step = sem("ln_step")
        rstd_ready = sem("rstd_ready")
        LN_STEPS = 5

        layers = [AttentionEvents(sem, L) for L in range(2)]

        m_xg = sem("m_xg")
        m_xgT_ps = sem("m_xgT_ps")
        m_xgT_sb = sem("m_xgT_sb")
        m_logit_ps = sem("m_logit_ps")
        m_logit_sb = sem("m_logit_sb")
        m_top = sem("m_top")
        m_carry = sem("m_carry")
        m_topi = sem("m_topi")
        m_gate = sem("m_gate")
        m_egap = sem("m_egap")
        m_comb = sem("m_comb")
        m_combT_ps = sem("m_combT_ps")
        m_combT_sb = sem("m_combT_sb")
        m_h_ps = sem("m_h_ps")
        m_h_sb = sem("m_h_sb")
        m_y_ps = sem("m_y_ps")
        m_y_added = sem("m_y_added")
        GATE_STEPS = 9

        f_xn = sem("f_xn")
        f_amax = sem("f_amax")
        f_xr = sem("f_xr")
        f_xq = sem("f_xq")
        f_xqT_ps = sem("f_xqT_ps")
        f_xqT_sb = sem("f_xqT_sb")
        f_h_ps = sem("f_h_ps")
        f_hpre = sem("f_hpre")
        f_gelu = sem("f_gelu")
        f_hmax = sem("f_hmax")
        f_hr = sem("f_hr")
        f_hq = sem("f_hq")
        f_hqT_ps = sem("f_hqT_ps")
        f_hqT_sb = sem("f_hqT_sb")
        f_y_ps = sem("f_y_ps")
        f_xb = sem("f_xb")
        f_out = sem("f_out")

        def after(eng, s, v):
            if not isinstance(v, int) or v > 0:
                eng.wait_ge(s, v)

        def one(tensor, n):
            return tensor[:, bass.ds(n, 1)].rearrange("p a b -> p (a b)")

        def pipeline(eng, step):
            FIRST, LAST, LOOP0, LOOP1 = -3, B, 3, B - 4

            def peeled(n):
                step(n, n % 2, lambda k: 0 <= n + k < B)

            for n in range(FIRST, LOOP0):
                peeled(n)
            with eng.Fori(LOOP0, LOOP1, 2) as n:
                step(n, 1, lambda k: True)
                step(n + 1, 0, lambda k: True)
            for n in range(LOOP1 + 1, LAST + 1):
                peeled(n)

        block = ctx.enter_context(nc.Block())

        @block.sync
        def _(sp):
            def load(dst, src):
                sp.dma_start(dst, src).then_inc(loaded, 16)

            load(X[:, :, :], t["x"])
            load(ident[:, :], t["c_ident"])
            load(wq[0][:, :], t["wq0"])
            load(wkv[0][:, :], t["wkv0"])
            load(ctxT[:, :, :], t["ctxT"])
            for i in range(2):
                load(rope_c[i][:, :, :], t[f"c_rope_c{i}"])
                load(rope_s[i][:, :, :], t[f"c_rope_s{i}"])
            load(pickf[:, :, :], t["c_pick"])
            load(maskf[:, 0, :], t["c_mask_qk"])
            load(maskf[:, 1, :], t["c_mask_kq"])
            load(iota[:, :], t["c_iota"])
            load(wo[0][:, :], t["wo0"])
            load(wq[1][:, :], t["wq1"])
            load(wkv[1][:, :], t["wkv1"])
            load(wo[1][:, :], t["wo1"])
            load(qkvb[:, :], t["qkvb"])
            load(ob[:, :], t["ob"])
            load(wg[:, :], t["wg"])
            load(bg[:, :], t["bg"])
            load(w1[:, :, :], t["w1"])
            load(b1[:, :, :], t["b1"])
            load(w2[:, :, :, :], t["w2"])
            load(b2[:, :], t["b2"])
            load(fw1[:, :], t["fw1"])
            load(fw2[:, :, :], t["fw2"])
            load(fb1[:, :], t["fb1"].broadcast_to([128, F]))
            load(fb2[:, :], t["fb2"].broadcast_to([128, D]))

            with sp.Fori(0, B - 1, 2) as n:
                for p in range(2):
                    sp.wait_ge(f_out, n + (p + 1))
                    sp.dma_start(out[:, bass.ds(n + p, 1), :].rearrange("p a b -> p (a b)"),
                                 yout[p][:, :]).then_inc(out_done[p], 16)
            for p in range(2):
                sp.wait_ge(out_done[p], 16 * (B // 2))

        @block.gpsimd
        def _(pool):
            pool.memset(minus_half[:, :], -0.5).then_inc(consts_pool, 1)
            pool.memset(stack[:, :, :], 0.0).then_inc(consts_pool, 1)
            for i in range(2):
                pool.memset(V[i][:, :, :], 1.0).then_inc(consts_pool, 1)
            pool.memset(msplit[:, :], 0.0).then_inc(consts_pool, 1)
            pool.memset(ones[:, :], 1.0).then_inc(consts_pool, 1)
            pool.memset(onesq[:, :], 1.0).then_inc(consts_pool, 1)
            pool.wait_ge(consts_pool, 7)
            pool.wait_ge(loaded, LOADS)
            for k in range(4):
                pool.wait_ge(ln_step, LN_STEPS * (k + 1))
                pool.tensor_tensor(rstd[:, :], var2[:, :], minus_half[:, :], ALU.pow).then_inc(rstd_ready, 1)
                if k in (0, 2):
                    a = layers[k // 2]

                    def context(a, n, p):
                        after(pool, a.proj_ps, n - 1)
                        pool.tensor_copy(ctx_now[p][:, :], one(ctxT, n)).then_inc(a.ctx_ready, 1)

                    if k == 2:
                        pool.wait_ge(layers[0].proj_ps, B)
                    context(a, 0, 0)
                    context(a, 1, 1)
                    with pool.Fori(2, B - 1, 2) as n:
                        context(a, n, 0)
                        context(a, n + 1, 1)
            pool.wait_ge(layers[1].x_done, B)

            def biased(n):
                after(pool, f_out, n)
                pool.tensor_tensor(xb[:, :], one(X, n), fb2[:, :], ALU.add).then_inc(f_xb, 1)

            biased(0)
            with pool.Fori(1, B) as n:
                biased(n)

        @block.tensor
        def _(pe):
            def turn_xn(a, k, p):
                pe.wait_ge(a.xn_ready, k + 1)
                after(pe, a.v_copied, k)
                after(pe, a.mT_sb, k - 1)
                pe.transpose(M[0][:, 0:128], xn[p][:, :], ident[:, :]).then_inc(a.xnT_ps, 1)

            def project(a, L, k, p):
                pe.wait_ge(a.ctx_ready, k + 1)
                pe.wait_ge(a.xnT_sb, k + 1)
                if L == 1:
                    pe.matmul(M[0][:, 128:512], ones[0:1, :], qkvb[0:1, :], start=True, stop=False,
                              skip_group_check=True)
                pe.matmul(M[0][:, 128:256], xnT[p][:, :], wq[L][:, :], start=(L == 0), stop=True,
                          skip_group_check=True)
                pe.matmul(M[0][:, 256:512], ctx_now[p][:, :], wkv[L][:, :], start=(L == 0), stop=True,
                          skip_group_check=True).then_inc(a.proj_ps, 1)

            def turn_q(a, k):
                pe.wait_ge(a.l_ready, k + 1)
                pe.wait_ge(a.dup_ready, k + 1)
                after(pe, a.kT_sb, k)
                for j in range(H // 2):
                    mm = pe.transpose(Mb[1][:, j * 128:(j + 1) * 128],
                                      stack[:, 2 * j:2 * j + 2, :].rearrange("p a b -> p (a b)"), identb[:, :])
                mm.then_inc(a.qT_ps, 1)

            def turn_k(a, k):
                pe.wait_ge(a.qT_sb, k + 1)
                for j in range(H // 2):
                    mm = pe.transpose(Mb[1][:, j * 128:(j + 1) * 128],
                                      stack[:, H + 2 * j:H + 2 * j + 2, :].rearrange("p a b -> p (a b)"),
                                      identb[:, :])
                mm.then_inc(a.kT_ps, 1)

            def masked(L, which, pair):
                if L == 1:
                    for b in range(2):
                        pe.matmul(pair[:, b, :, :], identb[:, :],
                                  mask[:, which:which + 1, :].broadcast_to([128, 4, 128]), start=True, stop=False,
                                  skip_group_check=True)

            def scores(a, L, k, p, u):
                if u == 0:
                    pe.wait_ge(a.qT_sb, k + 1)
                    pe.wait_ge(a.kT_sb, k + 1)
                after(pe, (a.exp0, a.exp1)[u], k)
                masked(L, 0, pairs[u])
                for i in range(4):
                    for b in range(2):
                        r, j = 64 * b, 4 * u + i
                        mm = pe.matmul(pairs[u][:, b, i, :], QT[p][r:r + ROWS, j, :], KT[p][r:r + ROWS, j, :],
                                       start=(L == 0), stop=True, skip_group_check=True)
                mm.then_inc((a.s0_ps, a.s1_ps)[u], 1)

            def turn_max(a, k):
                pe.wait_ge(a.ms_ready, k + 1)
                after(pe, a.v_copied, k + 2 if not isinstance(k, int) else min(k + 2, B))
                pe.transpose(Mb[0][:, 0:128], msplit[:, :], identb[:, :]).then_inc(a.mT_ps, 1)

            def scores_turned(a, L, k, p, u):
                pe.wait_ge((a.max0, a.max1)[u], k + 1)
                if u == 0:
                    pe.wait_ge(a.mT_sb, k + 1)
                masked(L, 1, pairs[u])
                for i in range(4):
                    for b in range(2):
                        r, j = 64 * b, 4 * u + i
                        pe.matmul(pairs[u][:, b, i, :], KT[p][r:r + ROWS, j, :], QT[p][r:r + ROWS, j, :],
                                  start=(L == 0), stop=False, skip_group_check=True)
                        mm = pe.matmul(pairs[u][:, b, i, :], pick[r:r + 64, 2 * j + b, :], mT[r:r + 64, :],
                                       start=False, stop=True, skip_group_check=True)
                mm.then_inc((a.st0_ps, a.st1_ps)[u], 1)

            def weighted(a, k, p, u):
                pe.wait_ge((a.exp0, a.exp1)[u], k + 1)
                if u == 0:
                    pe.wait_ge(a.v_copied, k + 1)
                    after(pe, a.oT_sb, k)
                for j in range(2 * u, 2 * u + 2):
                    for c in range(4):
                        h = 4 * j + c
                        mm = pe.matmul(M[2][32 * c:32 * c + 32, 128 * j:128 * j + 128], V[p][:, h, :],
                                       PT[u][:, 4 * (h % 2) + (h % 8) // 2, :], start=True, stop=True,
                                       skip_group_check=True)
                if u == 1:
                    mm.then_inc(a.pv1, 1)

            def turn_o(a, k):
                pe.wait_ge(a.oT_sb, k + 1)
                after(pe, a.x_done, k)
                for j in range(4):
                    mm = pe.transpose(M[3][:, j * 128:(j + 1) * 128], oT[:, j, :], ident[:, :])
                mm.then_inc(a.o_ps, 1)

            def turn_on(a, k):
                pe.wait_ge(a.on_ready, k + 1)
                pe.transpose(M[3][:, 0:128], on[:, :], ident[:, :]).then_inc(a.onT_ps, 1)

            def project_out(a, L, k):
                pe.wait_ge(a.onT_sb, k + 1)
                if L == 1:
                    pe.matmul(M[3][:, 128:256], ones[0:1, :], ob[0:1, :], start=True, stop=False,
                              skip_group_check=True)
                pe.matmul(M[3][:, 128:256], onT[:, :], wo[L][:, :], start=(L == 0), stop=True,
                          skip_group_check=True).then_inc(a.y_ps, 1)

            def attention(L):
                a = layers[L]

                def step(n, p, there):
                    q = 1 - p
                    if there(0):
                        scores_turned(a, L, n, p, 0)
                        scores_turned(a, L, n, p, 1)
                    if there(-1):
                        turn_o(a, n - 1)
                    if there(1):
                        scores(a, L, n + 1, q, 0)
                    if there(0):
                        weighted(a, n, p, 0)
                    if there(1):
                        scores(a, L, n + 1, q, 1)
                    if there(0):
                        weighted(a, n, p, 1)
                    if there(-1):
                        turn_on(a, n - 1)
                    if there(2):
                        turn_q(a, n + 2)
                    if there(-1):
                        project_out(a, L, n - 1)
                    if there(1):
                        turn_max(a, n + 1)
                    if there(3):
                        turn_xn(a, n + 3, q)
                    if there(2):
                        turn_k(a, n + 2)
                    if there(3):
                        project(a, L, n + 3, q)

                pipeline(pe, step)

            def moe_front(g, p):
                pe.wait_ge(m_xg, (g + 1) * G)
                after(pe, m_xgT_sb, g)
                for b in range(G):
                    mm = pe.transpose(M[0][:, b * 128:(b + 1) * 128], xg[:, b, :], ident[:, :])
                mm.then_inc(m_xgT_ps, 1)
                pe.wait_ge(m_xgT_sb, g + 1)
                after(pe, m_combT_sb, g)
                for b in range(G):
                    pe.matmul(M[1][:, b * E:(b + 1) * E], ones[0:1, :], bg[0:1, :], start=True, stop=False,
                              skip_group_check=True)
                    mm = pe.matmul(M[1][:, b * E:(b + 1) * E], xgT[p][:, b, :], wg[:, :], start=False, stop=True,
                                   skip_group_check=True)
                mm.then_inc(m_logit_ps, 1)

            def moe_comb(g, p):
                pe.wait_ge(m_comb, g + 1)
                for b in range(G):
                    mm = pe.transpose(M[1][0:E, b * 128:(b + 1) * 128], comb[p][:, b, :], ident[:, :])
                mm.then_inc(m_combT_ps, 1)

            def moe_hidden(g, p, e):
                for c in range(NCH):
                    k = e * NCH + c
                    bank = pairs[e % 2][:, c, :, :]
                    after(pe, m_h_sb, g * (E * NCH) + (k - 2 * NCH + 1))
                    pe.matmul(bank, w1[:, e, c * 128:(c + 1) * 128], xgT[p][:, :, :], start=True,
                              stop=True).then_inc(m_h_ps, 1)

            def moe_out(g, e):
                j = e + 1
                after(pe, m_y_added, g * ((E + 1) * G) + (j - 1) * G)
                pe.wait_ge(m_h_sb, g * (E * NCH) + (e + 1) * NCH)
                for b in range(G):
                    for c in range(NCH):
                        mm = pe.matmul(M[2 + j % 2][:, b * 128:(b + 1) * 128], hid[e % 2][c][:, b, :],
                                       w2[:, e, c, :], start=(c == 0), stop=(c == NCH - 1), skip_group_check=True)
                mm.then_inc(m_y_ps, 1)

            def moe_bias(g, p):
                pe.wait_ge(m_combT_sb, g + 1)
                after(pe, m_y_added, g * ((E + 1) * G))
                for b in range(G):
                    mm = pe.matmul(M[2][:, b * 128:(b + 1) * 128], combT[p][:, b, :], b2[:, :], start=True,
                                   stop=True, skip_group_check=True)
                mm.then_inc(m_y_ps, 1)

            def moe():
                def step(g, p, front=True):
                    moe_bias(g, p)
                    moe_hidden(g, p, 0)
                    for e in range(1, E):
                        moe_hidden(g, p, e)
                        moe_out(g, e - 1)
                        if front and e == 2:
                            moe_front(g + 1, 1 - p)
                        if front and e == 5:
                            moe_comb(g + 1, 1 - p)
                    moe_out(g, E - 1)

                moe_front(0, 0)
                moe_comb(0, 0)
                step(0, 0)
                with pe.Fori(1, NG - 2, 2) as g:
                    step(g, 1)
                    step(g + 1, 0)
                step(NG - 1, 1, front=False)

            def ffn_up(n, p):
                pe.wait_ge(f_xq, n + 1)
                after(pe, f_xqT_sb, n)
                pe.transpose(Mb[0][:, 0:128], fxq[:, :], identb[:, :]).then_inc(f_xqT_ps, 1)
                pe.wait_ge(f_xqT_sb, n + 1)
                after(pe, f_hpre, n)
                pe.matmul(M[1][:, :], fxqT[:, :], fw1q[:, :], start=True, stop=True).then_inc(f_h_ps, 1)

            def ffn_down(n):
                pe.wait_ge(f_hq, n + 1)
                after(pe, f_hqT_sb, n)
                for c in range(FC):
                    mm = pe.transpose(Mb[2][:, c * 128:(c + 1) * 128], hq[:, c * 128:(c + 1) * 128], identb[:, :])
                mm.then_inc(f_hqT_ps, 1)
                pe.wait_ge(f_hqT_sb, n + 1)
                after(pe, f_out, n)
                for c in range(FC):
                    mm = pe.matmul(M[3][:, 0:128], hqT[:, c, :], fw2q[:, c, :], start=(c == 0), stop=(c == FC - 1))
                mm.then_inc(f_y_ps, 1)

            def ffn():
                def step(n, p, front=True):
                    if front:
                        ffn_up(n + 1, 1 - p)
                    ffn_down(n)

                ffn_up(0, 0)
                for n in range(3):
                    step(n, n % 2)
                with pe.Fori(3, B - 2, 2) as n:
                    step(n, 1)
                    step(n + 1, 0)
                step(B - 1, 1, front=False)

            pe.wait_ge(loaded, LOADS)
            pe.wait_ge(consts_pool, 7)
            pe.wait_ge(consts_dve, 3)
            pe.wait_ge(wabs_ready, 2)
            pe.matmul(M[3][:, 0:2], onesq[:, :], wsum[:, :], start=True, stop=True).then_inc(wsum_ps, 1)
            pe.wait_ge(wstep, 6)
            attention(0)
            pe.wait_ge(layers[0].x_done, B)
            moe()
            pe.wait_ge(m_y_added, NG * (E + 1) * G)
            attention(1)
            pe.wait_ge(layers[1].x_done, B)
            ffn()

        @block.scalar
        def _(act):
            def xnT_out(a, k, p):
                act.wait_ge(a.xnT_ps, k + 1)
                act.copy(xnT[p][:, :], M[0][:, 0:128]).then_inc(a.xnT_sb, 1)

            def v_out(a, k, p):
                act.wait_ge(a.proj_read, k + 1)
                after(act, a.pv1, k - 1)
                act.copy(V[p][:, :, 0:DH], M[0][:, 384:512].rearrange("p (h d) -> p h d", h=H)).then_inc(a.v_copied, 1)

            def high_parts(a, k):
                act.wait_ge(a.qk_ready, k + 1)
                after(act, a.kT_ps, k)
                view = stack[:, :, 0:ROWS].rearrange("p h (s d) -> p h s d", d=DH)
                act.copy(view[:, 0:H, 1:4, :], qk[:, 0:H, :].unsqueeze(2).broadcast_to([128, H, 3, DH])
                         ).then_inc(a.h_ready, 1)
                act.copy(view[:, H:, 0:5:2, :], qk[:, H:, :].unsqueeze(2).broadcast_to([128, H, 3, DH])
                         ).then_inc(a.h_ready, 1)

            def middle_again(a, k):
                act.wait_ge(a.m_ready, k + 1)
                view = stack[:, :, 0:ROWS].rearrange("p h (s d) -> p h s d", d=DH)
                act.copy(view[:, 0:H, 0, :], view[:, 0:H, 5, :])
                act.copy(view[:, H:, 1, :], view[:, H:, 5, :]).then_inc(a.dup_ready, 1)

            def qT_out(a, k, p):
                act.wait_ge(a.qT_ps, k + 1)
                after(act, a.st1_ps, k - 1)
                act.copy(QT[p][:, :, :], Mb[1][:, :].rearrange("p (j q) -> p j q", j=H // 2)).then_inc(a.qT_sb, 1)

            def kT_out(a, k, p):
                act.wait_ge(a.kT_ps, k + 1)
                act.copy(KT[p][:, :, :], Mb[1][:, :].rearrange("p (j q) -> p j q", j=H // 2)).then_inc(a.kT_sb, 1)

            def exps(a, k, u):
                act.wait_ge((a.st0_ps, a.st1_ps)[u], k + 1)
                after(act, a.pv1, k)
                act.activation(PT[u][:, :, :], pairs[u][:, :, :, :].rearrange("p b i q -> p (b i) q"),
                               ACT.Exp).then_inc((a.exp0, a.exp1)[u], 1)

            def oT_out(a, k):
                act.wait_ge(a.pv1, k + 1)
                after(act, a.o_ps, k)
                act.copy(oT[:, :, :], M[2][:, :].rearrange("p (j q) -> p j q", j=4)).then_inc(a.oT_sb, 1)

            def onT_out(a, k):
                act.wait_ge(a.onT_ps, k + 1)
                act.copy(onT[:, :], M[3][:, 0:128]).then_inc(a.onT_sb, 1)

            def attention(L):
                a = layers[L]

                def step(n, p, there):
                    q = 1 - p
                    if there(0):
                        exps(a, n, 0)
                    if there(2):
                        high_parts(a, n + 2)
                    if there(0):
                        exps(a, n, 1)
                    if there(2):
                        middle_again(a, n + 2)
                    if there(0):
                        oT_out(a, n)
                    if there(2):
                        v_out(a, n + 2, p)
                    if there(-1):
                        onT_out(a, n - 1)
                    if there(2):
                        qT_out(a, n + 2, p)
                    if there(3):
                        xnT_out(a, n + 3, q)
                    if there(2):
                        kT_out(a, n + 2, p)

                pipeline(act, step)

            def moe_front(g, p):
                act.wait_ge(m_xgT_ps, g + 1)
                act.copy(xgT[p][:, :, :], M[0][:, :].rearrange("p (b q) -> p b q", b=G)).then_inc(m_xgT_sb, 1)

            def moe_gate(g):
                act.wait_ge(m_gate, g * GATE_STEPS + 1)
                act.activation(egap[:, :], gap[:, :], ACT.Exp).then_inc(m_egap, 1)

            def moe_combT(g, p):
                act.wait_ge(m_combT_ps, g + 1)
                act.copy(combT[p][:, :, :], M[1][0:E, :].rearrange("p (b q) -> p b q", b=G)).then_inc(m_combT_sb, 1)

            def moe_relu(g, e):
                for c in range(NCH):
                    act.wait_ge(m_h_ps, g * (E * NCH) + (e * NCH + c + 1))
                    after(act, m_y_ps, g * (E + 1) + e)
                    act.activation(hid[e % 2][c][:, :, :], pairs[e % 2][:, c, :, :], ACT.Relu,
                                   bias=b1[:, e, c:c + 1]).then_inc(m_h_sb, 1)

            def moe():
                def step(g, p, front=True):
                    moe_relu(g, 0)
                    for e in range(1, E):
                        moe_relu(g, e)
                        if front and e == 2:
                            moe_front(g + 1, 1 - p)
                            moe_gate(g + 1)
                        if front and e == 5:
                            moe_combT(g + 1, 1 - p)

                moe_front(0, 0)
                moe_gate(0)
                moe_combT(0, 0)
                step(0, 0)
                with act.Fori(1, NG - 2, 2) as g:
                    step(g, 1)
                    step(g + 1, 0)
                step(NG - 1, 1, front=False)

            def ffn_up(n, p):
                act.wait_ge(f_xqT_ps, n + 1)
                act.copy(fxqT[:, :], Mb[0][:, 0:128]).then_inc(f_xqT_sb, 1)
                act.wait_ge(f_hpre, n + 1)
                after(act, f_hr, n - 1)
                act.activation(hact[p][:, :], hpre[p][:, :], ACT.Gelu).then_inc(f_gelu, 1)

            def ffn_down(n):
                act.wait_ge(f_hqT_ps, n + 1)
                act.copy(hqT[:, :, :], Mb[2][:, 0:F].rearrange("p (c q) -> p c q", c=FC)).then_inc(f_hqT_sb, 1)

            act.wait_ge(loaded, LOADS)
            act.wait_ge(consts_pool, 7)
            attention(0)
            moe()
            attention(1)

            def ffn_step(n, p, front=True):
                if front:
                    ffn_up(n + 1, 1 - p)
                ffn_down(n)

            ffn_up(0, 0)
            for n in range(3):
                ffn_step(n, n % 2)
            with act.Fori(3, B - 2, 2) as n:
                ffn_step(n, 1)
                ffn_step(n + 1, 0)
            ffn_step(B - 1, 1, front=False)

        @block.vector
        def _(dve):
            def moments(k):
                dve.wait_ge(stats_ready, B * (k + 1))
                if k > 0:
                    dve.wait_ge(rstd_ready, k)
                base = LN_STEPS * k
                dve.tensor_tensor(mean[:, :], stats[:, :, 1], stats[:, :, 4], ALU.add).then_inc(ln_step, 1)
                dve.tensor_tensor(half_d[:, :], stats[:, :, 1], stats[:, :, 4], ALU.subtract)
                dve.tensor_tensor(var[:, :], stats[:, :, 2], stats[:, :, 5], ALU.add).then_inc(ln_step, 1)
                dve.wait_ge(ln_step, base + 2)
                dve.scalar_tensor_tensor(half_d[:, :], half_d[:, :], 0.25, half_d[:, :], ALU.mult,
                                         ALU.mult).then_inc(ln_step, 1)
                dve.tensor_scalar(var[:, :], var[:, :], 1.0 / D, EPS, ALU.mult, ALU.add)
                dve.tensor_scalar(mean[:, :], mean[:, :], 0.5, None, ALU.mult).then_inc(ln_step, 1)
                dve.wait_ge(ln_step, base + 4)
                dve.tensor_tensor(var2[:, :], var[:, :], half_d[:, :], ALU.add).then_inc(ln_step, 1)
                dve.wait_ge(rstd_ready, k + 1)

            def normalised(dst, n):
                return dve.tensor_scalar(dst, one(X, n), mean[:, bass.ds(n, 1)], rstd[:, bass.ds(n, 1)],
                                         ALU.subtract, ALU.mult)

            def normalise(a, k, p):
                after(dve, a.xnT_ps, k - 1)
                normalised(xn[p][:, :], k).then_inc(a.xn_ready, 1)

            def rotate(a, L, k):
                dve.wait_ge(a.proj_ps, k + 1)
                after(dve, a.qk_ready, k)
                P4 = M[0][:, 128:384].rearrange("p (a h d) -> p a h d", a=2, d=DH)
                r1 = rot1[:, :, :].rearrange("p (a h) d -> p a h d", a=2)
                r2 = rot2[:, :, :].rearrange("p (a h) d -> p a h d", a=2)
                c, s, hd = rope_c[L], rope_s[L], DH // 2
                dve.tensor_tensor(r1, P4, c[:, :, :].unsqueeze(2).broadcast_to([128, 2, H, DH]), ALU.mult)
                dve.tensor_tensor(r2[:, :, :, 0:hd], P4[:, :, :, hd:DH],
                                  s[:, :, 0:hd].unsqueeze(2).broadcast_to([128, 2, H, hd]), ALU.mult)
                dve.tensor_tensor(r2[:, :, :, hd:DH], P4[:, :, :, 0:hd],
                                  s[:, :, hd:DH].unsqueeze(2).broadcast_to([128, 2, H, hd]),
                                  ALU.mult).then_inc(a.proj_read, 1)

            def rotated(a, k):
                dve.wait_ge(a.proj_read, k + 1)
                after(dve, a.h_ready, 2 * k)
                after(dve, a.rest_ready, k)
                dve.tensor_tensor(qk[:, :, :], rot1[:, :, :], rot2[:, :, :], ALU.add).then_inc(a.qk_ready, 1)

            view = stack[:, :, 0:ROWS].rearrange("p h (s d) -> p h s d", d=DH)

            def split_middle(a, k):
                dve.wait_ge(a.h_ready, 2 * k + 2)
                after(dve, a.l_ready, k)
                dve.tensor_tensor(qk_rest[:, :, :], qk[:, :, :], view[:, :, 2, :],
                                  ALU.subtract).then_inc(a.rest_ready, 1)
                dve.wait_ge(a.rest_ready, k + 1)
                dve.tensor_copy(view[:, :, 5, :], qk_rest[:, :, :]).then_inc(a.m_ready, 1)

            def split_low(a, k):
                dve.wait_ge(a.m_ready, k + 1)
                dve.tensor_tensor(view[:, 0:H, Q_L, :], qk_rest[:, 0:H, :], view[:, 0:H, 5, :], ALU.subtract)
                dve.tensor_tensor(view[:, H:, K_L, :], qk_rest[:, H:, :], view[:, H:, 5, :],
                                  ALU.subtract).then_inc(a.l_ready, 1)

            def maxima(a, k, u):
                dve.wait_ge((a.s0_ps, a.s1_ps)[u], k + 1)
                after(dve, a.ms_ready, k)
                dve.tensor_reduce(nmax[:, 8 * u:8 * u + 8].rearrange("p (i b) -> p b i", b=2),
                                  pairs[u][:, :, :, :], AX.X, ALU.max, negate=True).then_inc((a.max0, a.max1)[u], 1)

            halves = msplit[:, :].rearrange("p (r c) -> p r c", r=2)
            nmax_twice = nmax[:, :].unsqueeze(1).broadcast_to([128, 2, H])

            def max_high(a, k):
                after(dve, a.mT_ps, k)
                dve.wait_ge(a.max1, k + 1)
                dve.tensor_copy(halves[:, :, 0:H], nmax_twice).then_inc(a.mh_ready, 1)

            def max_low(a, k):
                dve.wait_ge(a.mh_ready, k + 1)
                dve.tensor_tensor(halves[:, :, H:2 * H], nmax_twice, halves[:, :, 0:H],
                                  ALU.subtract).then_inc(a.ms_ready, 1)

            def mT_out(a, k):
                dve.wait_ge(a.mT_ps, k + 1)
                after(dve, a.st1_ps, k)
                dve.tensor_copy(mT[:, :], Mb[0][:, 0:128]).then_inc(a.mT_sb, 1)

            O = M[3][:, :].rearrange("p (h d) -> p h d", h=H)

            def denominators(a, k):
                dve.wait_ge(a.o_ps, k + 1)
                dve.reciprocal(rden[:, :], O[:, :, DH]).then_inc(a.rden_ready, 1)

            def divide(a, k):
                dve.wait_ge(a.rden_ready, k + 1)
                after(dve, a.onT_ps, k)
                dve.tensor_tensor(on[:, :].rearrange("p (h d) -> p h d", h=H), O[:, :, 0:DH],
                                  rden[:, :].unsqueeze(2).broadcast_to([128, H, DH]), ALU.mult).then_inc(a.on_ready, 1)

            def residual(a, k):
                dve.wait_ge(a.y_ps, k + 1)
                dve.tensor_tensor(one(X, k), M[3][:, 128:256], one(X, k), ALU.add).then_inc(a.x_done, 1)

            def next_stats(a, k):
                dve.wait_ge(a.x_done, k + 1)
                dve.bn_stats(one(stats, k), one(X, k)).then_inc(stats_ready, 1)

            def attention(L):
                a = layers[L]

                def step(n, p, there):
                    if there(2):
                        rotate(a, L, n + 2)
                        rotated(a, n + 2)
                    if there(-1):
                        denominators(a, n - 1)
                        divide(a, n - 1)
                    if there(2):
                        split_middle(a, n + 2)
                    if there(1):
                        maxima(a, n + 1, 0)
                    if there(2):
                        split_low(a, n + 2)
                    if there(1):
                        maxima(a, n + 1, 1)
                    if there(3):
                        normalise(a, n + 3, 1 - p)
                    if there(1):
                        max_high(a, n + 1)
                    if there(-1):
                        residual(a, n - 1)
                    if there(1):
                        max_low(a, n + 1)
                    if there(-1):
                        next_stats(a, n - 1)
                    if there(1):
                        mT_out(a, n + 1)

                pipeline(dve, step)

            def moe_front(g, p):
                after(dve, m_xgT_ps, g)
                for b in range(G):
                    normalised(xg[:, b, :], g * G + b).then_inc(m_xg, 1)

            def moe_gate(g, p):
                base = g * GATE_STEPS
                k = [0]

                def step(ins):
                    k[0] += 1
                    ins.then_inc(m_gate, 1)

                dve.wait_ge(m_logit_ps, g + 1)
                dve.tensor_copy(logit[:, :, :], M[1][:, 0:G * E].rearrange("p (b e) -> p b e", b=G)
                                ).then_inc(m_logit_sb, 1)
                dve.wait_ge(m_logit_sb, g + 1)
                after(dve, m_carry, 2 * g)
                dve.memset(carry[:, 0:1], 0.0).then_inc(m_carry, 1)
                for b in range(G):
                    dve.max(top[:, b, :], logit[:, b, :]).then_inc(m_top, 1)
                dve.wait_ge(m_top, (g + 1) * G)
                after(dve, m_carry, 2 * g)
                dve.memset(carry[:, 1:2], 0.0).then_inc(m_carry, 1)
                for b in range(G):
                    dve.max_index(topi[:, b, :], top[:, b, :], logit[:, b, :]).then_inc(m_topi, 1)
                after(dve, m_egap, g)
                step(dve.tensor_tensor(gap[:, :], top[:, :, 1], top[:, :, 0], ALU.subtract))
                dve.wait_ge(m_topi, (g + 1) * G)
                step(dve.tensor_copy(topf[:, :, :], topi[:, :, :]))
                dve.wait_ge(m_egap, g + 1)
                step(dve.tensor_scalar(egap1[:, :], egap[:, :], 1.0, None, ALU.add))
                dve.wait_ge(m_gate, base + 3)
                step(dve.reciprocal(w_first[:, :], egap1[:, :]))
                wide = iota[:, :].unsqueeze(1).broadcast_to([128, G, E])
                step(dve.tensor_tensor(pick1[:, :, :], wide, topf[:, :, 0:1].broadcast_to([128, G, E]), ALU.is_equal))
                step(dve.tensor_tensor(pick2[:, :, :], wide, topf[:, :, 1:2].broadcast_to([128, G, E]), ALU.is_equal))
                dve.wait_ge(m_gate, base + 6)
                step(dve.tensor_tensor(w_second[:, :], egap[:, :], w_first[:, :], ALU.mult))
                step(dve.tensor_tensor(pick1[:, :, :], pick1[:, :, :],
                                       w_first[:, :].unsqueeze(2).broadcast_to([128, G, E]), ALU.mult))
                dve.wait_ge(m_gate, base + 8)
                step(dve.tensor_tensor(pick2[:, :, :], pick2[:, :, :],
                                       w_second[:, :].unsqueeze(2).broadcast_to([128, G, E]), ALU.mult))
                assert k[0] == GATE_STEPS
                dve.wait_ge(m_gate, base + 9)
                dve.tensor_tensor(comb[p][:, :, :], pick1[:, :, :], pick2[:, :, :], ALU.add).then_inc(m_comb, 1)

            def moe_add(g, p, j):
                base = g * ((E + 1) * G)
                dve.wait_ge(m_y_ps, g * (E + 1) + (j + 1))
                for b in range(G):
                    after(dve, m_y_added, base + ((j - 1) * G + b + 1) if j > 0 else 0)
                    if j > 0:
                        dve.wait_ge(m_comb, g + 1)
                    Y = M[2 + j % 2][:, b * 128:(b + 1) * 128]
                    x = one(X, g * G + b)
                    if j == 0:
                        dve.tensor_tensor(x, Y, x, ALU.add).then_inc(m_y_added, 1)
                    else:
                        dve.scalar_tensor_tensor(x, Y, comb[p][:, b, j - 1:j], x, ALU.mult,
                                                 ALU.add).then_inc(m_y_added, 1)

            def moe_stats(g):
                dve.wait_ge(m_y_added, (g + 1) * ((E + 1) * G))
                for b in range(G):
                    dve.bn_stats(one(stats, g * G + b), one(X, g * G + b)).then_inc(stats_ready, 1)

            def moe():
                def step(g, p, front=True):
                    moe_add(g, p, 0)
                    for e in range(1, E):
                        moe_add(g, p, e)
                        if front and e == 1:
                            moe_front(g + 1, 1 - p)
                        if front and e == 2:
                            moe_gate(g + 1, 1 - p)
                    moe_add(g, p, E)
                    moe_stats(g)

                moe_front(0, 0)
                moe_gate(0, 0)
                step(0, 0)
                with dve.Fori(1, NG - 2, 2) as g:
                    step(g, 1)
                    step(g + 1, 0)
                step(NG - 1, 1, front=False)

            def scales(done, s, n, p, width_scale, src):
                dve.tensor_reduce(s[:, p, 0:1], src, AX.X, ALU.max, apply_absolute_value=True).then_inc(done, 1)
                dve.wait_ge(done, 4 * n + 1)
                dve.tensor_scalar(s[:, p, 1:2], s[:, p, 0:1], EPS, 1.0 / QB, ALU.max, ALU.mult).then_inc(done, 1)
                dve.wait_ge(done, 4 * n + 2)
                dve.reciprocal(s[:, p, 2:3], s[:, p, 1:2]).then_inc(done, 1)
                dve.tensor_tensor(s[:, p, 3:4], s[:, p, 1:2], width_scale, ALU.mult).then_inc(done, 1)
                dve.wait_ge(done, 4 * n + 4)

            def ffn_up(n, p):
                after(dve, f_xr, n)
                normalised(fxn[:, :], n).then_inc(f_xn, 1)
                dve.wait_ge(f_xn, n + 1)
                scales(f_amax, amax, n, p, wscale[:, 0:1], fxn[:, :])
                dve.tensor_scalar(fxr[:, :], fxn[:, :], amax[:, p, 2:3], MAGIC, ALU.mult, ALU.add).then_inc(f_xr, 1)
                dve.wait_ge(f_xr, n + 1)
                after(dve, f_xqT_ps, n)
                dve.tensor_scalar(fxq[:, :], fxr[:, :], MAGIC, QB, ALU.subtract, ALU.min).then_inc(f_xq, 1)
                dve.wait_ge(f_h_ps, n + 1)
                after(dve, f_gelu, n - 1)
                dve.scalar_tensor_tensor(hpre[p][:, :], M[1][:, :], amax[:, p, 3:4], fb1[:, :], ALU.mult,
                                         ALU.add).then_inc(f_hpre, 1)

            def ffn_down(n, p):
                dve.wait_ge(f_gelu, n + 1)
                scales(f_hmax, hmax, n, p, wscale[:, 1:2], hact[p][:, :])
                after(dve, f_hq, n)
                dve.tensor_scalar(hround[:, :], hact[p][:, :], hmax[:, p, 2:3], MAGIC, ALU.mult,
                                  ALU.add).then_inc(f_hr, 1)
                dve.wait_ge(f_hr, n + 1)
                after(dve, f_hqT_ps, n)
                dve.tensor_scalar(hq[:, :], hround[:, :], MAGIC, QB, ALU.subtract, ALU.min).then_inc(f_hq, 1)

            def ffn_out(n, p):
                dve.wait_ge(f_y_ps, n + 1)
                dve.wait_ge(f_xb, n + 1)
                after(dve, out_done[p], (n - p) * 8)
                dve.scalar_tensor_tensor(yout[p][:, :], M[3][:, 0:128], hmax[:, p, 3:4], xb[:, :], ALU.mult,
                                         ALU.add).then_inc(f_out, 1)

            def ffn():
                def step(n, p, front=True, tail=True):
                    if front:
                        ffn_up(n + 1, 1 - p)
                    ffn_down(n, p)
                    if tail:
                        ffn_out(n - 1, 1 - p)

                ffn_up(0, 0)
                step(0, 0, tail=False)
                step(1, 1)
                step(2, 0)
                with dve.Fori(3, B - 2, 2) as n:
                    step(n, 1)
                    step(n + 1, 0)
                step(B - 1, 1, front=False)
                ffn_out(B - 1, 1)

            dve.wait_ge(loaded, LOADS)
            dve.tensor_copy(identb[:, :], ident[:, :]).then_inc(consts_dve, 1)
            dve.tensor_copy(pick[:, :, :], pickf[:, :, :]).then_inc(consts_dve, 1)
            dve.tensor_copy(mask[:, :, :], maskf[:, :, :]).then_inc(consts_dve, 1)
            for i, w in enumerate((fw1[:, :], fw2[:, :, :].rearrange("p c d -> p (c d)"))):
                dve.tensor_reduce(wsum[:, i:i + 1], w, AX.X, ALU.add, apply_absolute_value=True).then_inc(wabs_ready, 1)
            dve.wait_ge(wsum_ps, 1)
            dve.tensor_scalar(wscale[:, :], M[3][:, 0:2], 1.0 / (D * F), EPS, ALU.mult, ALU.max).then_inc(wstep, 1)
            dve.wait_ge(wstep, 1)
            dve.reciprocal(wrecip[:, :], wscale[:, :]).then_inc(wstep, 1)
            dve.wait_ge(wstep, 2)
            for i, (w, wqt) in enumerate(((fw1[:, :], fw1q[:, :]),
                                          (fw2[:, :, :].rearrange("p c d -> p (c d)"),
                                           fw2q[:, :, :].rearrange("p c d -> p (c d)")))):
                dve.tensor_scalar(w, w, wrecip[:, i:i + 1], MAGIC, ALU.mult, ALU.add).then_inc(wstep, 1)
                dve.wait_ge(wstep, 3 + 2 * i)
                dve.tensor_scalar(wtmp[:, :], w, MAGIC, 1.0, ALU.subtract, ALU.min).then_inc(wstep, 1)
                dve.wait_ge(wstep, 4 + 2 * i)
                last = dve.tensor_scalar(wqt, wtmp[:, :], -1.0, None, ALU.max)
                last.then_inc(consts_dve, 1)
                dve.wait_ge(consts_dve, 4 + i)
            with dve.Fori(0, B - 7, 8) as n:
                for i in range(8):
                    dve.bn_stats(one(stats, n + i), one(X, n + i)).then_inc(stats_ready, 1)
            dve.wait_ge(consts_pool, 7)
            moments(0)
            attention(0)
            moments(1)
            moe()
            moments(2)
            attention(1)
            moments(3)
            ffn()


def constants():
    import numpy as np
    pos = np.arange(S, dtype=np.float32)
    freqs = [10000.0 ** (-np.arange(0, DH, 2, dtype=np.float32) / DH),
             1.0 / 10000.0 ** (np.arange(DH // 2, dtype=np.float32) / (DH // 2))]
    out = {"c_ident": np.eye(128, dtype=np.float32)}
    for i, f in enumerate(freqs):
        ang = pos[:, None] * f.astype(np.float32)[None, :]
        c, s = np.cos(ang), np.sin(ang)
        cc, ss = np.concatenate([c, c], 1), np.concatenate([-s, s], 1)
        q_scale = np.float32(DH ** -0.5)
        out[f"c_rope_c{i}"] = np.stack([cc * q_scale, cc], 1).astype(np.float32)
        out[f"c_rope_s{i}"] = np.stack([ss * q_scale, ss], 1).astype(np.float32)
    pick = np.zeros((2, 64, H, 128), np.float32)
    for h in range(H):
        pick[:, h, h] = 1.0
        pick[:, H + h, h] = 1.0
    out["c_pick"] = pick.reshape(128, H, 128)
    q, k = np.arange(S)[:, None], np.arange(S)[None, :]
    inside = (k <= q) & (k >= q - WINDOW)
    m = np.where(inside, 0.0, -1e30).astype(np.float32)
    out["c_mask_qk"], out["c_mask_kq"] = m, np.ascontiguousarray(m.T)
    out["c_iota"] = np.tile(np.arange(E, dtype=np.float32), (128, 1))
    return out


def kernel(**inputs):
    import numpy as np
    import concourse.bacc as bacc
    from concourse import mybir as mb
    from concourse.bass_utils import run_bass_kernel_spmd as run

    a = {k: np.asarray(v) for k, v in inputs.items()}
    perm = np.arange(D).reshape(H, DH)[:, [0, 2, 4, 6, 1, 3, 5, 7]].reshape(-1)
    arrays = {
        "x": a["x"].transpose(1, 0, 2),
        "ctxT": a["ctx_1024"].transpose(2, 0, 1),
        "wq0": a["L0_xattn_Wq"][:, perm],
        "wkv0": np.concatenate([a["L0_xattn_Wk"][:, perm], a["L0_xattn_Wv"]], 1),
        "wo0": a["L0_xattn_Wo"],
        "wq1": a["L1_xattn_q_w"].T,
        "wkv1": np.concatenate([a["L1_xattn_k_w"].T, a["L1_xattn_v_w"].T], 1),
        "wo1": a["L1_xattn_o_w"].T,
        "qkvb": np.concatenate([a["L1_xattn_q_b"], a["L1_xattn_k_b"], a["L1_xattn_v_b"]])[None],
        "ob": a["L1_xattn_o_b"][None],
        "wg": a["L0_ffn_Wg"],
        "bg": a["L0_ffn_bg"][None],
        "w1": a["L0_ffn_W1"].transpose(1, 0, 2),
        "b1": a["L0_ffn_b1"].reshape(E, NCH, 128).transpose(2, 0, 1),
        "w2": a["L0_ffn_W2"].reshape(E, NCH, 128, D).transpose(2, 0, 1, 3),
        "b2": a["L0_ffn_b2"],
        "fw1": a["L1_ffn_W1"].T,
        "fw2": a["L1_ffn_W2"].T.reshape(FC, 128, D).transpose(1, 0, 2),
        "fb1": a["L1_ffn_b1"][None],
        "fb2": a["L1_ffn_b2"][None],
    }
    arrays.update(constants())
    arrays = {k: np.ascontiguousarray(v) for k, v in arrays.items()}
    nc = bacc.Bacc("TRN2", target_bir_lowering=False, num_devices=1)
    t = {k: nc.dram_tensor(f"in_{k}", v.shape, mb.dt.from_np(v.dtype), kind="ExternalInput").ap()
         for k, v in arrays.items()}
    out = nc.dram_tensor("out_x", (S, B, D), mb.dt.float32, kind="ExternalOutput").ap()
    build(nc, t, out)
    r = run(nc, [{f"in_{k}": v for k, v in arrays.items()}], core_ids=[0])
    return np.ascontiguousarray(r.results[0]["out_x"].transpose(1, 0, 2))
```

```python
from contextlib import ExitStack

import concourse.bass as bass
from concourse import mybir

F32 = mybir.dt.float32
BF16 = mybir.dt.bfloat16
U32 = mybir.dt.uint32
U16 = mybir.dt.uint16
ACT = mybir.ActivationFunctionType
ALU = mybir.AluOpType
AX = mybir.AxisListType

B, S, D = 32, 128, 128
H = 16
DH = D // H
E = 8
HID = 256
NCH = HID // 128
G = 4
NG = B // G
F = 512
FC = F // 128
WINDOW = 64
EPS = 1e-5
QB = 127.0
MAGIC = 1.5 * 2.0 ** 23
SLOT = 64
ROWS = 6 * DH
Q_L, K_L = 4, 3


class AttentionEvents:

    def __init__(self, sem, L):
        self.xn_ready = sem(f"L{L}_xn_ready")
        self.ctx_ready = sem(f"L{L}_ctx_ready")
        self.xnT_ps = sem(f"L{L}_xnT_ps")
        self.xnT_sb = sem(f"L{L}_xnT_sb")
        self.proj_ps = sem(f"L{L}_proj_ps")
        self.proj_read = sem(f"L{L}_proj_read")
        self.v_copied = sem(f"L{L}_v_copied")
        self.qk_ready = sem(f"L{L}_qk_ready")
        self.h_ready = sem(f"L{L}_h_ready")
        self.rest_ready = sem(f"L{L}_rest_ready")
        self.m_ready = sem(f"L{L}_m_ready")
        self.l_ready = sem(f"L{L}_l_ready")
        self.qT_ps = sem(f"L{L}_qT_ps")
        self.kT_ps = sem(f"L{L}_kT_ps")
        self.qT_sb = sem(f"L{L}_qT_sb")
        self.kT_sb = sem(f"L{L}_kT_sb")
        self.s0_ps = sem(f"L{L}_s0_ps")
        self.s1_ps = sem(f"L{L}_s1_ps")
        self.max0 = sem(f"L{L}_max0")
        self.max1 = sem(f"L{L}_max1")
        self.mh_ready = sem(f"L{L}_mh_ready")
        self.ms_ready = sem(f"L{L}_ms_ready")
        self.mT_ps = sem(f"L{L}_mT_ps")
        self.mT_sb = sem(f"L{L}_mT_sb")
        self.st0_ps = sem(f"L{L}_st0_ps")
        self.st1_ps = sem(f"L{L}_st1_ps")
        self.exp0 = sem(f"L{L}_exp0")
        self.exp1 = sem(f"L{L}_exp1")
        self.pv1 = sem(f"L{L}_pv1")
        self.oT_sb = sem(f"L{L}_oT_sb")
        self.o_ps = sem(f"L{L}_o_ps")
        self.rden_ready = sem(f"L{L}_rden_ready")
        self.on_ready = sem(f"L{L}_on_ready")
        self.onT_ps = sem(f"L{L}_onT_ps")
        self.onT_sb = sem(f"L{L}_onT_sb")
        self.y_ps = sem(f"L{L}_y_ps")
        self.x_done = sem(f"L{L}_x_done")


def build(nc, t, out):
    ctx = ExitStack()
    with ctx:
        def sb(name, shape, dt=F32):
            return ctx.enter_context(nc.sbuf_tensor(name, shape, dt))

        def ps(name, shape, dt=F32):
            return ctx.enter_context(nc.psum_tensor(name, shape, dt))

        def sem(name):
            return ctx.enter_context(nc.semaphore(name))

        X = sb("X", [128, B, D])
        ctxT = sb("ctxT", [128, B, S])
        ident = sb("ident", [128, 128])
        identb = sb("identb", [128, 128], BF16)
        rope_c = [sb(f"rope_c{i}", [128, 2, DH]) for i in range(2)]
        rope_s = [sb(f"rope_s{i}", [128, 2, DH]) for i in range(2)]
        pick = sb("pick", [128, H, 128], BF16)
        mask = sb("mask", [128, 2, 128], BF16)
        iota = sb("iota", [128, E])
        wq = [sb(f"wq{i}", [128, D]) for i in range(2)]
        wkv = [sb(f"wkv{i}", [128, 2 * D]) for i in range(2)]
        wo = [sb(f"wo{i}", [128, D]) for i in range(2)]
        biases = sb("biases", [1, 4 * D])
        bias_rest = sb("bias_rest", [1, 2, 4 * D])
        bias_parts = sb("bias_parts", [1, 3, 4 * D], BF16)
        bias3 = sb("bias3", [3, 4 * D], BF16)
        ones3 = sb("ones3", [3, 128], BF16)
        wg = sb("wg", [128, E])
        bg = sb("bg", [E, 1])
        w1 = sb("w1", [128, E, HID])
        b1 = sb("b1", [128, E, NCH])
        w2 = sb("w2", [128, E, NCH, D])
        b2 = sb("b2", [E, D])
        fw1 = sb("fw1", [128, F])
        fw2 = sb("fw2", [128, FC, D])
        fw1q = sb("fw1q", [128, F], BF16)
        fw2q = sb("fw2q", [128, FC, D], BF16)
        fb1 = sb("fb1", [128, F])
        fb2 = sb("fb2", [128, D])
        onesq = sb("onesq", [128, 128])
        half = sb("half", [128, 2])
        magic = sb("magic", [128, 1])
        minus_half = sb("minus_half", [128, 2])
        wsum = sb("wsum", [128, 2])
        wscale = sb("wscale", [128, 2])
        wrecip = sb("wrecip", [128, 2])
        wtmp = sb("wtmp", [128, F])

        stats = sb("stats", [128, B, 6])
        mean = sb("mean", [128, B])
        ln_tmp = [[sb(f"ln_{x}{i}", [128, 2]) for x in ("m", "d", "q", "d2", "q2", "d3", "v")] for i in range(2)]
        rstd = sb("rstd", [128, B])

        xn = [sb(f"xn{i}", [128, D]) for i in range(2)]
        xnT = [sb(f"xnT{i}", [128, 128]) for i in range(2)]
        ctx_now = [sb(f"ctx_now{i}", [128, 128]) for i in range(2)]
        rot1 = sb("rot1", [128, 2 * H, DH])
        rot2 = sb("rot2", [128, 2 * H, DH])
        qk = sb("qk", [128, 2 * H, DH])
        qk_rest = sb("qk_rest", [128, 2 * H, DH])
        stack = [sb(f"stack{i}", [128, 2 * H, SLOT], BF16) for i in range(2)]
        QT = [sb(f"QT{i}", [128, H // 2, 128], BF16) for i in range(2)]
        KT = [sb(f"KT{i}", [128, H // 2, 128], BF16) for i in range(2)]
        V = [sb(f"V{i}", [128, H, 32]) for i in range(4)]
        nmax = sb("nmax", [128, H])
        msplit = sb("msplit", [128, 128], BF16)
        mT = sb("mT", [128, 128], BF16)
        PT = [sb(f"PT{i}", [128, H // 2, 128]) for i in range(2)]
        rden = sb("rden", [128, H])
        on = sb("on", [128, D])
        oT = sb("oT", [128, 4, 128])
        onT = sb("onT", [128, 128])

        xg = sb("xg", [128, G, D])
        xgT = [sb(f"xgT{i}", [128, G, 128]) for i in range(2)]
        lT = sb("lT", [E, G, 128])
        logit = sb("logit", [128, G, E])
        top = sb("top", [128, G, 8])
        topi = sb("topi", [128, G, 8], U32)
        topf = sb("topf", [128, G, 8])
        carry = sb("carry", [128, 2])
        gap = sb("gap", [128, G])
        egap = sb("egap", [128, G])
        egap1 = sb("egap1", [128, G])
        w_first = sb("w_first", [128, G])
        w_second = sb("w_second", [128, G])
        pick1 = sb("pick1", [128, G, E])
        pick2 = sb("pick2", [128, G, E])
        comb = [sb(f"comb{i}", [128, G, E]) for i in range(2)]
        combT = [sb(f"combT{i}", [E, G, 128]) for i in range(2)]
        hid = [[sb(f"hid{i}{c}", [128, G, 128]) for c in range(NCH)] for i in range(2)]

        fxn = sb("fxn", [128, D])
        fxq = sb("fxq", [128, D], BF16)
        fxr = sb("fxr", [128, D])
        fxqT = sb("fxqT", [128, 128], BF16)
        absmax = sb("absmax", [128, 2, 2])
        unit = sb("unit", [128, 2, 2])
        inverse = sb("inverse", [128, 2, 2])
        outscale = sb("outscale", [128, 2, 2])
        hpre = [sb(f"hpre{i}", [128, F]) for i in range(2)]
        hact = [sb(f"hact{i}", [128, F]) for i in range(2)]
        hround = sb("hround", [128, F])
        hq = sb("hq", [128, F], BF16)
        hqT = sb("hqT", [128, FC, 128], BF16)
        xb = sb("xb", [128, D])
        yout = [sb(f"yout{i}", [128, D]) for i in range(2)]

        pairs = [ps(f"pair{i}", [128, 2, 4, 128]) for i in range(2)]
        M = [ps(f"M{i}", [128, 512]) for i in range(4)]
        Mb = [m[:, :].bitcast(BF16) for m in M]

        loaded_first = sem("loaded_first")
        loaded_x = sem("loaded_x")
        loaded = sem("loaded")
        consts_pool = sem("consts_pool")
        bias_step = sem("bias_step")
        bias3_ready = sem("bias3_ready")
        wabs_ready = sem("wabs_ready")
        wsum_ps = sem("wsum_ps")
        wstep = sem("wstep")
        w_ternary = sem("w_ternary")
        out_done = [sem(f"out_done{i}") for i in range(2)]
        LOADS_FIRST, LOADS_X, LOADS = 16 * 8, 16 * 4, 16 * 19
        AHEAD = 8

        stats_ready = [sem(f"stats_ready{i}") for i in range(4)]
        ln_step = [sem(f"ln_step{i}") for i in range(4)]
        ln_ready = [sem(f"ln_ready{i}") for i in range(4)]
        LN_STEPS = 7
        CONSTS = 13
        WARM_UP = 16

        layers = [AttentionEvents(sem, L) for L in range(2)]

        m_xg = sem("m_xg")
        m_xgT_ps = sem("m_xgT_ps")
        m_xgT_sb = sem("m_xgT_sb")
        m_lT_ps = sem("m_lT_ps")
        m_lT_sb = sem("m_lT_sb")
        m_logit_ps = sem("m_logit_ps")
        m_logit_sb = sem("m_logit_sb")
        m_top = sem("m_top")
        m_carry = sem("m_carry")
        m_topi = sem("m_topi")
        m_gate = sem("m_gate")
        m_egap = sem("m_egap")
        m_comb = sem("m_comb")
        m_combT_ps = sem("m_combT_ps")
        m_combT_sb = sem("m_combT_sb")
        m_h_ps = sem("m_h_ps")
        m_h_sb = sem("m_h_sb")
        m_y_ps = sem("m_y_ps")
        m_y_added = sem("m_y_added")
        GATE_STEPS = 9

        f_xn = sem("f_xn")
        f_x_max = sem("f_x_max")
        f_h_max = sem("f_h_max")
        f_unit = sem("f_unit")
        f_inverse = sem("f_inverse")
        f_outscale = sem("f_outscale")
        f_xr = sem("f_xr")
        f_xq = sem("f_xq")
        f_xqT_ps = sem("f_xqT_ps")
        f_xqT_sb = sem("f_xqT_sb")
        f_h_ps = sem("f_h_ps")
        f_hpre = sem("f_hpre")
        f_gelu = sem("f_gelu")
        f_hr = sem("f_hr")
        f_hq = sem("f_hq")
        f_hqT_ps = sem("f_hqT_ps")
        f_hqT_sb = sem("f_hqT_sb")
        f_y_ps = sem("f_y_ps")
        f_xb = sem("f_xb")
        f_out = sem("f_out")

        def after(eng, s, v):
            if not isinstance(v, int) or v > 0:
                eng.wait_ge(s, v)

        def one(tensor, n):
            return tensor[:, bass.ds(n, 1)].rearrange("p a b -> p (a b)")

        def pipeline(eng, L, step):
            FIRST, LAST, LOOP0, TURNS = -5, B, 3, (5, 6)[L]

            def peeled(n):
                step(n, n % 4, lambda k: 0 <= n + k < B)

            for n in range(FIRST, LOOP0):
                peeled(n)
            if eng is nc.tensor:
                keep_warm(layers[L])
            with eng.Fori(LOOP0, LOOP0 + 4 * (TURNS - 1) + 1, 4) as n:
                for i in range(4):
                    step(n + i, (LOOP0 + i) % 4, lambda k: True)
            for n in range(LOOP0 + 4 * TURNS, LAST + 1):
                peeled(n)

        def ffn_pipeline(eng, step):
            FIRST, LAST, LOOP0, LOOP1 = -2, B, 3, B - 4

            def peeled(n):
                step(n, n % 2, lambda k: 0 <= n + k < B)

            for n in range(FIRST, LOOP0):
                peeled(n)
            with eng.Fori(LOOP0, LOOP1, 2) as n:
                step(n, 1, lambda k: True)
                step(n + 1, 0, lambda k: True)
            for n in range(LOOP1 + 1, LAST + 1):
                peeled(n)

        def keep_warm(a):
            nc.tensor.wait_ge(a.kT_sb, 5)
            for _ in range(WARM_UP):
                nc.tensor.matmul(M[1][:, :], identb[:, :], pick[:, 0:4, :], start=True, stop=True)

        block = ctx.enter_context(nc.Block())

        @block.sync
        def _(sp):
            def load(counter, *pairs):
                for dst, src in pairs:
                    sp.dma_start(dst, src).then_inc(counter, 16)

            load(loaded_first, (X[:, 0:AHEAD, :], t["x"][:, 0:AHEAD, :]), (ident[:, :], t["c_ident"]),
                 (ctxT[:, 0:AHEAD, :], t["ctxT"][:, 0:AHEAD, :]), (wq[0][:, :], t["wq0"]), (wkv[0][:, :], t["wkv0"]),
                 (rope_c[0][:, :, :], t["c_rope_c0"]), (rope_s[0][:, :, :], t["c_rope_s0"]),
                 (identb[:, :].bitcast(U16), t["c_identb"]))
            load(loaded_x, (pick[:, :, :].bitcast(U16), t["c_pick"]), (X[:, AHEAD:, :], t["x"][:, AHEAD:, :]),
                 (ctxT[:, AHEAD:, :], t["ctxT"][:, AHEAD:, :]), (wo[0][:, :], t["wo0"]))
            load(loaded, (mask[:, 0, :].bitcast(U16), t["c_mask_qk"]), (mask[:, 1, :].bitcast(U16), t["c_mask_kq"]),
                 (rope_c[1][:, :, :], t["c_rope_c1"]), (rope_s[1][:, :, :], t["c_rope_s1"]),
                 (iota[:, :], t["c_iota"]), (wq[1][:, :], t["wq1"]), (wkv[1][:, :], t["wkv1"]),
                 (wo[1][:, :], t["wo1"]), (biases[:, :], t["biases"]), (wg[:, :], t["wg"]),
                 (bg[:, :], t["bg"]), (w1[:, :, :], t["w1"]), (b1[:, :, :], t["b1"]), (w2[:, :, :, :], t["w2"]),
                 (b2[:, :], t["b2"]), (fw1[:, :], t["fw1"]), (fw2[:, :, :], t["fw2"]),
                 (fb1[:, :], t["fb1"].broadcast_to([128, F])), (fb2[:, :], t["fb2"].broadcast_to([128, D])))

            sp.wait_ge(bias_step, 5)
            for i in range(3):
                sp.dma_start(bias3[i:i + 1, :], bias_parts[0:1, i, :]).then_inc(bias3_ready, 16)

            with sp.Fori(0, B - 1, 2) as n:
                for p in range(2):
                    sp.wait_ge(f_out, n + (p + 1))
                    sp.dma_start(out[:, bass.ds(n + p, 1), :].rearrange("p a b -> p (a b)"),
                                 yout[p][:, :]).then_inc(out_done[p], 16)
            for p in range(2):
                sp.wait_ge(out_done[p], 16 * (B // 2))

        @block.gpsimd
        def _(pool):
            pool.memset(minus_half[:, :], -0.5).then_inc(consts_pool, 1)
            pool.memset(half[:, :], 0.5).then_inc(consts_pool, 1)
            for i in range(2):
                pool.memset(stack[i][:, :, :], 0.0).then_inc(consts_pool, 1)
            for i in range(4):
                pool.memset(V[i][:, :, :], 1.0).then_inc(consts_pool, 1)
            pool.memset(msplit[:, :], 0.0).then_inc(consts_pool, 1)
            pool.memset(ones3[:, :], 1.0).then_inc(consts_pool, 1)
            pool.memset(onesq[:, :], 1.0).then_inc(consts_pool, 1)
            pool.memset(absmax[:, :, :], 1.0).then_inc(consts_pool, 1)
            pool.memset(magic[:, :], MAGIC).then_inc(consts_pool, 1)
            pool.wait_ge(consts_pool, CONSTS)

            def moments(k, j):
                base = j * LN_STEPS
                at = bass.ds(j * 2, 2)
                pool.wait_ge(stats_ready[k], j * 2 + 2)
                after(pool, ln_ready[k], j * 2)
                if k > 1 and isinstance(j, int) and j == 0:
                    pool.wait_ge(ln_ready[k - 2], B)
                ln_m, ln_d, ln_q, ln_d2, ln_q2, ln_d3, ln_v = ln_tmp[k % 2]
                pool.tensor_tensor(ln_m[:, :], stats[:, at, 1], stats[:, at, 4], ALU.add).then_inc(ln_step[k], 1)
                pool.tensor_tensor(ln_d[:, :], stats[:, at, 1], stats[:, at, 4], ALU.subtract).then_inc(ln_step[k], 1)
                pool.tensor_tensor(ln_q[:, :], stats[:, at, 2], stats[:, at, 5], ALU.add).then_inc(ln_step[k], 1)
                pool.wait_ge(ln_step[k], base + 3)
                pool.tensor_tensor(mean[:, at], ln_m[:, :], half[:, 0:2], ALU.mult).then_inc(ln_ready[k], 1)
                pool.tensor_scalar(ln_d2[:, :], ln_d[:, :], 0.5, None, ALU.mult).then_inc(ln_step[k], 1)
                pool.tensor_scalar(ln_q2[:, :], ln_q[:, :], 1.0 / D, EPS, ALU.mult, ALU.add).then_inc(ln_step[k], 1)
                pool.wait_ge(ln_step[k], base + 5)
                pool.tensor_tensor(ln_d3[:, :], ln_d2[:, :], ln_d2[:, :], ALU.mult).then_inc(ln_step[k], 1)
                pool.wait_ge(ln_step[k], base + 6)
                pool.tensor_tensor(ln_v[:, :], ln_d3[:, :], ln_q2[:, :], ALU.add).then_inc(ln_step[k], 1)
                pool.wait_ge(ln_step[k], base + 7)
                pool.tensor_tensor(rstd[:, at], ln_v[:, :], minus_half[:, 0:2], ALU.pow).then_inc(ln_ready[k], 1)

            def context(a, n, p):
                after(pool, a.proj_ps, n - 1)
                pool.tensor_copy(ctx_now[p][:, :], one(ctxT, n)).then_inc(a.ctx_ready, 1)

            def contexts(a, n):
                context(a, n, 0)
                context(a, n + 1, 1)

            a = layers[0]
            pool.wait_ge(loaded_first, LOADS_FIRST)
            contexts(a, 0)
            moments(0, 0)
            moments(0, 1)
            contexts(a, 2)
            moments(0, 2)
            contexts(a, 4)
            moments(0, 3)
            contexts(a, 6)
            moments(0, 4)
            moments(1, 0)
            pool.wait_ge(loaded_x, LOADS_X)
            with pool.Fori(1, B // 2 - 4) as j:
                moments(0, j + 4)
                contexts(a, j * 2 + 6)
                moments(1, j)
            contexts(a, B - 2)
            for j in range(B // 2 - 4, B // 2):
                moments(1, j)
            moments(2, 0)
            moments(2, 1)
            with pool.Fori(1, NG) as g:
                moments(2, g * 2)
                moments(2, g * 2 + 1)
            a = layers[1]
            contexts(a, 0)
            contexts(a, 2)
            contexts(a, 4)
            contexts(a, 6)
            moments(3, 0)
            with pool.Fori(1, B // 2 - 3) as j:
                contexts(a, j * 2 + 6)
                moments(3, j)
            for j in range(B // 2 - 3, B // 2):
                moments(3, j)
            pool.wait_ge(loaded, LOADS)

            def biased(n):
                after(pool, f_out, n)
                pool.tensor_tensor(xb[:, :], one(X, n), fb2[:, :], ALU.add).then_inc(f_xb, 1)

            biased(0)
            with pool.Fori(1, B) as n:
                biased(n)

        @block.tensor
        def _(pe):
            def turn_xn(a, k, p):
                pe.wait_ge(a.xn_ready, k + 1)
                after(pe, a.v_copied, k)
                pe.transpose(M[0][:, 0:128], xn[p % 2][:, :], ident[:, :]).then_inc(a.xnT_ps, 1)

            def project(a, L, k, p):
                pe.wait_ge(a.ctx_ready, k + 1)
                pe.wait_ge(a.xnT_sb, k + 1)
                if L == 1:
                    pe.matmul(M[0][:, 128:512], ones3[:, :], bias3[:, 0:3 * D], start=True, stop=False,
                              skip_group_check=True)
                pe.matmul(M[0][:, 128:256], xnT[p % 2][:, :], wq[L][:, :], start=(L == 0), stop=True,
                          skip_group_check=True)
                pe.matmul(M[0][:, 256:512], ctx_now[p % 2][:, :], wkv[L][:, :], start=(L == 0), stop=True,
                          skip_group_check=True).then_inc(a.proj_ps, 1)

            def turn_q(a, k, p):
                pe.wait_ge(a.l_ready, k + 1)
                after(pe, a.kT_sb, k)
                for j in range(H // 2):
                    mm = pe.transpose(Mb[1][:, j * 128:(j + 1) * 128],
                                      stack[p % 2][:, 2 * j:2 * j + 2, :].rearrange("p a b -> p (a b)"),
                                      identb[:, :])
                mm.then_inc(a.qT_ps, 1)

            def turn_k(a, k, p):
                pe.wait_ge(a.qT_sb, k + 1)
                for j in range(H // 2):
                    mm = pe.transpose(Mb[1][:, j * 128:(j + 1) * 128],
                                      stack[p % 2][:, H + 2 * j:H + 2 * j + 2, :].rearrange("p a b -> p (a b)"),
                                      identb[:, :])
                mm.then_inc(a.kT_ps, 1)

            def masked(L, which, pair):
                if L == 1:
                    for b in range(2):
                        pe.matmul(pair[:, b, :, :], identb[:, :],
                                  mask[:, which:which + 1, :].broadcast_to([128, 4, 128]), start=True, stop=False,
                                  skip_group_check=True)

            def scores(a, L, k, p, u):
                if u == 0:
                    pe.wait_ge(a.qT_sb, k + 1)
                    pe.wait_ge(a.kT_sb, k + 1)
                after(pe, (a.exp0, a.exp1)[u], k)
                masked(L, 0, pairs[u])
                for i in range(4):
                    for b in range(2):
                        r, j = 64 * b, 4 * u + i
                        mm = pe.matmul(pairs[u][:, b, i, :], QT[p % 2][r:r + ROWS, j, :], KT[p % 2][r:r + ROWS, j, :],
                                       start=(L == 0), stop=True, skip_group_check=True)
                mm.then_inc((a.s0_ps, a.s1_ps)[u], 1)

            def turn_max(a, k):
                pe.wait_ge(a.ms_ready, k + 1)
                after(pe, a.oT_sb, k)
                pe.transpose(Mb[2][:, 0:128], msplit[:, :], identb[:, :]).then_inc(a.mT_ps, 1)

            def scores_turned(a, L, k, p, u):
                pe.wait_ge((a.max0, a.max1)[u], k + 1)
                if u == 0:
                    pe.wait_ge(a.mT_sb, k + 1)
                masked(L, 1, pairs[u])
                for i in range(4):
                    for b in range(2):
                        r, j = 64 * b, 4 * u + i
                        pe.matmul(pairs[u][:, b, i, :], KT[p % 2][r:r + ROWS, j, :], QT[p % 2][r:r + ROWS, j, :],
                                  start=(L == 0), stop=False, skip_group_check=True)
                        mm = pe.matmul(pairs[u][:, b, i, :], pick[r:r + 64, 2 * j + b, :], mT[r:r + 64, :],
                                       start=False, stop=True, skip_group_check=True)
                mm.then_inc((a.st0_ps, a.st1_ps)[u], 1)

            def weighted(a, k, p, u):
                pe.wait_ge((a.exp0, a.exp1)[u], k + 1)
                if u == 0:
                    pe.wait_ge(a.v_copied, k + 1)
                    pe.wait_ge(a.mT_sb, k + 1)
                for j in range(2 * u, 2 * u + 2):
                    for c in range(4):
                        h = 4 * j + c
                        mm = pe.matmul(M[2][32 * c:32 * c + 32, 128 * j:128 * j + 128], V[p][:, h, :],
                                       PT[u][:, 4 * (h % 2) + (h % 8) // 2, :], start=True, stop=True,
                                       skip_group_check=True)
                if u == 1:
                    mm.then_inc(a.pv1, 1)

            def turn_o(a, k):
                pe.wait_ge(a.oT_sb, k + 1)
                after(pe, a.x_done, k)
                for j in range(4):
                    mm = pe.transpose(M[3][:, j * 128:(j + 1) * 128], oT[:, j, :], ident[:, :])
                mm.then_inc(a.o_ps, 1)

            def turn_on(a, k):
                pe.wait_ge(a.on_ready, k + 1)
                pe.transpose(M[3][:, 0:128], on[:, :], ident[:, :]).then_inc(a.onT_ps, 1)

            def project_out(a, L, k):
                pe.wait_ge(a.onT_sb, k + 1)
                if L == 1:
                    pe.matmul(M[3][:, 128:256], ones3[:, :], bias3[:, 3 * D:], start=True, stop=False,
                              skip_group_check=True)
                pe.matmul(M[3][:, 128:256], onT[:, :], wo[L][:, :], start=(L == 0), stop=True,
                          skip_group_check=True).then_inc(a.y_ps, 1)

            def attention(L):
                a = layers[L]

                def step(n, p, there):
                    if L == 0 and isinstance(n, int) and n == 0:
                        pe.wait_ge(loaded_x, LOADS_X)
                    if there(0):
                        scores_turned(a, L, n, p, 0)
                        scores_turned(a, L, n, p, 1)
                    if there(2):
                        turn_q(a, n + 2, p + 2)
                    if there(1):
                        scores(a, L, n + 1, p + 1, 0)
                    if there(4):
                        turn_xn(a, n + 4, p + 4)
                    if there(-1):
                        turn_on(a, n - 1)
                    if there(0):
                        weighted(a, n, p, 0)
                    if there(1):
                        scores(a, L, n + 1, p + 1, 1)
                    if there(0):
                        weighted(a, n, p, 1)
                    if there(2):
                        turn_k(a, n + 2, p + 2)
                    if there(-1):
                        project_out(a, L, n - 1)
                    if there(4):
                        project(a, L, n + 4, p + 4)
                    if there(1):
                        turn_max(a, n + 1)
                    if there(0):
                        turn_o(a, n)

                pipeline(pe, L, step)

            def moe_turn_x(g):
                pe.wait_ge(m_xg, (g + 1) * G)
                after(pe, m_lT_sb, g)
                for b in range(G):
                    mm = pe.transpose(M[0][:, b * 128:(b + 1) * 128], xg[:, b, :], ident[:, :])
                mm.then_inc(m_xgT_ps, 1)

            def moe_logits(g, p):
                pe.wait_ge(m_xgT_sb, g + 1)
                pe.matmul(M[0][0:E, :], wg[:, :], xgT[p][:, :, :], start=True, stop=True).then_inc(m_lT_ps, 1)

            def moe_turn_logits(g):
                pe.wait_ge(m_lT_sb, g + 1)
                after(pe, m_combT_sb, g)
                for b in range(G):
                    mm = pe.matmul(M[1][:, b * E:(b + 1) * E], lT[:, b, :], ident[0:E, 0:E], start=True, stop=True,
                                   skip_group_check=True)
                mm.then_inc(m_logit_ps, 1)

            def moe_comb(g, p):
                pe.wait_ge(m_comb, g + 1)
                for b in range(G):
                    mm = pe.transpose(M[1][0:E, b * 128:(b + 1) * 128], comb[p][:, b, :], ident[:, :])
                mm.then_inc(m_combT_ps, 1)

            def moe_hidden(g, p, e):
                for c in range(NCH):
                    k = e * NCH + c
                    bank = pairs[e % 2][:, c, :, :]
                    after(pe, m_h_sb, g * (E * NCH) + (k - 2 * NCH + 1))
                    pe.matmul(bank, w1[:, e, c * 128:(c + 1) * 128], xgT[p][:, :, :], start=True,
                              stop=True).then_inc(m_h_ps, 1)

            def moe_out(g, p, e):
                j = e + 1
                after(pe, m_y_added, g * ((E + 1) * G) + (j - 1) * G)
                pe.wait_ge(m_h_sb, g * (E * NCH) + (e + 1) * NCH)
                for b in range(G):
                    for c in range(NCH):
                        mm = pe.matmul(M[2 + (j + p) % 2][:, b * 128:(b + 1) * 128], hid[e % 2][c][:, b, :],
                                       w2[:, e, c, :], start=(c == 0), stop=(c == NCH - 1), skip_group_check=True)
                mm.then_inc(m_y_ps, 1)

            def moe_bias(g, p):
                pe.wait_ge(m_combT_sb, g + 1)
                after(pe, m_y_added, g * ((E + 1) * G) - G)
                for b in range(G):
                    mm = pe.matmul(M[2 + p][:, b * 128:(b + 1) * 128], combT[p][:, b, :], b2[:, :], start=True,
                                   stop=True, skip_group_check=True)
                mm.then_inc(m_y_ps, 1)

            def moe():
                def step(g, p, front=True):
                    moe_hidden(g, p, 0)
                    moe_bias(g, p)
                    for e in range(1, E):
                        moe_hidden(g, p, e)
                        moe_out(g, p, e - 1)
                        if front and e == 2:
                            moe_turn_x(g + 1)
                        if front and e == 3:
                            moe_logits(g + 1, 1 - p)
                        if front and e == 4:
                            moe_turn_logits(g + 1)
                        if front and e == 6:
                            moe_comb(g + 1, 1 - p)
                    moe_out(g, p, E - 1)

                moe_turn_x(0)
                moe_logits(0, 0)
                moe_turn_logits(0)
                moe_comb(0, 0)
                step(0, 0)
                pe.wait_ge(wabs_ready, 2)
                pe.wait_ge(m_combT_sb, 2)
                pe.matmul(M[1][:, 0:2], onesq[:, :], wsum[:, :], start=True, stop=True).then_inc(wsum_ps, 1)
                pe.wait_ge(wstep, 1)
                with pe.Fori(1, NG - 2, 2) as g:
                    step(g, 1)
                    step(g + 1, 0)
                step(NG - 1, 1, front=False)

            def ffn_up(n):
                pe.wait_ge(f_xq, n + 1)
                after(pe, f_xqT_sb, n)
                pe.transpose(Mb[0][:, 0:128], fxq[:, :], identb[:, :]).then_inc(f_xqT_ps, 1)
                pe.wait_ge(f_xqT_sb, n + 1)
                after(pe, f_hpre, n)
                pe.matmul(M[1][:, :], fxqT[:, :], fw1q[:, :], start=True, stop=True).then_inc(f_h_ps, 1)

            def ffn_down(n):
                pe.wait_ge(f_hq, n + 1)
                after(pe, f_hqT_sb, n)
                for c in range(FC):
                    mm = pe.transpose(Mb[2][:, c * 128:(c + 1) * 128], hq[:, c * 128:(c + 1) * 128], identb[:, :])
                mm.then_inc(f_hqT_ps, 1)
                pe.wait_ge(f_hqT_sb, n + 1)
                after(pe, f_out, n)
                for c in range(FC):
                    mm = pe.matmul(M[3][:, 0:128], hqT[:, c, :], fw2q[:, c, :], start=(c == 0), stop=(c == FC - 1))
                mm.then_inc(f_y_ps, 1)

            def ffn():
                def step(n, p, there):
                    if there(-1):
                        ffn_down(n - 1)
                    if there(2):
                        ffn_up(n + 2)

                ffn_pipeline(pe, step)

            pe.wait_ge(loaded_first, LOADS_FIRST)
            pe.wait_ge(consts_pool, CONSTS)
            attention(0)
            pe.wait_ge(loaded, LOADS)
            moe()
            pe.wait_ge(bias3_ready, 16 * 3)
            attention(1)
            pe.wait_ge(w_ternary, 2)
            ffn()

        @block.scalar
        def _(act):
            def xnT_out(a, k, p):
                act.wait_ge(a.xnT_ps, k + 1)
                act.copy(xnT[p % 2][:, :], M[0][:, 0:128]).then_inc(a.xnT_sb, 1)

            def v_out(a, k, p):
                act.wait_ge(a.proj_read, k + 1)
                after(act, a.pv1, k - 3)
                act.copy(V[p % 4][:, :, 0:DH], M[0][:, 384:512].rearrange("p (h d) -> p h d", h=H)
                         ).then_inc(a.v_copied, 1)

            def high_parts(a, k, p):
                act.wait_ge(a.qk_ready, k + 1)
                after(act, a.kT_ps, k - 1)
                view = stack[p % 2][:, :, 0:ROWS].rearrange("p h (s d) -> p h s d", d=DH)
                act.copy(view[:, 0:H, 1:4, :], qk[:, 0:H, :].unsqueeze(2).broadcast_to([128, H, 3, DH])
                         ).then_inc(a.h_ready, 1)
                act.copy(view[:, H:, 0:5:2, :], qk[:, H:, :].unsqueeze(2).broadcast_to([128, H, 3, DH])
                         ).then_inc(a.h_ready, 1)

            def qT_out(a, k, p):
                act.wait_ge(a.qT_ps, k + 1)
                after(act, a.st1_ps, k - 1)
                act.copy(QT[p % 2][:, :, :], Mb[1][:, :].rearrange("p (j q) -> p j q", j=H // 2)).then_inc(a.qT_sb, 1)

            def kT_out(a, k, p):
                act.wait_ge(a.kT_ps, k + 1)
                act.copy(KT[p % 2][:, :, :], Mb[1][:, :].rearrange("p (j q) -> p j q", j=H // 2)).then_inc(a.kT_sb, 1)

            def exps(a, k, u):
                act.wait_ge((a.st0_ps, a.st1_ps)[u], k + 1)
                after(act, a.pv1, k)
                act.activation(PT[u][:, :, :], pairs[u][:, :, :, :].rearrange("p b i q -> p (b i) q"),
                               ACT.Exp).then_inc((a.exp0, a.exp1)[u], 1)

            def oT_out(a, k):
                act.wait_ge(a.pv1, k + 1)
                after(act, a.o_ps, k)
                act.copy(oT[:, :, :], M[2][:, :].rearrange("p (j q) -> p j q", j=4)).then_inc(a.oT_sb, 1)

            def onT_out(a, k):
                act.wait_ge(a.onT_ps, k + 1)
                act.copy(onT[:, :], M[3][:, 0:128]).then_inc(a.onT_sb, 1)

            def attention(L):
                a = layers[L]

                def step(n, p, there):
                    if there(3):
                        v_out(a, n + 3, p + 3)
                    if there(0):
                        exps(a, n, 0)
                        exps(a, n, 1)
                    if there(2):
                        qT_out(a, n + 2, p + 2)
                    if there(3):
                        high_parts(a, n + 3, p + 3)
                    if there(4):
                        xnT_out(a, n + 4, p + 4)
                    if there(-1):
                        onT_out(a, n - 1)
                    if there(0):
                        oT_out(a, n)
                    if there(2):
                        kT_out(a, n + 2, p + 2)

                pipeline(act, L, step)

            def moe_front(g, p):
                act.wait_ge(m_xgT_ps, g + 1)
                act.copy(xgT[p][:, :, :], M[0][:, :].rearrange("p (b q) -> p b q", b=G)).then_inc(m_xgT_sb, 1)

            def moe_logits(g):
                act.wait_ge(m_lT_ps, g + 1)
                act.activation(lT[:, :, :], M[0][0:E, :].rearrange("p (b q) -> p b q", b=G), ACT.Identity,
                               bias=bg[:, 0:1]).then_inc(m_lT_sb, 1)

            def moe_gate(g):
                act.wait_ge(m_gate, g * GATE_STEPS + 1)
                act.activation(egap[:, :], gap[:, :], ACT.Exp).then_inc(m_egap, 1)

            def moe_combT(g, p):
                act.wait_ge(m_combT_ps, g + 1)
                act.copy(combT[p][:, :, :], M[1][0:E, :].rearrange("p (b q) -> p b q", b=G)).then_inc(m_combT_sb, 1)

            def moe_relu(g, e):
                for c in range(NCH):
                    act.wait_ge(m_h_ps, g * (E * NCH) + (e * NCH + c + 1))
                    after(act, m_y_ps, g * (E + 1) + e)
                    act.activation(hid[e % 2][c][:, :, :], pairs[e % 2][:, c, :, :], ACT.Relu,
                                   bias=b1[:, e, c:c + 1]).then_inc(m_h_sb, 1)

            def moe():
                def step(g, p, front=True):
                    moe_relu(g, 0)
                    for e in range(1, E):
                        moe_relu(g, e)
                        if front and e == 2:
                            moe_front(g + 1, 1 - p)
                        if front and e == 3:
                            moe_logits(g + 1)
                        if front and e == 4:
                            moe_gate(g + 1)
                        if front and e == 6:
                            moe_combT(g + 1, 1 - p)

                moe_front(0, 0)
                moe_logits(0)
                moe_gate(0)
                moe_combT(0, 0)
                step(0, 0)
                with act.Fori(1, NG - 2, 2) as g:
                    step(g, 1)
                    step(g + 1, 0)
                step(NG - 1, 1, front=False)

            def ffn_turned_x(n):
                act.wait_ge(f_xqT_ps, n + 1)
                act.copy(fxqT[:, :], Mb[0][:, 0:128]).then_inc(f_xqT_sb, 1)

            def ffn_gelu(n, p):
                act.wait_ge(f_hpre, n + 1)
                after(act, f_hr, n - 1)
                act.activation(hact[p][:, :], hpre[p][:, :], ACT.Gelu).then_inc(f_gelu, 1)

            def ffn_round(n, p):
                act.wait_ge(f_inverse, n + 3)
                after(act, f_hq, n)
                act.activation(hround[:, :], hact[p][:, :], ACT.Identity, bias=magic[:, 0:1],
                               scale=inverse[:, p, 1:2]).then_inc(f_hr, 1)

            def ffn_turned_h(n):
                act.wait_ge(f_hqT_ps, n + 1)
                act.copy(hqT[:, :, :], Mb[2][:, 0:F].rearrange("p (c q) -> p c q", c=FC)).then_inc(f_hqT_sb, 1)

            def ffn():
                def step(n, p, there):
                    if there(-1):
                        ffn_turned_h(n - 1)
                    if there(1):
                        ffn_gelu(n + 1, 1 - p)
                    if there(0):
                        ffn_round(n, p)
                    if there(2):
                        ffn_turned_x(n + 2)

                ffn_pipeline(act, step)

            act.wait_ge(consts_pool, CONSTS)
            attention(0)
            act.wait_ge(loaded, LOADS)
            moe()
            attention(1)

            ffn()

        @block.vector
        def _(dve):
            def normalised(dst, n):
                return dve.tensor_scalar(dst, one(X, n), mean[:, bass.ds(n, 1)], rstd[:, bass.ds(n, 1)],
                                         ALU.subtract, ALU.mult)

            def normalise(a, L, k, p):
                dve.wait_ge(ln_ready[2 * L], k - p % 2 + 2)
                after(dve, a.xnT_ps, k - 1)
                normalised(xn[p % 2][:, :], k).then_inc(a.xn_ready, 1)

            def rotate(a, L, k):
                dve.wait_ge(a.proj_ps, k + 1)
                after(dve, a.qk_ready, k)
                P4 = M[0][:, 128:384].rearrange("p (a h d) -> p a h d", a=2, d=DH)
                r1 = rot1[:, :, :].rearrange("p (a h) d -> p a h d", a=2)
                r2 = rot2[:, :, :].rearrange("p (a h) d -> p a h d", a=2)
                c, s, hd = rope_c[L], rope_s[L], DH // 2
                dve.tensor_tensor(r1, P4, c[:, :, :].unsqueeze(2).broadcast_to([128, 2, H, DH]), ALU.mult)
                dve.tensor_tensor(r2[:, :, :, 0:hd], P4[:, :, :, hd:DH],
                                  s[:, :, 0:hd].unsqueeze(2).broadcast_to([128, 2, H, hd]), ALU.mult)
                dve.tensor_tensor(r2[:, :, :, hd:DH], P4[:, :, :, 0:hd],
                                  s[:, :, hd:DH].unsqueeze(2).broadcast_to([128, 2, H, hd]),
                                  ALU.mult).then_inc(a.proj_read, 1)

            def rotated(a, k):
                dve.wait_ge(a.proj_read, k + 1)
                after(dve, a.h_ready, 2 * k)
                after(dve, a.rest_ready, k)
                dve.tensor_tensor(qk[:, :, :], rot1[:, :, :], rot2[:, :, :], ALU.add).then_inc(a.qk_ready, 1)

            views = [x[:, :, 0:ROWS].rearrange("p h (s d) -> p h s d", d=DH) for x in stack]

            def rest(a, k, p):
                dve.wait_ge(a.h_ready, 2 * k + 2)
                after(dve, a.l_ready, k)
                dve.tensor_tensor(qk_rest[:, :, :], qk[:, :, :], views[p % 2][:, :, 2, :],
                                  ALU.subtract).then_inc(a.rest_ready, 1)

            def middle_parts(a, k, p):
                view = views[p % 2]
                dve.wait_ge(a.rest_ready, k + 1)
                for at, slots in ((slice(0, H), slice(0, 6, 5)), (slice(H, 2 * H), slice(1, 6, 4))):
                    last = dve.tensor_copy(view[:, at, slots, :],
                                           qk_rest[:, at, :].unsqueeze(2).broadcast_to([128, H, 2, DH]))
                last.then_inc(a.m_ready, 1)

            def low_parts(a, k, p):
                view = views[p % 2]
                dve.wait_ge(a.m_ready, k + 1)
                dve.tensor_tensor(view[:, 0:H, Q_L, :], qk_rest[:, 0:H, :], view[:, 0:H, 5, :], ALU.subtract)
                dve.tensor_tensor(view[:, H:, K_L, :], qk_rest[:, H:, :], view[:, H:, 5, :],
                                  ALU.subtract).then_inc(a.l_ready, 1)

            def maxima(a, k, u):
                dve.wait_ge((a.s0_ps, a.s1_ps)[u], k + 1)
                after(dve, a.ms_ready, k)
                dve.tensor_reduce(nmax[:, 8 * u:8 * u + 8].rearrange("p (i b) -> p b i", b=2),
                                  pairs[u][:, :, :, :], AX.X, ALU.max, negate=True).then_inc((a.max0, a.max1)[u], 1)

            halves = msplit[:, :].rearrange("p (r c) -> p r c", r=2)
            nmax_twice = nmax[:, :].unsqueeze(1).broadcast_to([128, 2, H])

            def max_high(a, k):
                after(dve, a.mT_ps, k)
                dve.wait_ge(a.max1, k + 1)
                dve.tensor_copy(halves[:, :, 0:H], nmax_twice).then_inc(a.mh_ready, 1)

            def max_low(a, k):
                dve.wait_ge(a.mh_ready, k + 1)
                dve.tensor_tensor(halves[:, :, H:2 * H], nmax_twice, halves[:, :, 0:H],
                                  ALU.subtract).then_inc(a.ms_ready, 1)

            def mT_out(a, k):
                dve.wait_ge(a.mT_ps, k + 1)
                after(dve, a.st1_ps, k)
                dve.tensor_copy(mT[:, :], Mb[2][:, 0:128]).then_inc(a.mT_sb, 1)

            O = M[3][:, :].rearrange("p (h d) -> p h d", h=H)

            def denominators(a, k):
                dve.wait_ge(a.o_ps, k + 1)
                dve.reciprocal(rden[:, :], O[:, :, DH]).then_inc(a.rden_ready, 1)

            def divide(a, k):
                dve.wait_ge(a.rden_ready, k + 1)
                after(dve, a.onT_ps, k)
                dve.tensor_tensor(on[:, :].rearrange("p (h d) -> p h d", h=H), O[:, :, 0:DH],
                                  rden[:, :].unsqueeze(2).broadcast_to([128, H, DH]), ALU.mult).then_inc(a.on_ready, 1)

            def residual(a, k):
                dve.wait_ge(a.y_ps, k + 1)
                dve.tensor_tensor(one(X, k), M[3][:, 128:256], one(X, k), ALU.add).then_inc(a.x_done, 1)

            def first_stats(k):
                dve.bn_stats(one(stats, k), one(X, k)).then_inc(stats_ready[0], 1)

            def next_stats(a, ln, k):
                dve.wait_ge(a.x_done, k + 1)
                dve.bn_stats(one(stats, k), one(X, k)).then_inc(stats_ready[ln], 1)

            def attention(L):
                a = layers[L]

                def step(n, p, there):
                    if there(2):
                        rest(a, n + 2, p + 2)
                    if there(3):
                        rotate(a, L, n + 3)
                    if there(2):
                        middle_parts(a, n + 2, p + 2)
                    if there(-1):
                        denominators(a, n - 1)
                    if there(2):
                        low_parts(a, n + 2, p + 2)
                    if there(3):
                        rotated(a, n + 3)
                    if there(-1):
                        divide(a, n - 1)
                    if there(1):
                        maxima(a, n + 1, 0)
                        maxima(a, n + 1, 1)
                        max_high(a, n + 1)
                    if there(5):
                        normalise(a, L, n + 5, p + 5)
                    if there(1):
                        max_low(a, n + 1)
                    if there(-1):
                        residual(a, n - 1)
                    if there(1):
                        mT_out(a, n + 1)
                    if there(-1):
                        next_stats(a, 2 * L + 1, n - 1)
                    if L == 0 and there(9):
                        if isinstance(n, int) and n + 9 == AHEAD:
                            dve.wait_ge(loaded_x, LOADS_X)
                        first_stats(n + 9)

                pipeline(dve, L, step)

            def moe_front(g, p):
                dve.wait_ge(ln_ready[1], g * G + G)
                after(dve, m_xgT_ps, g)
                for b in range(G):
                    normalised(xg[:, b, :], g * G + b).then_inc(m_xg, 1)

            def moe_gate(g, p):
                base = g * GATE_STEPS
                k = [0]

                def step(ins):
                    k[0] += 1
                    ins.then_inc(m_gate, 1)

                dve.wait_ge(m_logit_ps, g + 1)
                dve.tensor_copy(logit[:, :, :], M[1][:, 0:G * E].rearrange("p (b e) -> p b e", b=G)
                                ).then_inc(m_logit_sb, 1)
                dve.wait_ge(m_logit_sb, g + 1)
                after(dve, m_carry, 2 * g)
                dve.memset(carry[:, 0:1], 0.0).then_inc(m_carry, 1)
                for b in range(G):
                    dve.max(top[:, b, :], logit[:, b, :]).then_inc(m_top, 1)
                dve.wait_ge(m_top, (g + 1) * G)
                after(dve, m_carry, 2 * g)
                dve.memset(carry[:, 1:2], 0.0).then_inc(m_carry, 1)
                for b in range(G):
                    dve.max_index(topi[:, b, :], top[:, b, :], logit[:, b, :]).then_inc(m_topi, 1)
                after(dve, m_egap, g)
                step(dve.tensor_tensor(gap[:, :], top[:, :, 1], top[:, :, 0], ALU.subtract))
                dve.wait_ge(m_topi, (g + 1) * G)
                step(dve.tensor_copy(topf[:, :, :], topi[:, :, :]))
                dve.wait_ge(m_egap, g + 1)
                step(dve.tensor_scalar(egap1[:, :], egap[:, :], 1.0, None, ALU.add))
                dve.wait_ge(m_gate, base + 3)
                step(dve.reciprocal(w_first[:, :], egap1[:, :]))
                wide = iota[:, :].unsqueeze(1).broadcast_to([128, G, E])
                step(dve.tensor_tensor(pick1[:, :, :], wide, topf[:, :, 0:1].broadcast_to([128, G, E]), ALU.is_equal))
                step(dve.tensor_tensor(pick2[:, :, :], wide, topf[:, :, 1:2].broadcast_to([128, G, E]), ALU.is_equal))
                dve.wait_ge(m_gate, base + 6)
                step(dve.tensor_tensor(w_second[:, :], egap[:, :], w_first[:, :], ALU.mult))
                step(dve.tensor_tensor(pick1[:, :, :], pick1[:, :, :],
                                       w_first[:, :].unsqueeze(2).broadcast_to([128, G, E]), ALU.mult))
                dve.wait_ge(m_gate, base + 8)
                step(dve.tensor_tensor(pick2[:, :, :], pick2[:, :, :],
                                       w_second[:, :].unsqueeze(2).broadcast_to([128, G, E]), ALU.mult))
                assert k[0] == GATE_STEPS
                dve.wait_ge(m_gate, base + 9)
                dve.tensor_tensor(comb[p][:, :, :], pick1[:, :, :], pick2[:, :, :], ALU.add).then_inc(m_comb, 1)

            def moe_add(g, p, j):
                base = g * ((E + 1) * G)
                dve.wait_ge(m_y_ps, g * (E + 1) + (j + 1))
                for b in range(G):
                    after(dve, m_y_added, base + ((j - 1) * G + b + 1) if j > 0 else 0)
                    if j > 0:
                        dve.wait_ge(m_comb, g + 1)
                    Y = M[2 + (j + p) % 2][:, b * 128:(b + 1) * 128]
                    x = one(X, g * G + b)
                    if j == 0:
                        dve.tensor_tensor(x, Y, x, ALU.add).then_inc(m_y_added, 1)
                    else:
                        dve.scalar_tensor_tensor(x, Y, comb[p][:, b, j - 1:j], x, ALU.mult,
                                                 ALU.add).then_inc(m_y_added, 1)

            def moe_stats(g):
                dve.wait_ge(m_y_added, (g + 1) * ((E + 1) * G))
                for b in range(G):
                    dve.bn_stats(one(stats, g * G + b), one(X, g * G + b)).then_inc(stats_ready[2], 1)

            def moe():
                def step(g, p, front=True):
                    moe_add(g, p, 0)
                    for e in range(1, E):
                        moe_add(g, p, e)
                        if front and e == 1:
                            moe_front(g + 1, 1 - p)
                        if front and e == 4:
                            moe_gate(g + 1, 1 - p)
                    moe_add(g, p, E)
                    moe_stats(g)

                moe_front(0, 0)
                moe_gate(0, 0)
                step(0, 0)
                ternary_weights()
                split_biases()
                with dve.Fori(1, NG - 2, 2) as g:
                    step(g, 1)
                    step(g + 1, 0)
                step(NG - 1, 1, front=False)

            def ffn_normalise(n, p):
                dve.wait_ge(ln_ready[3], n - p + 2)
                after(dve, f_xr, n)
                normalised(fxn[:, :], n).then_inc(f_xn, 1)

            def ffn_x_max(n, p):
                dve.wait_ge(f_xn, n + 1)
                dve.tensor_reduce(absmax[:, p, 0:1], fxn[:, :], AX.X, ALU.max,
                                  apply_absolute_value=True).then_inc(f_x_max, 1)

            def ffn_h_max(n, p):
                dve.wait_ge(f_gelu, n + 1)
                dve.tensor_reduce(absmax[:, p, 1:2], hact[p][:, :], AX.X, ALU.max,
                                  apply_absolute_value=True).then_inc(f_h_max, 1)

            def ffn_scales(n, p, there, between):
                if there(2):
                    dve.wait_ge(f_x_max, n + 3)
                if there(0):
                    dve.wait_ge(f_h_max, n + 1)
                dve.tensor_scalar(unit[:, p, :], absmax[:, p, :], EPS, 1.0 / QB, ALU.max, ALU.mult).then_inc(f_unit, 1)
                between()
                dve.wait_ge(f_unit, n + 3)
                dve.reciprocal(inverse[:, p, :], unit[:, p, :]).then_inc(f_inverse, 1)
                dve.tensor_tensor(outscale[:, p, :], unit[:, p, :], wscale[:, :], ALU.mult).then_inc(f_outscale, 1)

            def ffn_round_x(n, p):
                dve.wait_ge(f_inverse, n + 1)
                dve.tensor_scalar(fxr[:, :], fxn[:, :], inverse[:, p, 0:1], MAGIC, ALU.mult, ALU.add).then_inc(f_xr, 1)
                dve.wait_ge(f_xr, n + 1)
                after(dve, f_xqT_ps, n)
                dve.tensor_scalar(fxq[:, :], fxr[:, :], MAGIC, QB, ALU.subtract, ALU.min).then_inc(f_xq, 1)

            def ffn_hidden(n, p):
                dve.wait_ge(f_h_ps, n + 1)
                dve.wait_ge(f_outscale, n + 1)
                after(dve, f_gelu, n - 1)
                dve.scalar_tensor_tensor(hpre[p][:, :], M[1][:, :], outscale[:, p, 0:1], fb1[:, :], ALU.mult,
                                         ALU.add).then_inc(f_hpre, 1)

            def ffn_round_h(n):
                dve.wait_ge(f_hr, n + 1)
                after(dve, f_hqT_ps, n)
                dve.tensor_scalar(hq[:, :], hround[:, :], MAGIC, QB, ALU.subtract, ALU.min).then_inc(f_hq, 1)

            def ffn_out(n, p):
                dve.wait_ge(f_y_ps, n + 1)
                dve.wait_ge(f_xb, n + 1)
                dve.wait_ge(f_outscale, n + 3)
                after(dve, out_done[p], (n - p) * 8)
                dve.scalar_tensor_tensor(yout[p][:, :], M[3][:, 0:128], outscale[:, p, 1:2], xb[:, :], ALU.mult,
                                         ALU.add).then_inc(f_out, 1)

            def ffn():
                def step(n, p, there):
                    q = 1 - p

                    def hidden():
                        if there(1):
                            ffn_hidden(n + 1, q)

                    if there(-1):
                        ffn_round_h(n - 1)
                    if there(2):
                        ffn_normalise(n + 2, p)
                    if there(0):
                        ffn_h_max(n, p)
                    if there(2):
                        ffn_x_max(n + 2, p)
                    if there(0) or there(2):
                        ffn_scales(n, p, there, hidden)
                    if there(-1):
                        ffn_out(n - 1, q)
                    if there(2):
                        ffn_round_x(n + 2, p)

                ffn_pipeline(dve, step)

            def split_biases():
                dve.tensor_copy(bias_parts[:, 0, :], biases[:, :]).then_inc(bias_step, 1)
                dve.wait_ge(bias_step, 1)
                dve.tensor_tensor(bias_rest[:, 0, :], biases[:, :], bias_parts[:, 0, :], ALU.subtract
                                  ).then_inc(bias_step, 1)
                dve.wait_ge(bias_step, 2)
                dve.tensor_copy(bias_parts[:, 1, :], bias_rest[:, 0, :]).then_inc(bias_step, 1)
                dve.wait_ge(bias_step, 3)
                dve.tensor_tensor(bias_rest[:, 1, :], bias_rest[:, 0, :], bias_parts[:, 1, :], ALU.subtract
                                  ).then_inc(bias_step, 1)
                dve.wait_ge(bias_step, 4)
                dve.tensor_copy(bias_parts[:, 2, :], bias_rest[:, 1, :]).then_inc(bias_step, 1)

            def ternary_weights():
                for i, w in enumerate((fw1[:, :], fw2[:, :, :].rearrange("p c d -> p (c d)"))):
                    dve.tensor_reduce(wsum[:, i:i + 1], w, AX.X, ALU.add, apply_absolute_value=True).then_inc(wabs_ready, 1)
                dve.wait_ge(wsum_ps, 1)
                dve.tensor_scalar(wscale[:, :], M[1][:, 0:2], 1.0 / (D * F), EPS, ALU.mult, ALU.max).then_inc(wstep, 1)
                dve.wait_ge(wstep, 1)
                dve.reciprocal(wrecip[:, :], wscale[:, :]).then_inc(wstep, 1)
                dve.wait_ge(wstep, 2)
                for i, (w, wqt) in enumerate(((fw1[:, :], fw1q[:, :]),
                                              (fw2[:, :, :].rearrange("p c d -> p (c d)"),
                                               fw2q[:, :, :].rearrange("p c d -> p (c d)")))):
                    dve.tensor_scalar(w, w, wrecip[:, i:i + 1], MAGIC, ALU.mult, ALU.add).then_inc(wstep, 1)
                    dve.wait_ge(wstep, 3 + 2 * i)
                    dve.tensor_scalar(wtmp[:, :], w, MAGIC, 1.0, ALU.subtract, ALU.min).then_inc(wstep, 1)
                    dve.wait_ge(wstep, 4 + 2 * i)
                    last = dve.tensor_scalar(wqt, wtmp[:, :], -1.0, None, ALU.max)
                    last.then_inc(w_ternary, 1)
                    dve.wait_ge(w_ternary, 1 + i)

            dve.wait_ge(loaded_first, LOADS_FIRST)
            for k in range(4):
                first_stats(k)
            dve.wait_ge(consts_pool, CONSTS)
            attention(0)
            dve.wait_ge(loaded, LOADS)
            moe()
            attention(1)
            ffn()


def constants():
    import numpy as np

    def bf16(x):
        return (np.ascontiguousarray(x).view(np.uint32) >> 16).astype(np.uint16)

    pos = np.arange(S, dtype=np.float32)
    freqs = [10000.0 ** (-np.arange(0, DH, 2, dtype=np.float32) / DH),
             1.0 / 10000.0 ** (np.arange(DH // 2, dtype=np.float32) / (DH // 2))]
    out = {"c_ident": np.eye(128, dtype=np.float32)}
    for i, f in enumerate(freqs):
        ang = pos[:, None] * f.astype(np.float32)[None, :]
        c, s = np.cos(ang), np.sin(ang)
        cc, ss = np.concatenate([c, c], 1), np.concatenate([-s, s], 1)
        q_scale = np.float32(DH ** -0.5)
        out[f"c_rope_c{i}"] = np.stack([cc * q_scale, cc], 1).astype(np.float32)
        out[f"c_rope_s{i}"] = np.stack([ss * q_scale, ss], 1).astype(np.float32)
    pick = np.zeros((2, 64, H, 128), np.float32)
    for h in range(H):
        pick[:, h, h] = 1.0
        pick[:, H + h, h] = 1.0
    out["c_pick"] = bf16(pick.reshape(128, H, 128))
    out["c_identb"] = bf16(out["c_ident"])
    q, k = np.arange(S)[:, None], np.arange(S)[None, :]
    inside = (k <= q) & (k >= q - WINDOW)
    m = np.where(inside, 0.0, -1e30).astype(np.float32)
    out["c_mask_qk"], out["c_mask_kq"] = bf16(m), bf16(m.T)
    out["c_iota"] = np.tile(np.arange(E, dtype=np.float32), (128, 1))
    return out


def kernel(**inputs):
    import numpy as np
    import concourse.bacc as bacc
    from concourse import mybir as mb
    from concourse.bass_utils import run_bass_kernel_spmd as run

    a = {k: np.asarray(v) for k, v in inputs.items()}
    perm = np.arange(D).reshape(H, DH)[:, [0, 2, 4, 6, 1, 3, 5, 7]].reshape(-1)
    arrays = {
        "x": a["x"].transpose(1, 0, 2),
        "ctxT": a["ctx_1024"].transpose(2, 0, 1),
        "wq0": a["L0_xattn_Wq"][:, perm],
        "wkv0": np.concatenate([a["L0_xattn_Wk"][:, perm], a["L0_xattn_Wv"]], 1),
        "wo0": a["L0_xattn_Wo"],
        "wq1": a["L1_xattn_q_w"].T,
        "wkv1": np.concatenate([a["L1_xattn_k_w"].T, a["L1_xattn_v_w"].T], 1),
        "wo1": a["L1_xattn_o_w"].T,
        "biases": np.concatenate([a[f"L1_xattn_{x}_b"] for x in "qkvo"])[None],
        "wg": a["L0_ffn_Wg"],
        "bg": a["L0_ffn_bg"][:, None],
        "w1": a["L0_ffn_W1"].transpose(1, 0, 2),
        "b1": a["L0_ffn_b1"].reshape(E, NCH, 128).transpose(2, 0, 1),
        "w2": a["L0_ffn_W2"].reshape(E, NCH, 128, D).transpose(2, 0, 1, 3),
        "b2": a["L0_ffn_b2"],
        "fw1": a["L1_ffn_W1"].T,
        "fw2": a["L1_ffn_W2"].T.reshape(FC, 128, D).transpose(1, 0, 2),
        "fb1": a["L1_ffn_b1"][None],
        "fb2": a["L1_ffn_b2"][None],
    }
    arrays.update(constants())
    arrays = {k: np.ascontiguousarray(v) for k, v in arrays.items()}
    nc = bacc.Bacc("TRN2", target_bir_lowering=False, num_devices=1)
    t = {k: nc.dram_tensor(f"in_{k}", v.shape, mb.dt.from_np(v.dtype), kind="ExternalInput").ap()
         for k, v in arrays.items()}
    out = nc.dram_tensor("out_x", (S, B, D), mb.dt.float32, kind="ExternalOutput").ap()
    build(nc, t, out)
    r = run(nc, [{f"in_{k}": v for k, v in arrays.items()}], core_ids=[0])
    return np.ascontiguousarray(r.results[0]["out_x"].transpose(1, 0, 2))
```

```python
from contextlib import ExitStack

import concourse.bass as bass
from concourse import mybir

F32 = mybir.dt.float32
BF16 = mybir.dt.bfloat16
U32 = mybir.dt.uint32
U16 = mybir.dt.uint16
ACT = mybir.ActivationFunctionType
ALU = mybir.AluOpType
AX = mybir.AxisListType

B, S, D = 32, 128, 128
H = 16
DH = D // H
E = 8
HID = 256
NCH = HID // 128
G = 4
NG = B // G
F = 512
FC = F // 128
WINDOW = 64
EPS = 1e-5
QB = 127.0
MAGIC = 1.5 * 2.0 ** 23
SLOT = 64
ROWS = 6 * DH
SPARE = SLOT - ROWS
SLOT_KEYS = S - SPARE
Q_L, K_L = 4, 3


class AttentionEvents:

    def __init__(self, sem, L):
        self.xn_ready = sem(f"L{L}_xn_ready")
        self.ctx_ready = sem(f"L{L}_ctx_ready")
        self.xnT_ps = sem(f"L{L}_xnT_ps")
        self.xnT_sb = sem(f"L{L}_xnT_sb")
        self.proj_ps = sem(f"L{L}_proj_ps")
        self.proj_read = sem(f"L{L}_proj_read")
        self.v_copied = sem(f"L{L}_v_copied")
        self.qk_ready = sem(f"L{L}_qk_ready")
        self.h_ready = sem(f"L{L}_h_ready")
        self.rest_ready = sem(f"L{L}_rest_ready")
        self.m_ready = sem(f"L{L}_m_ready")
        self.l_ready = sem(f"L{L}_l_ready")
        self.qT_ps = sem(f"L{L}_qT_ps")
        self.kT_ps = sem(f"L{L}_kT_ps")
        self.qT_sb = sem(f"L{L}_qT_sb")
        self.kT_sb = sem(f"L{L}_kT_sb")
        self.s0_ps = sem(f"L{L}_s0_ps")
        self.s1_ps = sem(f"L{L}_s1_ps")
        self.max0 = sem(f"L{L}_max0")
        self.max1 = sem(f"L{L}_max1")
        self.mh_ready = sem(f"L{L}_mh_ready")
        self.ms_ready = sem(f"L{L}_ms_ready")
        self.mT_ps = sem(f"L{L}_mT_ps")
        self.mT_sb = sem(f"L{L}_mT_sb")
        self.st0_ps = sem(f"L{L}_st0_ps")
        self.st1_ps = sem(f"L{L}_st1_ps")
        self.exp0 = sem(f"L{L}_exp0")
        self.exp1 = sem(f"L{L}_exp1")
        self.pv1 = sem(f"L{L}_pv1")
        self.oT_sb = sem(f"L{L}_oT_sb")
        self.o_ps = sem(f"L{L}_o_ps")
        self.rden_ready = sem(f"L{L}_rden_ready")
        self.on_ready = sem(f"L{L}_on_ready")
        self.onT_ps = sem(f"L{L}_onT_ps")
        self.onT_sb = sem(f"L{L}_onT_sb")
        self.y_ps = sem(f"L{L}_y_ps")
        self.x_done = sem(f"L{L}_x_done")


def build(nc, t, out):
    ctx = ExitStack()
    with ctx:
        def sb(name, shape, dt=F32):
            return ctx.enter_context(nc.sbuf_tensor(name, shape, dt))

        def ps(name, shape, dt=F32):
            return ctx.enter_context(nc.psum_tensor(name, shape, dt))

        def sem(name):
            return ctx.enter_context(nc.semaphore(name))

        X = sb("X", [128, B, D])
        ctxT = sb("ctxT", [128, B, S])
        ident = sb("ident", [128, 128])
        identb = sb("identb", [128, 128], BF16)
        rope_c = [sb(f"rope_c{i}", [128, 2, DH]) for i in range(2)]
        rope_s = [sb(f"rope_s{i}", [128, 2, DH]) for i in range(2)]
        pick = [sb(f"pick_max{i}", [128, H, 128], BF16) for i in range(2)]
        mask = sb("mask", [128, 128], BF16)
        spare_rows = sb("spare_rows", [128, 2, SPARE], BF16)
        iota = sb("iota", [128, E])
        wq = [sb(f"wq{i}", [128, D]) for i in range(2)]
        wkv = [sb(f"wkv{i}", [128, 2 * D]) for i in range(2)]
        wo = [sb(f"wo{i}", [128, D]) for i in range(2)]
        biases = sb("biases", [1, 4 * D])
        bias_rest = sb("bias_rest", [1, 2, 4 * D])
        bias_parts = sb("bias_parts", [1, 3, 4 * D], BF16)
        bias3 = sb("bias3", [3, 4 * D], BF16)
        ones3 = sb("ones3", [3, 128], BF16)
        wg = sb("wg", [128, E])
        bg = sb("bg", [E, 1])
        w1 = sb("w1", [128, E, HID])
        b1 = sb("b1", [128, E, NCH])
        w2 = sb("w2", [128, E, NCH, D])
        b2 = sb("b2", [E, D])
        fw1 = sb("fw1", [128, F])
        fw2 = sb("fw2", [128, FC, D])
        fw1q = sb("fw1q", [128, F], BF16)
        fw2q = sb("fw2q", [128, FC, D], BF16)
        fb1 = sb("fb1", [128, F])
        fb2 = sb("fb2", [128, D])
        onesq = sb("onesq", [128, 128])
        half = sb("half", [128, 2])
        first_exp = sb("first_exp", [128, 2])
        magic = sb("magic", [128, 1])
        minus_half = sb("minus_half", [128, 2])
        wsum = sb("wsum", [128, 2])
        wscale = sb("wscale", [128, 2])
        wrecip = sb("wrecip", [128, 2])
        wtmp = sb("wtmp", [128, F])

        stats = sb("stats", [128, B, 6])
        mean = sb("mean", [128, B])
        ln_tmp = [[sb(f"ln_{x}{i}", [128, 2]) for x in ("m", "d", "q", "d2", "q2", "d3", "v")] for i in range(2)]
        rstd = sb("rstd", [128, B])

        xn = [sb(f"xn{i}", [128, D]) for i in range(2)]
        xnT = [sb(f"xnT{i}", [128, 128]) for i in range(2)]
        ctx_now = [sb(f"ctx_now{i}", [128, 128]) for i in range(2)]
        rot1 = sb("rot1", [128, 2 * H, DH])
        rot2 = sb("rot2", [128, 2 * H, DH])
        qk = sb("qk", [128, 2 * H, DH])
        qk_rest = sb("qk_rest", [128, 2 * H, DH])
        stack = [sb(f"stack{i}", [128, 2 * H, SLOT], BF16) for i in range(2)]
        QT = [sb(f"QT{i}", [128, H // 2, 128], BF16) for i in range(4)]
        KT = [sb(f"KT{i}", [128, H // 2, 128], BF16) for i in range(4)]
        V = [sb(f"V{i}", [128, H, 32]) for i in range(4)]
        nmax = sb("nmax", [128, H])
        msplit = sb("msplit", [128, 128], BF16)
        mT = [[sb(f"mT{i}{u}", [128, 128], BF16) for u in range(2)] for i in range(2)]
        PT = [sb(f"PT{i}", [128, H // 2, 128]) for i in range(2)]
        rden = sb("rden", [128, H])
        on = sb("on", [128, D])
        oT = sb("oT", [128, 4, 128])
        onT = sb("onT", [128, 128])

        xg = sb("xg", [128, G, D])
        xgT = [sb(f"xgT{i}", [128, G, 128]) for i in range(2)]
        lT = sb("lT", [E, G, 128])
        logit = sb("logit", [128, G, E])
        top = sb("top", [128, G, 8])
        topi = sb("topi", [128, G, 8], U32)
        topf = sb("topf", [128, G, 8])
        carry = sb("carry", [128, 2])
        gap = sb("gap", [128, G])
        egap = sb("egap", [128, G])
        egap1 = sb("egap1", [128, G])
        w_first = sb("w_first", [128, G])
        w_second = sb("w_second", [128, G])
        pick1 = sb("pick1", [128, G, E])
        pick2 = sb("pick2", [128, G, E])
        comb = [sb(f"comb{i}", [128, G, E]) for i in range(2)]
        combT = [sb(f"combT{i}", [E, G, 128]) for i in range(2)]
        hid = [[sb(f"hid{i}{c}", [128, G, 128]) for c in range(NCH)] for i in range(2)]

        fxn = [sb(f"fxn{i}", [128, D]) for i in range(2)]
        fxq = sb("fxq", [128, D], BF16)
        fxr = sb("fxr", [128, D])
        fxqT = sb("fxqT", [128, 128], BF16)
        absmax = sb("absmax", [128, 2, 2])
        unit = sb("unit", [128, 2, 2])
        inverse = sb("inverse", [128, 2, 2])
        outscale = sb("outscale", [128, 2, 2])
        hpre = [sb(f"hpre{i}", [128, F]) for i in range(2)]
        hact = [sb(f"hact{i}", [128, F]) for i in range(2)]
        hround = sb("hround", [128, F])
        hq = sb("hq", [128, F], BF16)
        hqT = sb("hqT", [128, FC, 128], BF16)
        xb = sb("xb", [128, D])
        yout = [sb(f"yout{i}", [128, D]) for i in range(2)]

        pairs = [ps(f"pair{i}", [128, 2, 4, 128]) for i in range(2)]
        M = [ps(f"M{i}", [128, 512]) for i in range(4)]
        Mb = [m[:, :].bitcast(BF16) for m in M]

        loaded_first = sem("loaded_first")
        loaded_mT = sem("loaded_mT")
        loaded_x = sem("loaded_x")
        loaded = sem("loaded")
        consts_pool = sem("consts_pool")
        spare_ready = sem("spare_ready")
        bias_step = sem("bias_step")
        bias3_ready = sem("bias3_ready")
        wabs_ready = sem("wabs_ready")
        wsum_ps = sem("wsum_ps")
        wstep = sem("wstep")
        w_ternary = sem("w_ternary")
        out_done = [sem(f"out_done{i}") for i in range(2)]
        LOADS_FIRST, LOADS_X, LOADS = 16 * 8, 16 * 4, 16 * 20
        AHEAD = 8

        stats_ready = [sem(f"stats_ready{i}") for i in range(4)]
        ln_step = [sem(f"ln_step{i}") for i in range(4)]
        ln_ready = [sem(f"ln_ready{i}") for i in range(4)]
        LN_STEPS = 7
        CONSTS = 13

        layers = [AttentionEvents(sem, L) for L in range(2)]

        m_xg = sem("m_xg")
        m_xgT_ps = sem("m_xgT_ps")
        m_xgT_sb = sem("m_xgT_sb")
        m_lT_ps = sem("m_lT_ps")
        m_lT_sb = sem("m_lT_sb")
        m_logit_ps = sem("m_logit_ps")
        m_logit_sb = sem("m_logit_sb")
        m_top = sem("m_top")
        m_carry = sem("m_carry")
        m_topi = sem("m_topi")
        m_gate = sem("m_gate")
        m_egap = sem("m_egap")
        m_comb = sem("m_comb")
        m_combT_ps = sem("m_combT_ps")
        m_combT_sb = sem("m_combT_sb")
        m_h_ps = sem("m_h_ps")
        m_h_sb = sem("m_h_sb")
        m_y_ps = sem("m_y_ps")
        m_y_added = sem("m_y_added")
        GATE_STEPS = 9

        f_xn = sem("f_xn")
        f_x_max = sem("f_x_max")
        f_h_max = sem("f_h_max")
        f_unit = sem("f_unit")
        f_inverse = sem("f_inverse")
        f_outscale = sem("f_outscale")
        f_xr = sem("f_xr")
        f_xq = sem("f_xq")
        f_xqT_ps = sem("f_xqT_ps")
        f_xqT_sb = sem("f_xqT_sb")
        f_h_ps = sem("f_h_ps")
        f_hpre = sem("f_hpre")
        f_gelu = sem("f_gelu")
        f_hr = sem("f_hr")
        f_hq = sem("f_hq")
        f_hqT_ps = sem("f_hqT_ps")
        f_hqT_sb = sem("f_hqT_sb")
        f_y_ps = sem("f_y_ps")
        f_xb = sem("f_xb")
        f_out = sem("f_out")

        def after(eng, s, v):
            if not isinstance(v, int) or v > 0:
                eng.wait_ge(s, v)

        def one(tensor, n):
            return tensor[:, bass.ds(n, 1)].rearrange("p a b -> p (a b)")

        ATTENTION_FIRST, FFN_FIRST = -5, -3
        AHEAD_DVE, AHEAD_OTHERS = (1, 3, 5), (1, 3, 6)

        def peeled(step, n):
            step(n, n % 4, lambda k: 0 <= n + k < B)

        def pipeline(eng, step, first, beside):
            LAST, LOOP0, TURNS = B, 3, 5
            for n in range(first, LOOP0):
                peeled(step, n)
            with eng.Fori(LOOP0, LOOP0 + 4 * (TURNS - 1) + 1, 4) as n:
                for i in range(4):
                    step(n + i, (LOOP0 + i) % 4, lambda k: True)
            for n in range(LOOP0 + 4 * TURNS, LAST + 1):
                peeled(step, n)
                beside(n)

        def ffn_pipeline(eng, step):
            LAST, LOOP0, TURNS = B + 1, 3, 6
            for n in range(0, LOOP0):
                peeled(step, n)
            with eng.Fori(LOOP0, LOOP0 + 4 * (TURNS - 1) + 1, 4) as n:
                for i in range(4):
                    step(n + i, (LOOP0 + i) % 4, lambda k: True)
            for n in range(LOOP0 + 4 * TURNS, LAST + 1):
                peeled(step, n)

        def attention_ahead(eng, step, e):
            at = AHEAD_DVE if eng is nc.vector else AHEAD_OTHERS
            if e in at:
                peeled(step, ATTENTION_FIRST + at.index(e))

        block = ctx.enter_context(nc.Block())

        @block.sync
        def _(sp):
            def load(counter, *pairs):
                for dst, src in pairs:
                    sp.dma_start(dst, src).then_inc(counter, 16)

            load(loaded_first, (X[:, 0:AHEAD, :], t["x"][:, 0:AHEAD, :]), (ident[:, :], t["c_ident"]),
                 (ctxT[:, 0:AHEAD, :], t["ctxT"][:, 0:AHEAD, :]), (wq[0][:, :], t["wq0"]), (wkv[0][:, :], t["wkv0"]),
                 (rope_c[0][:, :, :], t["c_rope_c0"]), (rope_s[0][:, :, :], t["c_rope_s0"]),
                 (identb[:, :].bitcast(U16), t["c_identb"]))
            load(loaded_mT, *((mT[i][u][:, :].bitcast(U16), t["c_mask_rows"][u]) for i in range(2) for u in range(2)))
            load(loaded_x, (pick[0][:, :, :].bitcast(U16), t["c_pick0"]), (X[:, AHEAD:, :], t["x"][:, AHEAD:, :]),
                 (ctxT[:, AHEAD:, :], t["ctxT"][:, AHEAD:, :]), (wo[0][:, :], t["wo0"]))
            load(loaded, (mask[:, :].bitcast(U16), t["c_mask_qk"]), (spare_rows[:, :, :].bitcast(U16), t["c_spare_rows"]),
                 (pick[1][:, :, :].bitcast(U16), t["c_pick1"]),
                 (rope_c[1][:, :, :], t["c_rope_c1"]), (rope_s[1][:, :, :], t["c_rope_s1"]),
                 (iota[:, :], t["c_iota"]), (wq[1][:, :], t["wq1"]), (wkv[1][:, :], t["wkv1"]),
                 (wo[1][:, :], t["wo1"]), (biases[:, :], t["biases"]), (wg[:, :], t["wg"]),
                 (bg[:, :], t["bg"]), (w1[:, :, :], t["w1"]), (b1[:, :, :], t["b1"]), (w2[:, :, :, :], t["w2"]),
                 (b2[:, :], t["b2"]), (fw1[:, :], t["fw1"]), (fw2[:, :, :], t["fw2"]),
                 (fb1[:, :], t["fb1"].broadcast_to([128, F])), (fb2[:, :], t["fb2"].broadcast_to([128, D])))

            sp.wait_ge(bias_step, 5)
            for i in range(3):
                sp.dma_start(bias3[i:i + 1, :], bias_parts[0:1, i, :]).then_inc(bias3_ready, 16)

            with sp.Fori(0, B - 1, 2) as n:
                for p in range(2):
                    sp.wait_ge(f_out, n + (p + 1))
                    sp.dma_start(out[:, bass.ds(n + p, 1), :].rearrange("p a b -> p (a b)"),
                                 yout[p][:, :]).then_inc(out_done[p], 16)
            for p in range(2):
                sp.wait_ge(out_done[p], 16 * (B // 2))

        @block.gpsimd
        def _(pool):
            pool.memset(minus_half[:, :], -0.5).then_inc(consts_pool, 1)
            pool.memset(half[:, :], 0.5).then_inc(consts_pool, 1)
            for i in range(2):
                pool.memset(stack[i][:, :, :], 0.0).then_inc(consts_pool, 1)
            for i in range(4):
                pool.memset(V[i][:, :, :], 1.0).then_inc(consts_pool, 1)
            pool.memset(msplit[:, :], 0.0).then_inc(consts_pool, 1)
            pool.memset(ones3[:, :], 1.0).then_inc(consts_pool, 1)
            pool.memset(onesq[:, :], 1.0).then_inc(consts_pool, 1)
            pool.memset(absmax[:, :, :], 1.0).then_inc(consts_pool, 1)
            pool.memset(magic[:, :], MAGIC).then_inc(consts_pool, 1)
            pool.wait_ge(consts_pool, CONSTS)

            def moments(k, j):
                base = j * LN_STEPS
                at = bass.ds(j * 2, 2)
                pool.wait_ge(stats_ready[k], j * 2 + 2)
                after(pool, ln_ready[k], j * 2)
                if k > 1 and isinstance(j, int) and j == 0:
                    pool.wait_ge(ln_ready[k - 2], B)
                ln_m, ln_d, ln_q, ln_d2, ln_q2, ln_d3, ln_v = ln_tmp[k % 2]
                pool.tensor_tensor(ln_m[:, :], stats[:, at, 1], stats[:, at, 4], ALU.add).then_inc(ln_step[k], 1)
                pool.tensor_tensor(ln_d[:, :], stats[:, at, 1], stats[:, at, 4], ALU.subtract).then_inc(ln_step[k], 1)
                pool.tensor_tensor(ln_q[:, :], stats[:, at, 2], stats[:, at, 5], ALU.add).then_inc(ln_step[k], 1)
                pool.wait_ge(ln_step[k], base + 3)
                pool.tensor_tensor(mean[:, at], ln_m[:, :], half[:, 0:2], ALU.mult).then_inc(ln_ready[k], 1)
                pool.tensor_scalar(ln_d2[:, :], ln_d[:, :], 0.5, None, ALU.mult).then_inc(ln_step[k], 1)
                pool.tensor_scalar(ln_q2[:, :], ln_q[:, :], 1.0 / D, EPS, ALU.mult, ALU.add).then_inc(ln_step[k], 1)
                pool.wait_ge(ln_step[k], base + 5)
                pool.tensor_tensor(ln_d3[:, :], ln_d2[:, :], ln_d2[:, :], ALU.mult).then_inc(ln_step[k], 1)
                pool.wait_ge(ln_step[k], base + 6)
                pool.tensor_tensor(ln_v[:, :], ln_d3[:, :], ln_q2[:, :], ALU.add).then_inc(ln_step[k], 1)
                pool.wait_ge(ln_step[k], base + 7)
                pool.tensor_tensor(rstd[:, at], ln_v[:, :], minus_half[:, 0:2], ALU.pow).then_inc(ln_ready[k], 1)

            def context(a, n, p):
                after(pool, a.proj_ps, n - 1)
                pool.tensor_copy(ctx_now[p][:, :], one(ctxT, n)).then_inc(a.ctx_ready, 1)

            def contexts(a, n):
                context(a, n, 0)
                context(a, n + 1, 1)

            a = layers[0]
            pool.wait_ge(loaded_first, LOADS_FIRST)
            contexts(a, 0)
            moments(0, 0)
            moments(0, 1)
            contexts(a, 2)
            moments(0, 2)
            contexts(a, 4)
            moments(0, 3)
            contexts(a, 6)
            moments(0, 4)
            moments(1, 0)
            pool.wait_ge(loaded_x, LOADS_X)
            contexts(a, 8)
            with pool.Fori(1, B // 2 - 4) as j:
                moments(0, j + 4)
                contexts(a, j * 2 + 8)
                moments(1, j)
            for j in range(B // 2 - 4, B // 2):
                moments(1, j)
            pool.wait_ge(loaded, LOADS)
            pool.wait_ge(a.kT_ps, B)
            for i in range(2):
                for which in range(2):
                    pool.tensor_copy(stack[i][:, which * H:(which + 1) * H, ROWS:SLOT],
                                     spare_rows[:, which, :].unsqueeze(1).broadcast_to([128, H, SPARE])
                                     ).then_inc(spare_ready, 1)
            moments(2, 0)
            moments(2, 1)
            with pool.Fori(1, NG - 1) as g:
                moments(2, g * 2)
                moments(2, g * 2 + 1)
            a = layers[1]
            contexts(a, 0)
            contexts(a, 2)
            moments(2, B // 2 - 2)
            moments(2, B // 2 - 1)
            contexts(a, 4)
            contexts(a, 6)
            moments(3, 0)
            contexts(a, 8)
            with pool.Fori(1, B // 2 - 4) as j:
                contexts(a, j * 2 + 8)
                moments(3, j)
            for j in range(B // 2 - 4, B // 2):
                moments(3, j)
            pool.wait_ge(loaded, LOADS)

            def biased(n):
                after(pool, f_out, n)
                pool.tensor_tensor(xb[:, :], one(X, n), fb2[:, :], ALU.add).then_inc(f_xb, 1)

            biased(0)
            with pool.Fori(1, B) as n:
                biased(n)

        @block.tensor
        def _(pe):
            def up_to_next(k):
                return min(k + 2, B) if isinstance(k, int) else k + 2

            def turn_xn(a, k, p):
                pe.wait_ge(a.xn_ready, k + 1)
                after(pe, a.v_copied, k)
                pe.transpose(M[0][:, 0:128], xn[p % 2][:, :], ident[:, :]).then_inc(a.xnT_ps, 1)

            def project(a, L, k, p):
                pe.wait_ge(a.ctx_ready, k + 1)
                pe.wait_ge(a.xnT_sb, k + 1)
                if L == 1:
                    pe.matmul(M[0][:, 128:512], ones3[:, :], bias3[:, 0:3 * D], start=True, stop=False,
                              skip_group_check=True)
                pe.matmul(M[0][:, 128:256], xnT[p % 2][:, :], wq[L][:, :], start=(L == 0), stop=True,
                          skip_group_check=True)
                pe.matmul(M[0][:, 256:512], ctx_now[p % 2][:, :], wkv[L][:, :], start=(L == 0), stop=True,
                          skip_group_check=True).then_inc(a.proj_ps, 1)

            def turn_q(a, k, p):
                pe.wait_ge(a.l_ready, k + 1)
                after(pe, a.kT_sb, k)
                for j in range(H // 2):
                    mm = pe.transpose(Mb[1][:, j * 128:(j + 1) * 128],
                                      stack[p % 2][:, 2 * j:2 * j + 2, :].rearrange("p a b -> p (a b)"),
                                      identb[:, :])
                mm.then_inc(a.qT_ps, 1)

            def turn_k(a, k, p):
                pe.wait_ge(a.qT_sb, k + 1)
                for j in range(H // 2):
                    mm = pe.transpose(Mb[1][:, j * 128:(j + 1) * 128],
                                      stack[p % 2][:, H + 2 * j:H + 2 * j + 2, :].rearrange("p a b -> p (a b)"),
                                      identb[:, :])
                mm.then_inc(a.kT_ps, 1)

            def masked(L, pair):
                if L == 1:
                    for b in range(2):
                        pe.matmul(pair[:, b, :, :], identb[:, :],
                                  mask[:, :].unsqueeze(1).broadcast_to([128, 4, 128]), start=True, stop=False,
                                  skip_group_check=True)

            def scores(a, L, k, p, u):
                if u == 0:
                    pe.wait_ge(a.qT_sb, k + 1)
                    pe.wait_ge(a.kT_sb, k + 1)
                after(pe, (a.exp0, a.exp1)[u], k - 1)
                masked(L, pairs[u])
                for i in range(4):
                    for b in range(2):
                        r, j = 64 * b, 4 * u + i
                        mm = pe.matmul(pairs[u][:, b, i, :], QT[p % 4][r:r + SLOT, j, :], KT[p % 4][r:r + SLOT, j, :],
                                       start=(L == 0), stop=True, skip_group_check=True)
                mm.then_inc((a.s0_ps, a.s1_ps)[u], 1)

            def turn_max(a, k):
                pe.wait_ge(a.ms_ready, k + 1)
                after(pe, a.oT_sb, k - 1)
                pe.transpose(Mb[2][:, 0:128], msplit[:, :], identb[:, :]).then_inc(a.mT_ps, 1)

            def scores_turned(a, L, k, p, u):
                pe.wait_ge((a.max0, a.max1)[u], up_to_next(k))
                if u == 0:
                    pe.wait_ge(a.mT_sb, k + 1)
                for i in range(4):
                    for b in range(2):
                        r, j = 64 * b, 4 * u + i
                        pe.matmul(pairs[u][:, b, i, :], KT[p % 4][r:r + SLOT, j, :], QT[p % 4][r:r + SLOT, j, :],
                                  start=True, stop=False, skip_group_check=True)
                        mm = pe.matmul(pairs[u][:, b, i, :], pick[L][:, 2 * j + b, :], mT[p % 2][u][:, :],
                                       start=False, stop=True, skip_group_check=True)
                mm.then_inc((a.st0_ps, a.st1_ps)[u], 1)

            def weighted(a, k, p, u):
                pe.wait_ge((a.exp0, a.exp1)[u], k + 1)
                if u == 0:
                    pe.wait_ge(a.v_copied, k + 1)
                    pe.wait_ge(a.mT_sb, up_to_next(k))
                for j in range(2 * u, 2 * u + 2):
                    for c in range(4):
                        h = 4 * j + c
                        mm = pe.matmul(M[2][32 * c:32 * c + 32, 128 * j:128 * j + 128], V[p][:, h, :],
                                       PT[u][:, 4 * (h % 2) + (h % 8) // 2, :], start=True, stop=True,
                                       skip_group_check=True)
                if u == 1:
                    mm.then_inc(a.pv1, 1)

            def turn_o(a, k):
                pe.wait_ge(a.oT_sb, k + 1)
                after(pe, a.x_done, k)
                for j in range(4):
                    mm = pe.transpose(M[3][:, j * 128:(j + 1) * 128], oT[:, j, :], ident[:, :])
                mm.then_inc(a.o_ps, 1)

            def turn_on(a, k):
                pe.wait_ge(a.on_ready, k + 1)
                pe.transpose(M[3][:, 0:128], on[:, :], ident[:, :]).then_inc(a.onT_ps, 1)

            def project_out(a, L, k):
                pe.wait_ge(a.onT_sb, k + 1)
                if L == 1:
                    pe.matmul(M[3][:, 128:256], ones3[:, :], bias3[:, 3 * D:], start=True, stop=False,
                              skip_group_check=True)
                pe.matmul(M[3][:, 128:256], onT[:, :], wo[L][:, :], start=(L == 0), stop=True,
                          skip_group_check=True).then_inc(a.y_ps, 1)

            def attention(L):
                a = layers[L]

                def step(n, p, there):
                    if L == 0 and isinstance(n, int) and n == 0:
                        pe.wait_ge(loaded_x, LOADS_X)
                    if there(0):
                        scores_turned(a, L, n, p, 0)
                        scores_turned(a, L, n, p, 1)
                    if there(1):
                        turn_max(a, n + 1)
                    if there(-1):
                        turn_o(a, n - 1)
                    if there(4):
                        turn_xn(a, n + 4, p + 4)
                    if there(2):
                        scores(a, L, n + 2, p + 2, 0)
                    if there(3):
                        turn_q(a, n + 3, p + 3)
                    if there(4):
                        project(a, L, n + 4, p + 4)
                    if there(-1):
                        turn_on(a, n - 1)
                    if there(2):
                        scores(a, L, n + 2, p + 2, 1)
                    if there(3):
                        turn_k(a, n + 3, p + 3)
                    if there(0):
                        weighted(a, n, p, 0)
                        weighted(a, n, p, 1)
                    if there(-1):
                        project_out(a, L, n - 1)

                return step

            def moe_turn_x(g):
                pe.wait_ge(m_xg, (g + 1) * G)
                after(pe, m_lT_sb, g)
                for b in range(G):
                    mm = pe.transpose(M[0][:, b * 128:(b + 1) * 128], xg[:, b, :], ident[:, :])
                mm.then_inc(m_xgT_ps, 1)

            def moe_logits(g, p):
                pe.wait_ge(m_xgT_sb, g + 1)
                pe.matmul(M[0][0:E, :], wg[:, :], xgT[p][:, :, :], start=True, stop=True).then_inc(m_lT_ps, 1)

            def moe_turn_logits(g):
                pe.wait_ge(m_lT_sb, g + 1)
                after(pe, m_combT_sb, g)
                for b in range(G):
                    mm = pe.matmul(M[1][:, b * E:(b + 1) * E], lT[:, b, :], ident[0:E, 0:E], start=True, stop=True,
                                   skip_group_check=True)
                mm.then_inc(m_logit_ps, 1)

            def moe_comb(g, p):
                pe.wait_ge(m_comb, g + 1)
                for b in range(G):
                    mm = pe.transpose(M[1][0:E, b * 128:(b + 1) * 128], comb[p][:, b, :], ident[:, :])
                mm.then_inc(m_combT_ps, 1)

            def moe_hidden(g, p, e):
                for c in range(NCH):
                    k = e * NCH + c
                    bank = pairs[e % 2][:, c, :, :]
                    after(pe, m_h_sb, g * (E * NCH) + (k - 2 * NCH + 1))
                    pe.matmul(bank, w1[:, e, c * 128:(c + 1) * 128], xgT[p][:, :, :], start=True,
                              stop=True).then_inc(m_h_ps, 1)

            def moe_out(g, p, e):
                j = e + 1
                after(pe, m_y_added, g * ((E + 1) * G) + (j - 1) * G)
                pe.wait_ge(m_h_sb, g * (E * NCH) + (e + 1) * NCH)
                if isinstance(g, int) and g == 0 and e == 0:
                    pe.wait_ge(layers[0].x_done, B)
                for b in range(G):
                    for c in range(NCH):
                        mm = pe.matmul(M[2 + (j + p) % 2][:, b * 128:(b + 1) * 128], hid[e % 2][c][:, b, :],
                                       w2[:, e, c, :], start=(c == 0), stop=(c == NCH - 1), skip_group_check=True)
                mm.then_inc(m_y_ps, 1)

            def moe_bias(g, p):
                pe.wait_ge(m_combT_sb, g + 1)
                after(pe, m_y_added, g * ((E + 1) * G) - G)
                for b in range(G):
                    mm = pe.matmul(M[2 + p][:, b * 128:(b + 1) * 128], combT[p][:, b, :], b2[:, :], start=True,
                                   stop=True, skip_group_check=True)
                mm.then_inc(m_y_ps, 1)

            def moe():
                def step(g, p, front=True):
                    moe_hidden(g, p, 0)
                    if isinstance(g, int) and g == 0:
                        moe_comb(0, 0)
                    moe_bias(g, p)
                    for e in range(1, E):
                        moe_hidden(g, p, e)
                        moe_out(g, p, e - 1)
                        if front and e == 2:
                            moe_turn_x(g + 1)
                        if front and e == 3:
                            moe_logits(g + 1, 1 - p)
                        if front and e == 4:
                            if not isinstance(g, int):
                                pe.wait_ge(wstep, 1)
                            moe_turn_logits(g + 1)
                        if front and e == 6:
                            moe_comb(g + 1, 1 - p)
                        if not front:
                            attention_ahead(pe, attention1, e)
                    moe_out(g, p, E - 1)

                step(0, 0)
                pe.wait_ge(wabs_ready, 2)
                pe.wait_ge(m_combT_sb, 2)
                pe.matmul(M[1][:, 0:2], onesq[:, :], wsum[:, :], start=True, stop=True).then_inc(wsum_ps, 1)
                with pe.Fori(1, NG - 2, 2) as g:
                    step(g, 1)
                    step(g + 1, 0)
                pe.wait_ge(bias3_ready, 16 * 3)
                pe.wait_ge(spare_ready, 4)
                step(NG - 1, 1, front=False)

            def ffn_up(n):
                pe.wait_ge(f_xq, n + 1)
                after(pe, f_xqT_sb, n)
                pe.transpose(Mb[0][:, 0:128], fxq[:, :], identb[:, :]).then_inc(f_xqT_ps, 1)
                pe.wait_ge(f_xqT_sb, n + 1)
                after(pe, f_hpre, n)
                pe.matmul(M[1][:, :], fxqT[:, :], fw1q[:, :], start=True, stop=True).then_inc(f_h_ps, 1)

            def ffn_down(n):
                pe.wait_ge(f_hq, n + 1)
                after(pe, f_hqT_sb, n)
                for c in range(FC):
                    mm = pe.transpose(Mb[2][:, c * 128:(c + 1) * 128], hq[:, c * 128:(c + 1) * 128], identb[:, :])
                mm.then_inc(f_hqT_ps, 1)
                pe.wait_ge(f_hqT_sb, n + 1)
                after(pe, f_out, n)
                for c in range(FC):
                    mm = pe.matmul(M[3][:, 0:128], hqT[:, c, :], fw2q[:, c, :], start=(c == 0), stop=(c == FC - 1))
                mm.then_inc(f_y_ps, 1)

            def ffn():
                def step(n, p, there):
                    p %= 2
                    if there(-1):
                        ffn_down(n - 1)
                    if there(2):
                        ffn_up(n + 2)

                return step

            pe.wait_ge(loaded_first, LOADS_FIRST)
            pe.wait_ge(consts_pool, CONSTS)
            attention0, attention1, ffn_step = attention(0), attention(1), ffn()

            def moe_beside(n):
                if n == B - 2:
                    pe.wait_ge(loaded, LOADS)
                    pe.wait_ge(layers[0].v_copied, B)
                    moe_turn_x(0)
                    moe_logits(0, 0)
                if n == B - 1:
                    moe_turn_logits(0)
            def ffn_beside(n):
                if n == B - 2:
                    pe.wait_ge(w_ternary, 2)
                    pe.wait_ge(layers[1].v_copied, B)
                if n in (B - 3, B - 2, B - 1):
                    peeled(ffn_step, FFN_FIRST + n - (B - 3))

            pipeline(pe, attention0, ATTENTION_FIRST, moe_beside)
            moe()
            pipeline(pe, attention1, ATTENTION_FIRST + len(AHEAD_DVE), ffn_beside)
            ffn_pipeline(pe, ffn_step)

        @block.scalar
        def _(act):
            def xnT_out(a, k, p):
                act.wait_ge(a.xnT_ps, k + 1)
                act.copy(xnT[p % 2][:, :], M[0][:, 0:128]).then_inc(a.xnT_sb, 1)

            def v_out(a, k, p):
                act.wait_ge(a.proj_read, k + 1)
                after(act, a.pv1, k - 3)
                act.copy(V[p % 4][:, :, 0:DH], M[0][:, 384:512].rearrange("p (h d) -> p h d", h=H)
                         ).then_inc(a.v_copied, 1)

            def high_parts(a, k, p):
                act.wait_ge(a.qk_ready, k + 1)
                after(act, a.kT_ps, k - 1)
                view = stack[p % 2][:, :, 0:ROWS].rearrange("p h (s d) -> p h s d", d=DH)
                act.copy(view[:, 0:H, 1:4, :], qk[:, 0:H, :].unsqueeze(2).broadcast_to([128, H, 3, DH])
                         ).then_inc(a.h_ready, 1)
                act.copy(view[:, H:, 0:5:2, :], qk[:, H:, :].unsqueeze(2).broadcast_to([128, H, 3, DH])
                         ).then_inc(a.h_ready, 1)

            def qT_out(a, k, p):
                act.wait_ge(a.qT_ps, k + 1)
                after(act, a.st1_ps, k - 3)
                act.copy(QT[p % 4][:, :, :], Mb[1][:, :].rearrange("p (j q) -> p j q", j=H // 2)).then_inc(a.qT_sb, 1)

            def kT_out(a, k, p):
                act.wait_ge(a.kT_ps, k + 1)
                act.copy(KT[p % 4][:, :, :], Mb[1][:, :].rearrange("p (j q) -> p j q", j=H // 2)).then_inc(a.kT_sb, 1)

            def mT_out(a, k, p):
                act.wait_ge(a.mT_ps, k + 1)
                after(act, a.st1_ps, k - 1)
                for u in range(2):
                    at = slice(32 * u, 32 * u + H)
                    last = act.copy(mT[p % 2][u][at, :], Mb[2][at, 0:128])
                last.then_inc(a.mT_sb, 1)

            def exps(a, k, u):
                act.wait_ge((a.st0_ps, a.st1_ps)[u], k + 1)
                after(act, a.pv1, k)
                act.activation(PT[u][:, :, :], pairs[u][:, :, :, :].rearrange("p b i q -> p (b i) q"),
                               ACT.Exp).then_inc((a.exp0, a.exp1)[u], 1)

            def oT_out(a, k):
                act.wait_ge(a.pv1, k + 1)
                after(act, a.o_ps, k)
                act.copy(oT[:, :, :], M[2][:, :].rearrange("p (j q) -> p j q", j=4)).then_inc(a.oT_sb, 1)

            def onT_out(a, k):
                act.wait_ge(a.onT_ps, k + 1)
                act.copy(onT[:, :], M[3][:, 0:128]).then_inc(a.onT_sb, 1)

            def attention(L):
                a = layers[L]

                def step(n, p, there):
                    if there(0):
                        exps(a, n, 0)
                        exps(a, n, 1)
                    if there(4):
                        xnT_out(a, n + 4, p + 4)
                    if there(1):
                        mT_out(a, n + 1, p + 1)
                    if there(3):
                        qT_out(a, n + 3, p + 3)
                    if there(-1):
                        onT_out(a, n - 1)
                    if there(3):
                        kT_out(a, n + 3, p + 3)
                    if there(4):
                        high_parts(a, n + 4, p + 4)
                        v_out(a, n + 4, p + 4)
                    if there(0):
                        oT_out(a, n)

                return step

            def moe_front(g, p):
                act.wait_ge(m_xgT_ps, g + 1)
                act.copy(xgT[p][:, :, :], M[0][:, :].rearrange("p (b q) -> p b q", b=G)).then_inc(m_xgT_sb, 1)

            def moe_logits(g):
                act.wait_ge(m_lT_ps, g + 1)
                act.activation(lT[:, :, :], M[0][0:E, :].rearrange("p (b q) -> p b q", b=G), ACT.Identity,
                               bias=bg[:, 0:1]).then_inc(m_lT_sb, 1)

            def moe_gate(g):
                act.wait_ge(m_gate, g * GATE_STEPS + 1)
                act.activation(egap[:, :], gap[:, :], ACT.Exp).then_inc(m_egap, 1)

            def moe_combT(g, p):
                act.wait_ge(m_combT_ps, g + 1)
                act.copy(combT[p][:, :, :], M[1][0:E, :].rearrange("p (b q) -> p b q", b=G)).then_inc(m_combT_sb, 1)

            def moe_relu(g, e):
                for c in range(NCH):
                    act.wait_ge(m_h_ps, g * (E * NCH) + (e * NCH + c + 1))
                    after(act, m_y_ps, g * (E + 1) + e)
                    act.activation(hid[e % 2][c][:, :, :], pairs[e % 2][:, c, :, :], ACT.Relu,
                                   bias=b1[:, e, c:c + 1]).then_inc(m_h_sb, 1)

            def moe():
                def step(g, p, front=True):
                    moe_relu(g, 0)
                    if isinstance(g, int) and g == 0:
                        moe_combT(0, 0)
                    for e in range(1, E):
                        moe_relu(g, e)
                        if front and e == 2:
                            moe_front(g + 1, 1 - p)
                        if front and e == 3:
                            moe_logits(g + 1)
                        if front and e == 4:
                            moe_gate(g + 1)
                        if front and e == 6:
                            moe_combT(g + 1, 1 - p)
                        if not front:
                            attention_ahead(act, attention1, e)

                step(0, 0)
                with act.Fori(1, NG - 2, 2) as g:
                    step(g, 1)
                    step(g + 1, 0)
                step(NG - 1, 1, front=False)

            def ffn_turned_x(n):
                act.wait_ge(f_xqT_ps, n + 1)
                act.copy(fxqT[:, :], Mb[0][:, 0:128]).then_inc(f_xqT_sb, 1)

            def ffn_gelu(n, p):
                act.wait_ge(f_hpre, n + 1)
                after(act, f_hr, n - 1)
                act.activation(hact[p][:, :], hpre[p][:, :], ACT.Gelu).then_inc(f_gelu, 1)

            def ffn_round(n, p):
                act.wait_ge(f_inverse, n + 3)
                after(act, f_hq, n)
                act.activation(hround[:, :], hact[p][:, :], ACT.Identity, bias=magic[:, 0:1],
                               scale=inverse[:, p, 1:2]).then_inc(f_hr, 1)

            def ffn_turned_h(n):
                act.wait_ge(f_hqT_ps, n + 1)
                act.copy(hqT[:, :, :], Mb[2][:, 0:F].rearrange("p (c q) -> p c q", c=FC)).then_inc(f_hqT_sb, 1)

            def ffn():
                def step(n, p, there):
                    p %= 2
                    if there(-1):
                        ffn_turned_h(n - 1)
                    if there(0):
                        ffn_round(n, p)
                    if there(1):
                        ffn_gelu(n + 1, 1 - p)
                    if there(2):
                        ffn_turned_x(n + 2)

                return step

            act.wait_ge(consts_pool, CONSTS)
            act.activation(first_exp[:, :], half[:, :], ACT.Exp)
            attention0, attention1, ffn_step = attention(0), attention(1), ffn()
            act.wait_ge(loaded_mT, 16 * 4)

            def moe_beside(n):
                if n == B - 2:
                    act.wait_ge(loaded, LOADS)
                    moe_front(0, 0)
                    moe_logits(0)
                if n == B:
                    moe_gate(0)

            def ffn_beside(n):
                if n in (B - 3, B - 2, B - 1):
                    peeled(ffn_step, FFN_FIRST + n - (B - 3))

            pipeline(act, attention0, ATTENTION_FIRST, moe_beside)
            moe()
            pipeline(act, attention1, ATTENTION_FIRST + len(AHEAD_DVE), ffn_beside)
            ffn_pipeline(act, ffn_step)

        @block.vector
        def _(dve):
            def normalised(dst, n):
                return dve.tensor_scalar(dst, one(X, n), mean[:, bass.ds(n, 1)], rstd[:, bass.ds(n, 1)],
                                         ALU.subtract, ALU.mult)

            def normalise(a, L, k, p):
                dve.wait_ge(ln_ready[2 * L], k - p % 2 + 2)
                after(dve, a.xnT_ps, k - 1)
                normalised(xn[p % 2][:, :], k).then_inc(a.xn_ready, 1)

            def rotate(a, L, k):
                dve.wait_ge(a.proj_ps, k + 1)
                after(dve, a.qk_ready, k)
                P4 = M[0][:, 128:384].rearrange("p (a h d) -> p a h d", a=2, d=DH)
                r1 = rot1[:, :, :].rearrange("p (a h) d -> p a h d", a=2)
                r2 = rot2[:, :, :].rearrange("p (a h) d -> p a h d", a=2)
                c, s, hd = rope_c[L], rope_s[L], DH // 2
                dve.tensor_tensor(r1, P4, c[:, :, :].unsqueeze(2).broadcast_to([128, 2, H, DH]), ALU.mult)
                dve.tensor_tensor(r2[:, :, :, 0:hd], P4[:, :, :, hd:DH],
                                  s[:, :, 0:hd].unsqueeze(2).broadcast_to([128, 2, H, hd]), ALU.mult)
                dve.tensor_tensor(r2[:, :, :, hd:DH], P4[:, :, :, 0:hd],
                                  s[:, :, hd:DH].unsqueeze(2).broadcast_to([128, 2, H, hd]),
                                  ALU.mult).then_inc(a.proj_read, 1)

            def rotated(a, k):
                dve.wait_ge(a.proj_read, k + 1)
                after(dve, a.h_ready, 2 * k)
                after(dve, a.rest_ready, k)
                dve.tensor_tensor(qk[:, :, :], rot1[:, :, :], rot2[:, :, :], ALU.add).then_inc(a.qk_ready, 1)

            views = [x[:, :, 0:ROWS].rearrange("p h (s d) -> p h s d", d=DH) for x in stack]

            def rest(a, k, p):
                dve.wait_ge(a.h_ready, 2 * k + 2)
                after(dve, a.l_ready, k)
                dve.tensor_tensor(qk_rest[:, :, :], qk[:, :, :], views[p % 2][:, :, 2, :],
                                  ALU.subtract).then_inc(a.rest_ready, 1)

            def middle_parts(a, k, p):
                view = views[p % 2]
                dve.wait_ge(a.rest_ready, k + 1)
                for at, slots in ((slice(0, H), slice(0, 6, 5)), (slice(H, 2 * H), slice(1, 6, 4))):
                    last = dve.tensor_copy(view[:, at, slots, :],
                                           qk_rest[:, at, :].unsqueeze(2).broadcast_to([128, H, 2, DH]))
                last.then_inc(a.m_ready, 1)

            def low_parts(a, k, p):
                view = views[p % 2]
                dve.wait_ge(a.m_ready, k + 1)
                dve.tensor_tensor(view[:, 0:H, Q_L, :], qk_rest[:, 0:H, :], view[:, 0:H, 5, :], ALU.subtract)
                dve.tensor_tensor(view[:, H:, K_L, :], qk_rest[:, H:, :], view[:, H:, 5, :],
                                  ALU.subtract).then_inc(a.l_ready, 1)

            def maxima(a, k, u):
                dve.wait_ge((a.s0_ps, a.s1_ps)[u], k + 1)
                after(dve, a.ms_ready, k)
                dve.tensor_reduce(nmax[:, 8 * u:8 * u + 8].rearrange("p (i b) -> p b i", b=2),
                                  pairs[u][:, :, :, :], AX.X, ALU.max, negate=True).then_inc((a.max0, a.max1)[u], 1)

            halves = msplit[:, 0:64].rearrange("p (u c) -> p u c", u=2)
            nmax_halves = nmax[:, :].rearrange("p (u c) -> p u c", u=2)

            def max_high(a, k):
                after(dve, a.mT_ps, k)
                dve.wait_ge(a.max1, k + 1)
                dve.tensor_copy(halves[:, :, 0:H // 2], nmax_halves).then_inc(a.mh_ready, 1)

            def max_low(a, k):
                dve.wait_ge(a.mh_ready, k + 1)
                dve.tensor_tensor(halves[:, :, H // 2:H], nmax_halves, halves[:, :, 0:H // 2],
                                  ALU.subtract).then_inc(a.ms_ready, 1)

            O = M[3][:, :].rearrange("p (h d) -> p h d", h=H)

            def denominators(a, k):
                dve.wait_ge(a.o_ps, k + 1)
                dve.reciprocal(rden[:, :], O[:, :, DH]).then_inc(a.rden_ready, 1)

            def divide(a, k):
                dve.wait_ge(a.rden_ready, k + 1)
                after(dve, a.onT_ps, k)
                dve.tensor_tensor(on[:, :].rearrange("p (h d) -> p h d", h=H), O[:, :, 0:DH],
                                  rden[:, :].unsqueeze(2).broadcast_to([128, H, DH]), ALU.mult).then_inc(a.on_ready, 1)

            def residual(a, k):
                dve.wait_ge(a.y_ps, k + 1)
                dve.tensor_tensor(one(X, k), M[3][:, 128:256], one(X, k), ALU.add).then_inc(a.x_done, 1)

            def first_stats(k):
                dve.bn_stats(one(stats, k), one(X, k)).then_inc(stats_ready[0], 1)

            def next_stats(a, ln, k):
                dve.wait_ge(a.x_done, k + 1)
                dve.bn_stats(one(stats, k), one(X, k)).then_inc(stats_ready[ln], 1)

            def attention(L):
                a = layers[L]

                def step(n, p, there):
                    if there(3):
                        rest(a, n + 3, p + 3)
                    if L == 0 and there(9):
                        if isinstance(n, int) and n + 9 == AHEAD:
                            dve.wait_ge(loaded_x, LOADS_X)
                        first_stats(n + 9)
                    if there(3):
                        middle_parts(a, n + 3, p + 3)
                    if there(5):
                        normalise(a, L, n + 5, p + 5)
                    if there(3):
                        low_parts(a, n + 3, p + 3)
                    if there(-1):
                        denominators(a, n - 1)
                        divide(a, n - 1)
                    if there(2):
                        maxima(a, n + 2, 0)
                    if there(4):
                        rotate(a, L, n + 4)
                        rotated(a, n + 4)
                    if there(2):
                        maxima(a, n + 2, 1)
                    if there(-1):
                        residual(a, n - 1)
                    if there(2):
                        max_high(a, n + 2)
                    if there(-1):
                        next_stats(a, 2 * L + 1, n - 1)
                    if there(2):
                        max_low(a, n + 2)

                return step

            def moe_front(g, p):
                dve.wait_ge(ln_ready[1], g * G + G)
                after(dve, m_xgT_ps, g)
                for b in range(G):
                    normalised(xg[:, b, :], g * G + b).then_inc(m_xg, 1)

            def moe_gate(g, p):
                base = g * GATE_STEPS
                k = [0]

                def step(ins):
                    k[0] += 1
                    ins.then_inc(m_gate, 1)

                dve.wait_ge(m_logit_ps, g + 1)
                dve.tensor_copy(logit[:, :, :], M[1][:, 0:G * E].rearrange("p (b e) -> p b e", b=G)
                                ).then_inc(m_logit_sb, 1)
                dve.wait_ge(m_logit_sb, g + 1)
                after(dve, m_carry, 2 * g)
                dve.memset(carry[:, 0:1], 0.0).then_inc(m_carry, 1)
                for b in range(G):
                    dve.max(top[:, b, :], logit[:, b, :]).then_inc(m_top, 1)
                dve.wait_ge(m_top, (g + 1) * G)
                after(dve, m_carry, 2 * g)
                dve.memset(carry[:, 1:2], 0.0).then_inc(m_carry, 1)
                for b in range(G):
                    dve.max_index(topi[:, b, :], top[:, b, :], logit[:, b, :]).then_inc(m_topi, 1)
                after(dve, m_egap, g)
                step(dve.tensor_tensor(gap[:, :], top[:, :, 1], top[:, :, 0], ALU.subtract))
                dve.wait_ge(m_topi, (g + 1) * G)
                step(dve.tensor_copy(topf[:, :, :], topi[:, :, :]))
                dve.wait_ge(m_egap, g + 1)
                step(dve.tensor_scalar(egap1[:, :], egap[:, :], 1.0, None, ALU.add))
                dve.wait_ge(m_gate, base + 3)
                step(dve.reciprocal(w_first[:, :], egap1[:, :]))
                wide = iota[:, :].unsqueeze(1).broadcast_to([128, G, E])
                step(dve.tensor_tensor(pick1[:, :, :], wide, topf[:, :, 0:1].broadcast_to([128, G, E]), ALU.is_equal))
                step(dve.tensor_tensor(pick2[:, :, :], wide, topf[:, :, 1:2].broadcast_to([128, G, E]), ALU.is_equal))
                dve.wait_ge(m_gate, base + 6)
                step(dve.tensor_tensor(w_second[:, :], egap[:, :], w_first[:, :], ALU.mult))
                step(dve.tensor_tensor(pick1[:, :, :], pick1[:, :, :],
                                       w_first[:, :].unsqueeze(2).broadcast_to([128, G, E]), ALU.mult))
                dve.wait_ge(m_gate, base + 8)
                step(dve.tensor_tensor(pick2[:, :, :], pick2[:, :, :],
                                       w_second[:, :].unsqueeze(2).broadcast_to([128, G, E]), ALU.mult))
                assert k[0] == GATE_STEPS
                dve.wait_ge(m_gate, base + 9)
                dve.tensor_tensor(comb[p][:, :, :], pick1[:, :, :], pick2[:, :, :], ALU.add).then_inc(m_comb, 1)

            def moe_add(g, p, j):
                base = g * ((E + 1) * G)
                dve.wait_ge(m_y_ps, g * (E + 1) + (j + 1))
                for b in range(G):
                    after(dve, m_y_added, base + ((j - 1) * G + b + 1) if j > 0 else 0)
                    if j > 0:
                        dve.wait_ge(m_comb, g + 1)
                    Y = M[2 + (j + p) % 2][:, b * 128:(b + 1) * 128]
                    x = one(X, g * G + b)
                    if j == 0:
                        dve.tensor_tensor(x, Y, x, ALU.add).then_inc(m_y_added, 1)
                    else:
                        dve.scalar_tensor_tensor(x, Y, comb[p][:, b, j - 1:j], x, ALU.mult,
                                                 ALU.add).then_inc(m_y_added, 1)

            def moe_stats(g):
                dve.wait_ge(m_y_added, (g + 1) * ((E + 1) * G))
                for b in range(G):
                    dve.bn_stats(one(stats, g * G + b), one(X, g * G + b)).then_inc(stats_ready[2], 1)

            def moe():
                def step(g, p, front=True):
                    moe_add(g, p, 0)
                    for e in range(1, E):
                        moe_add(g, p, e)
                        if front and e == 1:
                            moe_front(g + 1, 1 - p)
                        if front and e == 4:
                            moe_gate(g + 1, 1 - p)
                        if isinstance(g, int) and g == 0 and e == 6:
                            weight_sums()
                        if not front:
                            attention_ahead(dve, attention1, e)
                    moe_add(g, p, E)
                    moe_stats(g)

                step(0, 0)
                ternary_weights()
                split_biases()
                with dve.Fori(1, NG - 2, 2) as g:
                    step(g, 1)
                    step(g + 1, 0)
                step(NG - 1, 1, front=False)

            def ffn_normalise(n, p):
                dve.wait_ge(ln_ready[3], n - p + 2)
                after(dve, f_xr, n - 1)
                normalised(fxn[p][:, :], n).then_inc(f_xn, 1)

            def ffn_x_max(n, p):
                dve.wait_ge(f_xn, n + 1)
                dve.tensor_reduce(absmax[:, p, 0:1], fxn[p][:, :], AX.X, ALU.max,
                                  apply_absolute_value=True).then_inc(f_x_max, 1)

            def ffn_h_max(n, p):
                dve.wait_ge(f_gelu, n + 1)
                dve.tensor_reduce(absmax[:, p, 1:2], hact[p][:, :], AX.X, ALU.max,
                                  apply_absolute_value=True).then_inc(f_h_max, 1)

            def ffn_scales(n, p, there, between):
                if there(2):
                    dve.wait_ge(f_x_max, n + 3)
                if there(0):
                    dve.wait_ge(f_h_max, n + 1)
                dve.tensor_scalar(unit[:, p, :], absmax[:, p, :], EPS, 1.0 / QB, ALU.max, ALU.mult).then_inc(f_unit, 1)
                between()
                dve.wait_ge(f_unit, n + 3)
                dve.reciprocal(inverse[:, p, :], unit[:, p, :]).then_inc(f_inverse, 1)
                dve.tensor_tensor(outscale[:, p, :], unit[:, p, :], wscale[:, :], ALU.mult).then_inc(f_outscale, 1)

            def ffn_round_x(n, p, between):
                dve.wait_ge(f_inverse, n + 1)
                dve.tensor_scalar(fxr[:, :], fxn[p][:, :], inverse[:, p, 0:1], MAGIC, ALU.mult, ALU.add).then_inc(f_xr, 1)
                between()
                dve.wait_ge(f_xr, n + 1)
                after(dve, f_xqT_ps, n)
                dve.tensor_scalar(fxq[:, :], fxr[:, :], MAGIC, QB, ALU.subtract, ALU.min).then_inc(f_xq, 1)

            def ffn_hidden(n, p):
                dve.wait_ge(f_h_ps, n + 1)
                dve.wait_ge(f_outscale, n + 1)
                after(dve, f_gelu, n - 1)
                dve.scalar_tensor_tensor(hpre[p][:, :], M[1][:, :], outscale[:, p, 0:1], fb1[:, :], ALU.mult,
                                         ALU.add).then_inc(f_hpre, 1)

            def ffn_round_h(n):
                dve.wait_ge(f_hr, n + 1)
                after(dve, f_hqT_ps, n)
                dve.tensor_scalar(hq[:, :], hround[:, :], MAGIC, QB, ALU.subtract, ALU.min).then_inc(f_hq, 1)

            def ffn_out(n, p):
                dve.wait_ge(f_y_ps, n + 1)
                dve.wait_ge(f_xb, n + 1)
                dve.wait_ge(f_outscale, n + 3)
                after(dve, out_done[p], (n - p) * 8)
                dve.scalar_tensor_tensor(yout[p][:, :], M[3][:, 0:128], outscale[:, p, 1:2], xb[:, :], ALU.mult,
                                         ALU.add).then_inc(f_out, 1)

            def ffn():
                def step(n, p, there):
                    p %= 2
                    q = 1 - p

                    def hidden():
                        if there(1):
                            ffn_hidden(n + 1, q)

                    def normalise_next():
                        if there(3):
                            ffn_normalise(n + 3, q)

                    if there(-1):
                        ffn_round_h(n - 1)
                    if there(2):
                        ffn_x_max(n + 2, p)
                    if there(0):
                        ffn_h_max(n, p)
                    if there(-2):
                        ffn_out(n - 2, p)
                    if there(0) or there(2):
                        ffn_scales(n, p, there, hidden)
                    if there(2):
                        ffn_round_x(n + 2, p, normalise_next)
                    else:
                        normalise_next()

                return step

            def split_biases():
                dve.tensor_copy(bias_parts[:, 0, :], biases[:, :]).then_inc(bias_step, 1)
                dve.wait_ge(bias_step, 1)
                dve.tensor_tensor(bias_rest[:, 0, :], biases[:, :], bias_parts[:, 0, :], ALU.subtract
                                  ).then_inc(bias_step, 1)
                dve.wait_ge(bias_step, 2)
                dve.tensor_copy(bias_parts[:, 1, :], bias_rest[:, 0, :]).then_inc(bias_step, 1)
                dve.wait_ge(bias_step, 3)
                dve.tensor_tensor(bias_rest[:, 1, :], bias_rest[:, 0, :], bias_parts[:, 1, :], ALU.subtract
                                  ).then_inc(bias_step, 1)
                dve.wait_ge(bias_step, 4)
                dve.tensor_copy(bias_parts[:, 2, :], bias_rest[:, 1, :]).then_inc(bias_step, 1)

            def weight_sums():
                for i, w in enumerate((fw1[:, :], fw2[:, :, :].rearrange("p c d -> p (c d)"))):
                    dve.tensor_reduce(wsum[:, i:i + 1], w, AX.X, ALU.add, apply_absolute_value=True).then_inc(wabs_ready, 1)

            def ternary_weights():
                dve.wait_ge(wsum_ps, 1)
                dve.tensor_scalar(wscale[:, :], M[1][:, 0:2], 1.0 / (D * F), EPS, ALU.mult, ALU.max).then_inc(wstep, 1)
                dve.wait_ge(wstep, 1)
                dve.reciprocal(wrecip[:, :], wscale[:, :]).then_inc(wstep, 1)
                dve.wait_ge(wstep, 2)
                for i, (w, wqt) in enumerate(((fw1[:, :], fw1q[:, :]),
                                              (fw2[:, :, :].rearrange("p c d -> p (c d)"),
                                               fw2q[:, :, :].rearrange("p c d -> p (c d)")))):
                    dve.tensor_scalar(w, w, wrecip[:, i:i + 1], MAGIC, ALU.mult, ALU.add).then_inc(wstep, 1)
                    dve.wait_ge(wstep, 3 + 2 * i)
                    dve.tensor_scalar(wtmp[:, :], w, MAGIC, 1.0, ALU.subtract, ALU.min).then_inc(wstep, 1)
                    dve.wait_ge(wstep, 4 + 2 * i)
                    last = dve.tensor_scalar(wqt, wtmp[:, :], -1.0, None, ALU.max)
                    last.then_inc(w_ternary, 1)
                    dve.wait_ge(w_ternary, 1 + i)

            dve.wait_ge(loaded_first, LOADS_FIRST)
            for k in range(4):
                first_stats(k)
            dve.wait_ge(consts_pool, CONSTS)
            attention0, attention1, ffn_step = attention(0), attention(1), ffn()

            def moe_beside(n):
                if n == B - 3:
                    dve.wait_ge(loaded, LOADS)
                    moe_front(0, 0)
                if n == B:
                    moe_gate(0, 0)

            def ffn_beside(n):
                if n in (B - 3, B - 2, B - 1):
                    peeled(ffn_step, FFN_FIRST + n - (B - 3))

            pipeline(dve, attention0, ATTENTION_FIRST, moe_beside)
            moe()
            pipeline(dve, attention1, ATTENTION_FIRST + len(AHEAD_DVE), ffn_beside)
            ffn_pipeline(dve, ffn_step)


def constants():
    import numpy as np

    def bf16(x):
        return (np.ascontiguousarray(x).view(np.uint32) >> 16).astype(np.uint16)

    pos = np.arange(S, dtype=np.float32)
    freqs = [10000.0 ** (-np.arange(0, DH, 2, dtype=np.float32) / DH),
             1.0 / 10000.0 ** (np.arange(DH // 2, dtype=np.float32) / (DH // 2))]
    out = {"c_ident": np.eye(128, dtype=np.float32)}
    for i, f in enumerate(freqs):
        ang = pos[:, None] * f.astype(np.float32)[None, :]
        c, s = np.cos(ang), np.sin(ang)
        cc, ss = np.concatenate([c, c], 1), np.concatenate([-s, s], 1)
        q_scale = np.float32(DH ** -0.5)
        out[f"c_rope_c{i}"] = np.stack([cc * q_scale, cc], 1).astype(np.float32)
        out[f"c_rope_s{i}"] = np.stack([ss * q_scale, ss], 1).astype(np.float32)
    rows = [np.array([r for r in range(S) if not 32 * u <= r < 32 * u + H]) for u in range(2)]
    picks = np.zeros((2, 128, H, 128), np.float32)
    for h in range(H):
        u, c = divmod(h, H // 2)
        picks[:, 32 * u + c, h] = 1.0
        picks[:, 32 * u + H // 2 + c, h] = 1.0
        picks[1, rows[u], h, np.arange(SLOT_KEYS)] = 1.0
    out["c_pick0"], out["c_pick1"] = bf16(picks[0]), bf16(picks[1])
    out["c_identb"] = bf16(out["c_ident"])
    q, k = np.arange(S)[:, None], np.arange(S)[None, :]
    inside = (k <= q) & (k >= q - WINDOW)
    m = np.where(inside, 0.0, -1e30).astype(np.float32)
    out["c_mask_qk"] = bf16(m)
    mask_rows = np.zeros((2, S, S), np.float32)
    for u in range(2):
        mask_rows[u, rows[u]] = m.T[:SLOT_KEYS]
    out["c_mask_rows"] = bf16(mask_rows)
    out["c_spare_rows"] = bf16(np.stack([m[:, SLOT_KEYS:], np.eye(S, dtype=np.float32)[:, SLOT_KEYS:]], 1))
    out["c_iota"] = np.tile(np.arange(E, dtype=np.float32), (128, 1))
    return out


def kernel(**inputs):
    import numpy as np
    import concourse.bacc as bacc
    from concourse import mybir as mb
    from concourse.bass_utils import run_bass_kernel_spmd as run

    a = {k: np.asarray(v) for k, v in inputs.items()}
    perm = np.arange(D).reshape(H, DH)[:, [0, 2, 4, 6, 1, 3, 5, 7]].reshape(-1)
    arrays = {
        "x": a["x"].transpose(1, 0, 2),
        "ctxT": a["ctx_1024"].transpose(2, 0, 1),
        "wq0": a["L0_xattn_Wq"][:, perm],
        "wkv0": np.concatenate([a["L0_xattn_Wk"][:, perm], a["L0_xattn_Wv"]], 1),
        "wo0": a["L0_xattn_Wo"],
        "wq1": a["L1_xattn_q_w"].T,
        "wkv1": np.concatenate([a["L1_xattn_k_w"].T, a["L1_xattn_v_w"].T], 1),
        "wo1": a["L1_xattn_o_w"].T,
        "biases": np.concatenate([a[f"L1_xattn_{x}_b"] for x in "qkvo"])[None],
        "wg": a["L0_ffn_Wg"],
        "bg": a["L0_ffn_bg"][:, None],
        "w1": a["L0_ffn_W1"].transpose(1, 0, 2),
        "b1": a["L0_ffn_b1"].reshape(E, NCH, 128).transpose(2, 0, 1),
        "w2": a["L0_ffn_W2"].reshape(E, NCH, 128, D).transpose(2, 0, 1, 3),
        "b2": a["L0_ffn_b2"],
        "fw1": a["L1_ffn_W1"].T,
        "fw2": a["L1_ffn_W2"].T.reshape(FC, 128, D).transpose(1, 0, 2),
        "fb1": a["L1_ffn_b1"][None],
        "fb2": a["L1_ffn_b2"][None],
    }
    arrays.update(constants())
    arrays = {k: np.ascontiguousarray(v) for k, v in arrays.items()}
    nc = bacc.Bacc("TRN2", target_bir_lowering=False, num_devices=1)
    t = {k: nc.dram_tensor(f"in_{k}", v.shape, mb.dt.from_np(v.dtype), kind="ExternalInput").ap()
         for k, v in arrays.items()}
    out = nc.dram_tensor("out_x", (S, B, D), mb.dt.float32, kind="ExternalOutput").ap()
    build(nc, t, out)
    r = run(nc, [{f"in_{k}": v for k, v in arrays.items()}], core_ids=[0])
    return np.ascontiguousarray(r.results[0]["out_x"].transpose(1, 0, 2))
```
